# Optimizing a Trainium2 kernel written in Bass

```python
import numpy as np
import jax
import jax.numpy as jnp

def _softmax(x, axis=-1):
    return jax.nn.softmax(x, axis=axis)

def _gelu(x):
    return jax.nn.gelu(x, approximate=True)

def _silu(x):
    return jax.nn.silu(x)

def _sigmoid(x):
    return jax.nn.sigmoid(x)

def _layernorm(x, axis=-1, eps=1e-05):
    m = jnp.mean(x, axis=axis, keepdims=True)
    v = jnp.var(x, axis=axis, keepdims=True)
    return (x - m) / jnp.sqrt(v + eps)

def _scatter_add(tgt, idx, src, axis=0):
    return tgt.at[idx].add(src)

def _segment_sum(src, seg, n):
    return jax.ops.segment_sum(src, seg, n)
kernel_name = 'mk_gnn_preln_d4_gnn_r64_dc423c'

def setup_inputs(seed: int=0):
    np.random.seed(seed)
    _w = jnp.asarray

    def _rec_inputs():
        import jax
        import jax.numpy as jnp
        _gk = jax.random.key(seed)
        x = -8.776e-05 + 1 * jax.random.normal(jax.random.fold_in(_gk, 1), (20000, 256), jnp.float32)
        src = jax.random.randint(jax.random.fold_in(_gk, 2), (5000,), 0, 20000, jnp.int32)
        dst = jax.random.randint(jax.random.fold_in(_gk, 3), (5000,), 0, 20000, jnp.int32)
        _o = jnp.argsort(dst, stable=True)
        src = src[_o]
        dst = dst[_o]
        edge_attr_64 = 0.000279952 + 1.00013 * jax.random.normal(jax.random.fold_in(_gk, 12), (5000, 64), jnp.float32)
        edge_type_8 = jax.random.randint(jax.random.fold_in(_gk, 14), (5000,), 0, 8, jnp.int32)
        edge_weight = jax.random.uniform(jax.random.fold_in(_gk, 15), (5000,), jnp.float32, 0.0, 1)
        return (x, src, dst, edge_attr_64, edge_type_8, edge_weight)
    x, src, dst, edge_attr_64, edge_type_8, edge_weight = _rec_inputs()

    def _L0_gnn_setup():
        import jax, jax.numpy as jnp
        import numpy as np
        N = 20000
        E = 5000
        F_IN = 256
        H = 8
        C = 32
        EDGE_DIM = 64
        NEG_SLOPE = 0.2
        key = jax.random.key(seed)
        ks = jax.random.split(key, 9)
        x = jax.random.normal(ks[0], (N, F_IN), dtype=jnp.float32)
        edge_index = jax.random.randint(ks[1], (2, E), 0, N, dtype=jnp.int32)
        edge_attr = jax.random.normal(ks[2], (E, EDGE_DIM), dtype=jnp.float32)
        s_in = 1.0 / np.sqrt(F_IN)
        s_e = 1.0 / np.sqrt(EDGE_DIM)
        s_c = 1.0 / np.sqrt(C)
        W = jax.random.normal(ks[3], (F_IN, H * C), dtype=jnp.float32) * s_in
        W_edge = jax.random.normal(ks[4], (EDGE_DIM, H * C), dtype=jnp.float32) * s_e
        att_src = jax.random.normal(ks[5], (H, C), dtype=jnp.float32) * s_c
        att_dst = jax.random.normal(ks[6], (H, C), dtype=jnp.float32) * s_c
        att_edge = jax.random.normal(ks[7], (H, C), dtype=jnp.float32) * s_c
        bias = jnp.zeros((H * C,), dtype=jnp.float32)
        return {'x': x, 'edge_index': edge_index, 'edge_attr': edge_attr, 'W': W, 'W_edge': W_edge, 'att_src': att_src, 'att_dst': att_dst, 'att_edge': att_edge, 'bias': bias}
    _L0_gnn_all = _L0_gnn_setup()
    _L0_gnn_in = {k: v for k, v in _L0_gnn_all.items() if k in ('W', 'W_edge', 'att_src', 'att_dst', 'att_edge', 'bias')}
    del _L0_gnn_all

    def _L1_gnn_setup():
        import jax, jax.numpy as jnp
        import numpy as np
        N_NODES = 50000
        N_EDGES = 12500
        IN_FEAT = 256
        OUT_FEAT = 256
        NUM_RELS = 8
        NUM_BASES = 8
        SUBMAT_IN = IN_FEAT // NUM_BASES
        SUBMAT_OUT = OUT_FEAT // NUM_BASES
        key = jax.random.key(seed)
        k_h, k_w, k_src, k_dst, k_rel, k_norm = jax.random.split(key, 6)
        h = jax.random.normal(k_h, (N_NODES, IN_FEAT), dtype=jnp.float32)
        weight = jax.random.normal(k_w, (NUM_RELS, NUM_BASES * SUBMAT_IN * SUBMAT_OUT), dtype=jnp.float32) * 0.05
        edge_src = jax.random.randint(k_src, (N_EDGES,), 0, N_NODES, dtype=jnp.int32)
        edge_dst = jax.random.randint(k_dst, (N_EDGES,), 0, N_NODES, dtype=jnp.int32)
        edge_rel = jax.random.randint(k_rel, (N_EDGES,), 0, NUM_RELS, dtype=jnp.int32)
        edge_norm = jax.random.uniform(k_norm, (N_EDGES,), dtype=jnp.float32)
        return {'h': h, 'weight': weight, 'edge_src': edge_src, 'edge_dst': edge_dst, 'edge_rel': edge_rel, 'edge_norm': edge_norm}
    _L1_gnn_all = _L1_gnn_setup()
    _L1_gnn_in = {k: v for k, v in _L1_gnn_all.items() if k in ('weight',)}
    del _L1_gnn_all

    def _L2_gnn_setup():
        import jax, jax.numpy as jnp
        import numpy as np
        NUM_NODES = 625
        NUM_REL = 8
        NUM_BASES = 4
        EMB = 256
        NUM_LAYERS = 3
        NUM_EDGES = 10000

        def _rgcn_layer(x, src, seg, inv_cnt, comp, basis, root, bias):
            N, D = x.shape
            R = comp.shape[0]
            W = jnp.einsum('rb,bio->rio', comp, basis)
            agg = jax.ops.segment_sum(x[src], seg, num_segments=R * N) * inv_cnt
            agg = agg.reshape(R, N, D)
            out = jnp.einsum('rni,rio->no', agg, W) + x @ root + bias
            return out
        key = jax.random.key(seed)
        ks = jax.random.split(key, 7)
        edge_index = jax.random.randint(ks[0], (2, NUM_EDGES), 0, NUM_NODES)
        edge_type = jax.random.randint(ks[1], (NUM_EDGES,), 0, NUM_REL)
        embeddings = jax.random.normal(ks[2], (NUM_NODES, EMB), dtype=jnp.float32)
        scale = 1.0 / np.sqrt(EMB)
        comps = jax.random.normal(ks[3], (NUM_LAYERS, NUM_REL, NUM_BASES), dtype=jnp.float32) * scale
        bases = jax.random.normal(ks[4], (NUM_LAYERS, NUM_BASES, EMB, EMB), dtype=jnp.float32) * scale
        roots = jax.random.normal(ks[5], (NUM_LAYERS, EMB, EMB), dtype=jnp.float32) * scale
        biases = jnp.zeros((NUM_LAYERS, EMB), dtype=jnp.float32)
        return {'edge_index': edge_index, 'edge_type': edge_type, 'embeddings': embeddings, 'comps': comps, 'bases': bases, 'roots': roots, 'biases': biases}
    _L2_gnn_all = _L2_gnn_setup()
    _L2_gnn_in = {k: v for k, v in _L2_gnn_all.items() if k in ('comps', 'bases', 'roots', 'biases')}
    del _L2_gnn_all

    def _L3_gnn_setup():
        import jax, jax.numpy as jnp
        import numpy as np
        N, E, D_IN, D_OUT = (50000, 25000, 256, 256)
        key = jax.random.key(seed)
        k1, k2, k3, k4, k5, k6 = jax.random.split(key, 6)
        x = jax.random.normal(k1, (N, D_IN), dtype=jnp.float32)
        edge_index = jax.random.randint(k2, (2, E), 0, N, dtype=jnp.int64)
        s = 1.0 / np.sqrt(D_IN)
        W1 = jax.random.uniform(k3, (D_OUT, D_IN), minval=-s, maxval=s, dtype=jnp.float32)
        b1 = jax.random.uniform(k4, (D_OUT,), minval=-s, maxval=s, dtype=jnp.float32)
        W2 = jax.random.uniform(k5, (D_OUT, D_IN), minval=-s, maxval=s, dtype=jnp.float32)
        b2 = jax.random.uniform(k6, (D_OUT,), minval=-s, maxval=s, dtype=jnp.float32)
        return {'x': x, 'W1': W1, 'b1': b1, 'W2': W2, 'b2': b2, 'edge_index': edge_index}
    _L3_gnn_all = _L3_gnn_setup()
    _L3_gnn_in = {k: v for k, v in _L3_gnn_all.items() if k in ('W1', 'b1', 'W2', 'b2')}
    del _L3_gnn_all
    return {'x': x, 'src': src, 'dst': dst, 'edge_attr_64': edge_attr_64, 'edge_type_8': edge_type_8, 'edge_weight': edge_weight, 'L0_gnn_W': _L0_gnn_in['W'], 'L0_gnn_W_edge': _L0_gnn_in['W_edge'], 'L0_gnn_att_src': _L0_gnn_in['att_src'], 'L0_gnn_att_dst': _L0_gnn_in['att_dst'], 'L0_gnn_att_edge': _L0_gnn_in['att_edge'], 'L0_gnn_bias': _L0_gnn_in['bias'], 'L1_gnn_weight': _L1_gnn_in['weight'], 'L2_gnn_comps': _L2_gnn_in['comps'], 'L2_gnn_bases': _L2_gnn_in['bases'], 'L2_gnn_roots': _L2_gnn_in['roots'], 'L2_gnn_biases': _L2_gnn_in['biases'], 'L3_gnn_W1': _L3_gnn_in['W1'], 'L3_gnn_b1': _L3_gnn_in['b1'], 'L3_gnn_W2': _L3_gnn_in['W2'], 'L3_gnn_b2': _L3_gnn_in['b2']}

def reference(x, src, dst, edge_attr_64, edge_type_8, edge_weight, L0_gnn_W, L0_gnn_W_edge, L0_gnn_att_src, L0_gnn_att_dst, L0_gnn_att_edge, L0_gnn_bias, L1_gnn_weight, L2_gnn_comps, L2_gnn_bases, L2_gnn_roots, L2_gnn_biases, L3_gnn_W1, L3_gnn_b1, L3_gnn_W2, L3_gnn_b2):
    import jax
    import jax.numpy as jnp

    def _L0_gnn_ref(x, edge_index, edge_attr, W, W_edge, att_src, att_dst, att_edge, bias):
        import jax, jax.numpy as jnp
        import numpy as np
        N = 20000
        E = 5000
        F_IN = 256
        H = 8
        C = 32
        EDGE_DIM = 64
        NEG_SLOPE = 0.2
        h = jax.nn.relu(x)
        xh = (h @ W).reshape(N, H, C)
        loop = jnp.arange(N, dtype=edge_index.dtype)
        src = jnp.concatenate([edge_index[0], loop])
        dst = jnp.concatenate([edge_index[1], loop])
        mean_ea = jnp.mean(edge_attr, axis=0, keepdims=True)
        ea = jnp.concatenate([edge_attr, jnp.broadcast_to(mean_ea, (N, EDGE_DIM))], axis=0)
        eh = (ea @ W_edge).reshape(-1, H, C)
        a_src = jnp.sum(xh * att_src, axis=-1)
        a_dst = jnp.sum(xh * att_dst, axis=-1)
        a_edge = jnp.sum(eh * att_edge, axis=-1)
        a = a_src[src] + a_dst[dst] + a_edge
        a = jax.nn.leaky_relu(a, NEG_SLOPE)
        amax = jax.ops.segment_max(a, dst, num_segments=N)
        ex = jnp.exp(a - amax[dst])
        denom = jax.ops.segment_sum(ex, dst, num_segments=N)
        alpha = ex / (denom[dst] + 1e-16)
        msg = alpha[:, :, None] * xh[src]
        out = jax.ops.segment_sum(msg, dst, num_segments=N)
        return out.reshape(N, H * C) + bias

    def _L1_gnn_ref(h, weight, edge_src, edge_dst, edge_rel, edge_norm):
        import jax, jax.numpy as jnp
        import numpy as np
        N_NODES = 50000
        N_EDGES = 12500
        IN_FEAT = 256
        OUT_FEAT = 256
        NUM_RELS = 8
        NUM_BASES = 8
        SUBMAT_IN = IN_FEAT // NUM_BASES
        SUBMAT_OUT = OUT_FEAT // NUM_BASES
        'RGCNBlockLayer forward (self_loop=False, bias=None, activation=None).\n\n            Per relation r: agg_r[v] = sum_{(u->v) in rel r} norm_e * h[u]\n            then block-diagonal matmul out_r = blockmm(agg_r, W_r); output = sum_r out_r.\n            '
        N, in_feat = h.shape
        R = weight.shape[0]
        msg = h[edge_src] * edge_norm[:, None]
        seg = edge_rel * N + edge_dst
        agg = jax.ops.segment_sum(msg, seg, num_segments=R * N)
        agg = agg.reshape(R, N, NUM_BASES, SUBMAT_IN)
        W = weight.reshape(R, NUM_BASES, SUBMAT_IN, SUBMAT_OUT)
        out = jnp.einsum('rnbi,rbio->nbo', agg, W)
        return out.reshape(N, NUM_BASES * SUBMAT_OUT)

    def _L2_gnn_ref(edge_index, edge_type, embeddings, comps, bases, roots, biases):
        import jax, jax.numpy as jnp
        import numpy as np
        NUM_NODES = 625
        NUM_REL = 8
        NUM_BASES = 4
        EMB = 256
        NUM_LAYERS = 3
        NUM_EDGES = 10000

        def _rgcn_layer(x, src, seg, inv_cnt, comp, basis, root, bias):
            N, D = x.shape
            R = comp.shape[0]
            W = jnp.einsum('rb,bio->rio', comp, basis)
            agg = jax.ops.segment_sum(x[src], seg, num_segments=R * N) * inv_cnt
            agg = agg.reshape(R, N, D)
            out = jnp.einsum('rni,rio->no', agg, W) + x @ root + bias
            return out
        src, dst = (edge_index[0], edge_index[1])
        N = embeddings.shape[0]
        R = comps.shape[1]
        seg = edge_type * N + dst
        cnt = jax.ops.segment_sum(jnp.ones_like(seg, dtype=embeddings.dtype), seg, num_segments=R * N)
        inv_cnt = (1.0 / jnp.maximum(cnt, 1.0))[:, None]
        x = _rgcn_layer(embeddings, src, seg, inv_cnt, comps[0], bases[0], roots[0], biases[0])
        for i in range(1, NUM_LAYERS - 1):
            x = _rgcn_layer(jax.nn.relu(x), src, seg, inv_cnt, comps[i], bases[i], roots[i], biases[i])
        return x

    def _L3_gnn_ref(x, W1, b1, W2, b2, edge_index):
        import jax, jax.numpy as jnp
        import numpy as np
        N, E, D_IN, D_OUT = (50000, 25000, 256, 256)
        dst = edge_index[0]
        nbr = edge_index[1]
        n = x.shape[0]
        agg = jax.ops.segment_sum(x[nbr], dst, num_segments=n)
        cnt = jax.ops.segment_sum(jnp.ones((nbr.shape[0],), x.dtype), dst, num_segments=n)
        mean = agg / jnp.maximum(cnt, 1.0)[:, None]
        return x @ W1.T + b1 + mean @ W2.T + b2
    edge_index = jnp.stack([src, dst])
    h = jnp.maximum(_layernorm(x, axis=-1), 0.0)
    x = x + _L0_gnn_ref(h, edge_index, edge_attr_64, L0_gnn_W, L0_gnn_W_edge, L0_gnn_att_src, L0_gnn_att_dst, L0_gnn_att_edge, L0_gnn_bias)
    h = jnp.maximum(_layernorm(x, axis=-1), 0.0)
    x = x + _L1_gnn_ref(h, L1_gnn_weight, src, dst, edge_type_8, edge_weight)
    h = jnp.maximum(_layernorm(x, axis=-1), 0.0)
    x = x + _L2_gnn_ref(edge_index, edge_type_8, h, L2_gnn_comps, L2_gnn_bases, L2_gnn_roots, L2_gnn_biases)
    h = jnp.maximum(_layernorm(x, axis=-1), 0.0)
    x = x + _L3_gnn_ref(h, L3_gnn_W1, L3_gnn_b1, L3_gnn_W2, L3_gnn_b2, edge_index)
    return x

_drawn_inputs = setup_inputs


def setup_inputs(seed=0):
    import zlib

    import numpy as np

    out = dict(_drawn_inputs(seed))
    spreads = {'L0_gnn_bias': (0.0, 0.1), 'L2_gnn_biases': (0.0, 0.1)}
    factors = {'L0_gnn_att_dst': 3.474}
    for name, (base, spread) in spreads.items():
        noise = np.random.default_rng([zlib.crc32(name.encode()), seed]).standard_normal(out[name].shape)
        drawn = base * np.exp(spread * noise) if base else spread * noise
        out[name] = jnp.asarray(drawn.astype(out[name].dtype))
    for name, factor in factors.items():
        out[name] = (out[name] * factor).astype(out[name].dtype)
    return out
```

```python
from contextlib import ExitStack, contextmanager

import concourse.bass as bass
from concourse import mybir

F32 = mybir.dt.float32
BF16 = mybir.dt.bfloat16
I32 = mybir.dt.int32
ALU = mybir.AluOpType
ACT = mybir.ActivationFunctionType
AX_X = mybir.AxisListType.X
ds = bass.ds

P = 128
N, D, E = 20000, 256, 5000
H, C = 8, 32
R = 8
NB = 4
ED = 64
ET = -(-E // P)
EP = ET * P
EQ = E // ET
NQ = 125
G = 4
EG = ET // G
NT = N // P
REM = N - NT * P
NG = 3
NI = NT // (G * NG)
HI = 160
PAD_KEY = 156 * 128 + 127
FAR = 1 << 20
EPS = 1e-5
BIG = 1e30
SLOPE = 0.2
GD = G * D
AW = D + H
TW = H + 3 * D
assert EQ * ET == E and NI * G * NG == NT and EG % 2 == 0 and N % NQ == 0


class Link:

    def __init__(self, eng, sem):
        self.eng, self.sem, self.base, self.i, self.per, self.c = eng, sem, 0, None, 0, 0

    def enter(self, i, per):
        self.i, self.per, self.c = i, per, 0

    def leave(self, times):
        assert self.c == self.per, ("increments of the loop's body", self.c, self.per)
        self.base, self.i, self.c = self.base + times * self.per, None, 0

    def mark(self, ins):
        ins.then_inc(self.sem, 1)
        if self.i is None:
            self.base += 1
            return self.base
        self.c += 1
        return self.i * self.per + (self.base + self.c)

    def until(self, value):
        self.eng.wait_ge(self.sem, value)

    def __call__(self, ins):
        self.until(self.mark(ins))


class Carve:

    def __init__(self, buf):
        self.buf, self.at = buf, 0

    def __call__(self, n):
        self.at += n
        return self.buf[:, self.at - n:self.at]


@contextmanager
def step(nc):
    mine = []

    def sem(name):
        mine.append(nc.alloc_semaphore(name=name))
        return mine[-1]

    yield sem
    nc.clear_and_free_semaphores(mine)
    nc.all_engine_barrier()


class Store:
    pass


def bc(ap, n):
    return ap.unsqueeze(2).to_broadcast([ap.shape[0], ap.shape[1], n])


def constants(nc, sem, m):
    done = sem("const_done")
    with nc.Block() as block:
        @block.gpsimd
        def _(pool):
            link = Link(pool, done)
            pool.memset(m.ident[:, :], 0.0).then_inc(done, 1)
            pool.memset(m.ones[:, :], 1.0).then_inc(done, 1)
            pool.memset(m.onesf[:, :], 1.0).then_inc(done, 1)
            pool.memset(m.eps[:, :], EPS).then_inc(done, 1)
            pool.memset(m.e127[:, :], 0.0).then_inc(done, 1)
            pool.iota(m.iota[:, :], pattern=[[1, HI]], base=0, channel_multiplier=0,
                      allow_small_or_imprecise_dtypes=True).then_inc(done, 1)
            pool.iota(m.part[:, :], pattern=[[0, 1]], base=0, channel_multiplier=1,
                      allow_small_or_imprecise_dtypes=True).then_inc(done, 1)
            pool.wait_ge(done, 7)
            link.base = 7
            link(pool.affine_select(out=m.ident[:, :], in_=m.ident[:, :], compare_op=ALU.not_equal,
                                    fill=1.0, base=0, pattern=[[-1, P]], channel_multiplier=1))
            link(pool.affine_select(out=m.tri[:, :], in_=m.onesf[:, :], compare_op=ALU.is_gt,
                                    fill=0.0, base=0, pattern=[[-1, P]], channel_multiplier=1))
            link(pool.affine_select(out=m.triu[:, :], in_=m.onesf[:, :], compare_op=ALU.is_gt,
                                    fill=0.0, base=0, pattern=[[1, P]], channel_multiplier=-1))
            link(pool.affine_select(out=m.e127[:, :], in_=m.e127[:, :], compare_op=ALU.not_equal,
                                    fill=1.0, base=1 - P, pattern=[[0, 1]], channel_multiplier=1))
            link(pool.tensor_copy(m.identb[:, :], m.ident[:, :]))


def sort_edges(nc, sem, m, key, rec_d):
    cut = Carve(m.xs)
    lin = cut(5 * ET).bitcast(I32)
    hilo_i = cut(2 * ET).bitcast(I32)
    keyf, hif, lof, rank = cut(ET), cut(ET), cut(ET), cut(ET)
    before, inside = cut(ET), cut(ET)
    rank_i = cut(ET).bitcast(I32)
    rec = cut(8 * ET).bitcast(I32)
    oh_lo = [cut(P // 2).bitcast(BF16) for _ in range(2)]
    oh_hi = [cut(HI // 2).bitcast(BF16) for _ in range(2)]
    oh_loT, dcol = [cut(P) for _ in range(2)], [cut(P) for _ in range(2)]
    junk1, junk2 = cut(P), cut(HI)
    count, total, upto, table = cut(HI), cut(HI), cut(HI), cut(HI)
    zero = cut(HI // 2).bitcast(BF16)
    rank_s = [cut(G).bitcast(I32) for _ in range(2)]
    rec_s = [cut(8 * G).bitcast(I32) for _ in range(2)]
    psC, psW, psX = m.PS[:, 0:HI], m.PS[:, 512:512 + HI], m.PS[:, 1024:1024 + HI]
    psLT = m.PS[:, 1536:1536 + P // 2].bitcast(BF16)
    psD, psG, psN = m.PS[:, 2048:2048 + P], m.PS[:, 2560:2560 + HI], m.PS[:, 3072:3072 + HI]

    cleared, loaded, numbered = sem(f"so{key}_cleared"), sem(f"so{key}_loaded"), sem(f"so{key}_numbered")
    hot, counted, summed, split = sem(f"so{key}_hot"), sem(f"so{key}_counted"), sem(f"so{key}_summed"), sem(f"so{key}_split")
    hot2, turned, turned_out, looked = (sem(f"so{key}_hot2"), sem(f"so{key}_turned"), sem(f"so{key}_turned_out"),
                                        sem(f"so{key}_looked"))
    added, ranked, staged, gate = (sem(f"so{key}_added"), sem(f"so{key}_ranked"), sem(f"so{key}_staged"),
                                   sem(f"so{key}_gate"))
    sent = [sem(f"so{key}_sent{u}") for u in range(2)]
    dve_own = sem(f"so{key}_dve")
    with nc.Block() as block:
        @block.sync
        def _(sp):
            sp.wait_ge(cleared, 5)
            for k, a in enumerate((m.src, m.dst, m.rel, m.ew)):
                sp.dma_start(lin[0:EQ, k * ET:(k + 1) * ET],
                             a.rearrange("(p t) -> p t", t=ET).bitcast(I32)).then_inc(loaded, 16)
            sp.wait_ge(loaded, 64)

        @block.gpsimd
        def _(pool):
            for k, v in enumerate((PAD_KEY, 0, 0, 0) if key == 0 else (0, PAD_KEY, 0, 0)):
                pool.memset(lin[:, k * ET:(k + 1) * ET], v).then_inc(cleared, 1)
            pool.memset(zero, 0.0).then_inc(cleared, 1)
            pool.iota(lin[:, 4 * ET:5 * ET], pattern=[[1, ET]], base=0,
                      channel_multiplier=ET).then_inc(numbered, 1)
            pool.wait_ge(ranked, 1)
            with pool.Fori(0, EG // 2) as i:
                for u in range(2):
                    pool.wait_ge(sent[u], i * (16 * G))
                    pool.tensor_copy(rank_s[u], rank_i[:, ds((i * 2 + u) * G, G)]).then_inc(staged, 1)
                    pool.tensor_copy(rec_s[u], rec[:, ds((i * 2 + u) * (8 * G), 8 * G)])\
                        .then_inc(staged, 1)
                    pool.wait_ge(staged, i * 4 + (2 * u + 2))
                    pool.sem_inc(gate, 1)
                    for t in range(G):
                        pool.indirect_dma_start(
                            rec_d[:, :], bass.IndirectOffsetOnAxis(ap=rank_s[u][:, t:t + 1], axis=0),
                            rec_s[u][:, 8 * t:8 * t + 8], None).then_inc(sent[u], 16)
            for u in range(2):
                pool.wait_ge(sent[u], EG // 2 * 16 * G)

        @block.vector
        def _(dve):
            link = Link(dve, dve_own)
            dve.wait_ge(loaded, 64)
            dve.wait_ge(numbered, 1)
            dve.tensor_scalar(hilo_i[:, 0:ET], lin[:, key * ET:(key + 1) * ET], 7, None, ALU.arith_shift_right)
            link(dve.tensor_scalar(hilo_i[:, ET:], lin[:, key * ET:(key + 1) * ET], P - 1, None, ALU.bitwise_and))
            dve.tensor_copy(keyf, lin[:, key * ET:(key + 1) * ET])
            for k in range(5):
                dve.tensor_copy(rec.rearrange("p (t c) -> p t c", c=8)[:, :, k],
                                lin[:, k * ET:(k + 1) * ET])
            for k in range(5, 8):
                dve.tensor_copy(rec.rearrange("p (t c) -> p t c", c=8)[:, :, k], lin[:, 0:ET])
            dve.tensor_copy(hif, hilo_i[:, 0:ET])
            link(dve.tensor_copy(lof, hilo_i[:, ET:]))
            with dve.Fori(0, ET // 2) as i:
                for u in range(2):
                    dve.wait_ge(counted, i * 2 + u)
                    dve.tensor_scalar(oh_lo[u], m.iota[:, 0:P], lof[:, ds(i * 2 + u, 1)], None,
                                      ALU.is_equal)
                    dve.tensor_scalar(oh_hi[u], m.iota[:, :], hif[:, ds(i * 2 + u, 1)], None,
                                      ALU.is_equal).then_inc(hot, 1)
            dve.wait_ge(counted, ET + 2)
            dve.tensor_copy(count, psC).then_inc(split, 1)
            dve.wait_ge(summed, 1)
            link(dve.tensor_copy(total, psX))
            link(dve.tensor_tensor_scan(upto, m.ones[:, 0:HI], total, 0.0, ALU.mult, ALU.add))
            link(dve.tensor_tensor(upto, upto, total, ALU.subtract))
            dve.tensor_tensor(table, upto, psW, ALU.add).then_inc(added, 1)
            with dve.Fori(0, ET // 2) as i:
                link.enter(i, 2)
                for u in range(2):
                    t = i * 2 + u
                    dve.wait_ge(looked, t)
                    dve.tensor_scalar(oh_lo[u], m.iota[:, 0:P], lof[:, ds(t, 1)], None, ALU.is_equal)
                    dve.tensor_scalar(dcol[u], m.onesf[:, :], keyf[:, ds(t, 1)], None, ALU.mult)
                    dve.tensor_scalar(oh_hi[u], m.iota[:, :], hif[:, ds(t, 1)], None,
                                      ALU.is_equal).then_inc(hot2, 1)
                    dve.wait_ge(turned, t + 1)
                    dve.scalar_tensor_tensor(junk1, psD, keyf[:, ds(t, 1)], m.tri[:, :],
                                             ALU.is_equal, ALU.mult,
                                             accum_out=inside[:, ds(t, 1)])
                    dve.wait_ge(looked, t + 1)
                    link(dve.scalar_tensor_tensor(junk2, m.iota[:, :], hif[:, ds(t, 1)], psG,
                                             ALU.is_equal, ALU.mult,
                                             accum_out=before[:, ds(t, 1)]))
                    dve.tensor_tensor(table, table, psN, ALU.add).then_inc(added, 1)
                link.leave(ET // 2)
            dve.wait_ge(added, ET + 1)
            link(dve.tensor_tensor(rank, before, inside, ALU.add))
            dve.tensor_copy(rank_i, rank).then_inc(ranked, 1)

        @block.scalar
        def _(act):
            with act.Fori(0, ET // 2) as i:
                for u in range(2):
                    act.wait_ge(turned, i * 2 + (u + 1))
                    act.activation(oh_loT[u], psLT, ACT.Copy).then_inc(turned_out, 1)

        @block.tensor
        def _(pe):
            pe.wait_ge(cleared, 5)
            pe.matmul(psC, zero[:, 0:P], zero, start=True, stop=False).then_inc(counted, 1)
            with pe.Fori(0, ET // 2) as i:
                for u in range(2):
                    pe.wait_ge(hot, i * 2 + (u + 1))
                    pe.matmul(psC, oh_lo[u], oh_hi[u], start=False, stop=False).then_inc(counted, 1)
            pe.matmul(psC, zero[:, 0:P], zero, start=False, stop=True).then_inc(counted, 1)
            pe.wait_ge(split, 1)
            pe.matmul(psW, m.triu[:, :], count, start=True, stop=True)
            pe.matmul(psX, m.onesf[:, :], count, start=True, stop=True).then_inc(summed, 1)
            with pe.Fori(0, ET // 2) as i:
                for u in range(2):
                    t = i * 2 + u
                    pe.wait_ge(hot2, t + 1)
                    pe.transpose(psLT, oh_lo[u], m.identb[:, :])
                    pe.transpose(psD, dcol[u], m.ident[:, :]).then_inc(turned, 1)
                    pe.wait_ge(turned_out, t + 1)
                    pe.wait_ge(added, t + 1)
                    pe.matmul(psN, oh_lo[u], oh_hi[u], start=True, stop=True)
                    pe.matmul(psG, oh_loT[u], table, start=True, stop=True).then_inc(looked, 1)


def records(nc, sem, m):
    cut = Carve(m.xs)
    lastc, far = cut(ET), cut(ET)
    posidx, place = cut(ET).bitcast(I32), cut(ET).bitcast(I32)
    clear = cut(N // NQ).bitcast(I32)
    row, prev, nxt = cut(2 * P), cut(P), cut(P)
    keep, last = cut(P), cut(P)
    ends = cut(4)
    idx_s = [cut(G).bitcast(I32) for _ in range(2)]
    val_s = [cut(G).bitcast(I32) for _ in range(2)]
    psA, psL = m.PS[0:ET, 0:2 * P], m.PS[:, 512:512 + ET]
    srec3 = m.srec[:, :].rearrange("p (t c) -> p t c", c=8)
    loaded, filled, cleared, turned, rowed = (sem("re_loaded"), sem("re_filled"), sem("re_cleared"),
                                              sem("re_turned"), sem("re_rowed"))
    cols, wrote, back, flags, flipped, indexed = (sem("re_cols"), sem("re_wrote"), sem("re_back"),
                                                  sem("re_flags"), sem("re_flipped"),
                                                  sem("re_indexed"))
    kept, staged, gate, looked = sem("re_kept"), sem("re_staged"), sem("re_gate"), sem("re_looked")
    posted, slots = [sem(f"re_posted{u}") for u in range(2)], [sem(f"re_slots{u}") for u in range(2)]
    nodes_in, dve_own, moved = sem("re_nodes"), sem("re_dve"), sem("re_moved")
    with nc.Block() as block:
        @block.sync
        def _(sp):
            sp.dma_start(srec3, m.rec_d.rearrange("(t q) c -> q t c", q=P)).then_inc(loaded, 16)
            sp.wait_ge(filled, 4)
            sp.dma_start(m.pos_d.rearrange("(p t) c -> p (t c)", p=NQ), clear[0:NQ, :])\
                .then_inc(cleared, 16)
            sp.dma_start(m.row_d[0:1, 0:1], ends[0:1, 0:1]).then_inc(wrote, 16)
            sp.dma_start(m.row_d[0:1, EP + 1:EP + 2], ends[0:1, 1:2]).then_inc(wrote, 16)
            sp.dma_start(m.row_d[2:3, EP:EP + 1], ends[0:1, 2:3]).then_inc(wrote, 16)
            sp.wait_ge(rowed, 1)
            sp.dma_start(m.row_d[0, 1:EP + 1].rearrange("(t q) -> t q", q=P), row[0:ET, 0:P])\
                .then_inc(wrote, 16)
            sp.dma_start(m.row_d[1, 0:EP].rearrange("(t q) -> t q", q=P), row[0:ET, P:2 * P])\
                .then_inc(wrote, 16)
            sp.wait_ge(wrote, 80)
            sp.dma_start(prev[0:ET, :], m.row_d[0, 0:EP].rearrange("(t q) -> t q", q=P))\
                .then_inc(back, 16)
            sp.dma_start(nxt[0:ET, :], m.row_d[0, 2:EP + 2].rearrange("(t q) -> t q", q=P))\
                .then_inc(back, 16)
            sp.wait_ge(flags, 1)
            sp.dma_start(m.row_d[2, 0:EP].rearrange("(t q) -> t q", q=P), keep[0:ET, :])\
                .then_inc(kept, 16)
            for u in range(2):
                sp.wait_ge(posted[u], EG // 2 * 16 * G)
            sp.dma_start(m.posn[:, 0:NT],
                         m.pos_d[0:NT * P, :].rearrange("(p t) c -> p (t c)", p=P)).then_inc(nodes_in, 16)
            sp.dma_start(m.posn[0:REM, NT:NT + 1], m.pos_d[NT * P:N, :]).then_inc(nodes_in, 16)
            sp.wait_ge(kept, 16)
            sp.wait_ge(nodes_in, 32)

        @block.gpsimd
        def _(pool):
            pool.memset(clear, FAR).then_inc(filled, 1)
            pool.memset(m.posn[:, :], FAR).then_inc(filled, 1)
            pool.memset(ends[:, 0:2], -5.0).then_inc(filled, 1)
            pool.memset(ends[:, 2:4], 0.0).then_inc(filled, 1)
            pool.iota(place, pattern=[[P, ET]], base=0, channel_multiplier=1).then_inc(filled, 1)
            bound = pool.to_reg(N - 1)
            pool.wait_ge(indexed, 1)
            pool.wait_ge(cleared, 16)
            pool.wait_ge(filled, 5)
            with pool.Fori(0, EG // 2) as i:
                for u in range(2):
                    pool.wait_ge(posted[u], i * (16 * G))
                    pool.tensor_copy(idx_s[u], posidx[:, ds((i * 2 + u) * G, G)]).then_inc(staged, 1)
                    pool.tensor_copy(val_s[u], place[:, ds((i * 2 + u) * G, G)]).then_inc(staged, 1)
                    pool.wait_ge(staged, i * 4 + (2 * u + 2))
                    pool.sem_inc(gate, 1)
                    for t in range(G):
                        pool.indirect_dma_start(
                            m.pos_d[:, :], bass.IndirectOffsetOnAxis(ap=idx_s[u][:, t:t + 1], axis=0),
                            val_s[u][:, t:t + 1], None, bounds_check=bound,
                            oob_is_err=False).then_inc(posted[u], 16)
            for u in range(2):
                pool.wait_ge(posted[u], EG // 2 * 16 * G)
            base = 2 * EG
            with pool.Fori(0, EG // 2) as i:
                for u in range(2):
                    pool.wait_ge(slots[u], i * (16 * G))
                    pool.wait_ge(looked, i * 2 + u)
                    pool.tensor_copy(idx_s[u], m.srec[:, ds((i * 2 + u) * (8 * G), 8 * G)]
                                     .rearrange("p (t c) -> p t c", c=8)[:, :, 0]).then_inc(staged, 1)
                    pool.wait_ge(staged, i * 2 + (base + u + 1))
                    pool.sem_inc(gate, 1)
                    for t in range(G):
                        pool.indirect_dma_start(
                            val_s[u][:, t:t + 1], None, m.pos_d[:, :],
                            bass.IndirectOffsetOnAxis(ap=idx_s[u][:, t:t + 1], axis=0))\
                            .then_inc(slots[u], 16)

        @block.vector
        def _(dve):
            link = Link(dve, dve_own)
            dve.wait_ge(loaded, 16)
            dve.memset(m.dstc[:, 0:1], -5.0)
            dve.tensor_copy(m.dstc[:, 1:ET + 1], srec3[:, :, 1])
            dve.tensor_copy(m.relc[:, :], srec3[:, :, 2]).then_inc(cols, 1)
            dve.wait_ge(back, 32)
            dve.tensor_tensor(keep[0:ET, :], row[0:ET, 0:P], prev[0:ET, :], ALU.is_equal)
            dve.tensor_tensor(last[0:ET, :], row[0:ET, 0:P], nxt[0:ET, :], ALU.not_equal)\
                .then_inc(flags, 1)
            dve.wait_ge(flipped, 1)
            link(dve.tensor_copy(lastc, psL))
            link(dve.tensor_scalar(far, lastc, -float(FAR), float(FAR), ALU.mult, ALU.add))
            link(dve.tensor_tensor(lastc, lastc, m.dstc[:, 1:ET + 1], ALU.mult))
            link(dve.tensor_tensor(lastc, lastc, far, ALU.add))
            dve.tensor_copy(posidx, lastc).then_inc(indexed, 1)
            with dve.Fori(0, EG // 2) as i:
                for u in range(2):
                    dve.wait_ge(slots[u], i * (16 * G) + 16 * G)
                    dve.tensor_copy(m.poss[:, ds((i * 2 + u) * G, G)], val_s[u]).then_inc(looked, 1)
            dve.wait_ge(looked, EG)
            dve.tensor_scalar(m.masks[:, :], m.poss[:, :], float(EP), None, ALU.is_lt)
            dve.wait_ge(nodes_in, 32)
            dve.tensor_scalar(m.maskn[:, :], m.posn[:, :], float(EP), None, ALU.is_lt)

        @block.scalar
        def _(act):
            act.wait_ge(turned, 1)
            act.activation(row[0:ET, :], psA, ACT.Copy).then_inc(rowed, 1)

        @block.tensor
        def _(pe):
            pe.wait_ge(cols, 1)
            pe.transpose(psA[:, 0:P], m.dstc[:, 1:ET + 1], m.ident[:, :])
            pe.transpose(psA[:, P:2 * P], m.relc[:, :], m.ident[:, :]).then_inc(turned, 1)
            pe.wait_ge(flags, 1)
            pe.transpose(psL, last[0:ET, :], m.ident[0:ET, 0:ET]).then_inc(flipped, 1)


def records_by_src(nc, sem, m):
    cut = Carve(m.xs)
    lastc, far = cut(ET), cut(ET)
    row, nxt, last, ends = cut(P), cut(P), cut(P), cut(4)
    psA, psL = m.PS[0:ET, 0:P], m.PS[:, 512:512 + ET]
    loaded, cleared, cols, turned, rowed = (sem("rs_loaded"), sem("rs_cleared"), sem("rs_cols"),
                                            sem("rs_turned"), sem("rs_rowed"))
    wrote, back, flags, flipped, dve_own = (sem("rs_wrote"), sem("rs_back"), sem("rs_flags"),
                                            sem("rs_flipped"), sem("rs_dve"))
    srec3 = m.srec2[:, :].rearrange("p (t c) -> p t c", c=8)
    with nc.Block() as block:
        @block.gpsimd
        def _(pool):
            pool.memset(ends, -5.0).then_inc(cleared, 1)

        @block.sync
        def _(sp):
            sp.dma_start(srec3, m.rec2_d.rearrange("(t q) c -> q t c", q=P)).then_inc(loaded, 16)
            sp.wait_ge(cleared, 1)
            sp.dma_start(m.row2_d[0:1, EP:EP + 1], ends[0:1, 0:1]).then_inc(wrote, 16)
            sp.wait_ge(rowed, 1)
            sp.dma_start(m.row2_d[0, 0:EP].rearrange("(t q) -> t q", q=P), row[0:ET, :])\
                .then_inc(wrote, 16)
            sp.wait_ge(wrote, 32)
            sp.dma_start(nxt[0:ET, :], m.row2_d[0, 1:EP + 1].rearrange("(t q) -> t q", q=P))\
                .then_inc(back, 16)
            sp.wait_ge(back, 16)

        @block.vector
        def _(dve):
            link = Link(dve, dve_own)
            dve.wait_ge(loaded, 16)
            dve.memset(m.srcc[:, 0:1], -5.0)
            dve.tensor_copy(m.srcc[:, 1:ET + 1], srec3[:, :, 0]).then_inc(cols, 1)
            dve.wait_ge(back, 16)
            dve.tensor_tensor(last[0:ET, :], row[0:ET, :], nxt[0:ET, :], ALU.not_equal)\
                .then_inc(flags, 1)
            dve.wait_ge(flipped, 1)
            link(dve.tensor_copy(lastc, psL))
            link(dve.tensor_scalar(far, lastc, -float(FAR), float(FAR), ALU.mult, ALU.add))
            link(dve.tensor_tensor(lastc, lastc, m.srcc[:, 1:ET + 1], ALU.mult))
            link(dve.tensor_tensor(lastc, lastc, far, ALU.add))
            dve.tensor_copy(m.to_node[:, :], lastc)

        @block.scalar
        def _(act):
            act.wait_ge(turned, 1)
            act.activation(row[0:ET, :], psA, ACT.Copy).then_inc(rowed, 1)

        @block.tensor
        def _(pe):
            pe.wait_ge(cols, 1)
            pe.transpose(psA, m.srcc[:, 1:ET + 1], m.ident[:, :]).then_inc(turned, 1)
            pe.wait_ge(flags, 1)
            pe.transpose(psL, last[0:ET, :], m.ident[0:ET, 0:ET]).then_inc(flipped, 1)


def small_weights(nc, sem, m):
    cut = Carve(m.xs)
    att = [cut(D) for _ in range(3)]
    we, tmp, eas, b2_b = cut(D), cut(2 * D), cut(ED), cut(D)
    ea_all = m.xh[0:EQ, 0:ET * ED]
    meane = m.PS[0:ED, 0:1]
    loaded, eas_in, rowsum, summed, mean, drawn, dve_own = (
        sem("sw_loaded"), sem("sw_eas_in"), sem("sw_rowsum"), sem("sw_summed"), sem("sw_mean"),
        sem("sw_drawn"), sem("sw_dve"))
    biased = sem("sw_biased")
    with nc.Block() as block:
        @block.sync
        def _(sp):
            sp.dma_start(ea_all, m.ea.rearrange("(p t) c -> p (t c)", t=ET)).then_inc(eas_in, 16)
            sp.dma_start(m.w0[:, :].rearrange("p (k n) -> p k n", k=2),
                         m.W0.rearrange("(k p) n -> p k n", p=P)).then_inc(loaded, 16)
            sp.dma_start(we[0:ED, :], m.Wedge).then_inc(loaded, 16)
            for a, dest in ((m.att_src, att[0]), (m.att_dst, att[1]), (m.att_edge, att[2])):
                sp.dma_start(dest, a.rearrange("h c -> (h c)").partition_broadcast(P))\
                    .then_inc(loaded, 16)
            sp.dma_start(m.bias0_b[:, :], m.bias0.partition_broadcast(P)).then_inc(loaded, 16)
            sp.dma_start(m.bias1_b[:, :], m.biases[1, :].partition_broadcast(P)).then_inc(loaded, 16)
            sp.dma_start(m.b12_b[:, :], m.b1.partition_broadcast(P)).then_inc(loaded, 16)
            sp.dma_start(b2_b, m.b2.partition_broadcast(P)).then_inc(loaded, 16)
            sp.dma_start(m.comps_b[:, :],
                         m.comps[0:2].rearrange("l r b -> (l r b)").partition_broadcast(P))\
                .then_inc(loaded, 16)
            for k in range(2):
                sp.dma_start(m.b0col[:, k:k + 1], m.biases[0, k * P:(k + 1) * P].unsqueeze(1))\
                    .then_inc(loaded, 16)
            sp.wait_ge(loaded, 192)
            sp.wait_ge(eas_in, 16)

        @block.vector
        def _(dve):
            link = Link(dve, dve_own)
            dve.wait_ge(eas_in, 16)
            dve.tensor_reduce(eas[0:EQ, :], ea_all.rearrange("p (t c) -> p c t", c=ED), AX_X,
                              ALU.add).then_inc(rowsum, 1)
            dve.wait_ge(loaded, 192)
            for j in range(2):
                for k in range(2):
                    link(dve.tensor_tensor(tmp[:, k * D:(k + 1) * D], m.w0[:, k * D:(k + 1) * D],
                                           att[j], ALU.mult))
                for k in range(2):
                    link(dve.tensor_reduce(m.wa[:, k * 3 * H + j * H:k * 3 * H + (j + 1) * H],
                                           tmp[:, k * D:(k + 1) * D].rearrange(
                                               "p (h c) -> p h c", c=C), AX_X, ALU.add))
            for k in range(2):
                o = k * 3 * H
                dve.tensor_tensor(m.wa[:, o + 2 * H:o + 3 * H], m.wa[:, o:o + H],
                                  m.wa[:, o + H:o + 2 * H], ALU.add)
            dve.tensor_tensor(m.b12_b[:, :], m.b12_b[:, :], b2_b, ALU.add)
            link(dve.tensor_tensor(tmp[0:ED, 0:D], we[0:ED, :], att[2][0:ED, :], ALU.mult))
            link(dve.tensor_reduce(m.we8[:, :], tmp[0:ED, 0:D].rearrange("p (h c) -> p h c", c=C),
                                   AX_X, ALU.add))
            dve.wait_ge(summed, 1)
            dve.tensor_scalar(m.emean[:, :], meane, 1.0 / E, None, ALU.mult).then_inc(mean, 1)
            dve.wait_ge(drawn, 1)
            dve.tensor_copy(m.amean[:, :], m.PS[0:H, 512:513])

        @block.tensor
        def _(pe):
            pe.wait_ge(rowsum, 1)
            pe.matmul(meane, eas[0:EQ, :], m.onesf[0:EQ, 0:1], start=True, stop=True)\
                .then_inc(summed, 1)
            pe.wait_ge(mean, 1)
            pe.matmul(m.PS[0:H, 512:513], m.we8[:, :], m.emean[:, :], start=True, stop=True)\
                .then_inc(drawn, 1)


def to_edge_major(dve, link, heads, scratch, out):
    link(dve.transpose(scratch[0:32, :], heads[0:32, :]))
    blocks = scratch[0:32, :].rearrange("p (t j c) -> p t j c", j=4, c=32)
    for j in range(4):
        last = dve.tensor_copy(out[32 * j:32 * j + 32, :].rearrange("p (t c) -> p t c", c=8),
                               blocks[:, :, j, 0:8])
    link(last)


def counts(nc, sem, m):
    sA, sL, sF, sK = (m.big[:, k * EP:(k + 1) * EP] for k in range(4))
    keep_next = m.big[0:R, 3 * EP + 1:4 * EP + 1]
    cut = Carve(m.xs)
    cnt, oh, tmp, sel, w = cut(ET * R), cut(ET * R), cut(ET * R), cut(ET), cut(ET)
    cleared, keeps, rels, dve_own = sem("co_cleared"), sem("co_keeps"), sem("co_rels"), sem("co_dve")

    def by8(ap):
        return ap.rearrange("p (t r) -> p t r", r=R)

    with nc.Block() as block:
        @block.gpsimd
        def _(pool):
            pool.memset(sA[0:32, :], 0.0).then_inc(cleared, 1)
            pool.memset(sL[0:32, :], 0.0).then_inc(cleared, 1)

        @block.sync
        def _(sp):
            sp.dma_start(m.big[0:R, 3 * EP:4 * EP + 1],
                         m.row_d[2, 0:EP + 1].partition_broadcast(R)).then_inc(keeps, 16)
            sp.wait_ge(cleared, 2)
            sp.dma_start(sL[0:R, :], m.row_d[1, 0:EP].partition_broadcast(R)).then_inc(rels, 16)
            sp.wait_ge(rels, 16)
            sp.wait_ge(keeps, 16)

        @block.vector
        def _(dve):
            link = Link(dve, dve_own)
            dve.wait_ge(rels, 16)
            dve.wait_ge(cleared, 2)
            link(dve.tensor_scalar(sA[0:R, :], sL[0:R, :], m.part[0:R, :], None, ALU.is_equal))
            dve.wait_ge(keeps, 16)
            link(dve.tensor_tensor_scan(sF[0:R, :], sK[0:R, :], sA[0:R, :], 0.0, ALU.mult, ALU.add))
            link(dve.tensor_tensor_scan(sA[0:R, ::-1], keep_next[:, ::-1], sF[0:R, ::-1], 0.0,
                                        ALU.mult, ALU.max))
            to_edge_major(dve, link, sA, sF, cnt)
            dve.tensor_scalar(m.big[0:R, 3 * EP:4 * EP + 1], m.big[0:R, 3 * EP:4 * EP + 1], -1.0,
                              BIG, ALU.add, ALU.mult)
            dve.tensor_copy(w, m.srec[:, :].bitcast(F32).rearrange("p (t c) -> p t c", c=8)[:, :, 3])
            link(dve.tensor_tensor(by8(oh), m.iota[:, 0:R].unsqueeze(1).to_broadcast([P, ET, R]),
                                   bc(m.relc[:, :], R), ALU.is_equal))
            dve.tensor_tensor(by8(m.co1[:, :]), by8(oh), bc(w, R), ALU.mult)
            dve.tensor_reduce(m.co3[:, :], by8(cnt), AX_X, ALU.add)
            link(dve.tensor_tensor(tmp, oh, cnt, ALU.mult))
            link(dve.tensor_reduce(sel, by8(tmp), AX_X, ALU.add))
            dve.tensor_scalar(m.co3[:, :], m.co3[:, :], 1.0, None, ALU.max)
            link(dve.tensor_scalar(sel, sel, 1.0, None, ALU.max))
            dve.reciprocal(m.co3[:, :], m.co3[:, :])
            link(dve.reciprocal(sel, sel))
            for l in range(2):
                for b in range(NB):
                    comp = m.comps_b[:, l * R * NB:(l + 1) * R * NB].rearrange(
                        "p (r b) -> p b r", b=NB)[:, b:b + 1, :].to_broadcast([P, ET, R])
                    link(dve.tensor_tensor(by8(tmp), by8(oh), comp, ALU.mult))
                    col = m.co2[l][:, :].rearrange("p (t b) -> p t b", b=NB)[:, :, b:b + 1]
                    link(dve.tensor_reduce(col, by8(tmp), AX_X, ALU.add))
                    link(dve.tensor_tensor(col, col, sel.unsqueeze(2), ALU.mult))


def ln_stats(dve, link, m, rows, u, done):
    n = len(rows)
    for t, r in enumerate(rows):
        last = dve.bn_stats(m.st[:, (u * G + t) * 6:(u * G + t + 1) * 6], r)
    link(last)
    dve.sem_inc(m.gate_dve, 1)
    for t in range(n):
        last = dve.bn_aggr(m.mv[:, (u * G + t) * 2:(u * G + t + 1) * 2],
                           m.st[:, (u * G + t) * 6:(u * G + t + 1) * 6])
    last.then_inc(done, 1)


def ln_parts(m, u, n):
    mv = m.mv[:, u * G * 2:(u * G + n) * 2].rearrange("p (t c) -> p t c", c=2)
    s = [m.ln[:, (u * 4 + k) * G:(u * 4 + k) * G + n] for k in range(4)]
    return mv[:, :, 0], mv[:, :, 1], s


def ln_scales(dve, link, m, u, n, done):
    mean, var, (std, nmr, a, r) = ln_parts(m, u, n)
    link(dve.reciprocal(r, std))
    link(dve.scalar_tensor_tensor(a, var, EPS, r, ALU.add, ALU.mult))
    link(dve.tensor_tensor(a, a, r, ALU.mult))
    link(dve.tensor_scalar(a, a, -0.5, 1.5, ALU.mult, ALU.add))
    link(dve.tensor_tensor(std, r, a, ALU.mult))
    dve.scalar_tensor_tensor(nmr, mean, -1.0, std, ALU.mult, ALU.mult).then_inc(done, 1)


def ln_apply(act, m, rows, u, h, done):
    _, _, (rstd, nmr, _, _) = ln_parts(m, u, len(rows))
    for t, r in enumerate(rows):
        last = act.activation(h[:, t * D:(t + 1) * D], r, ACT.Relu, scale=rstd[:, t:t + 1],
                              bias=nmr[:, t:t + 1])
    last.then_inc(done, 1)


def turn(pe, m, h, ps, n, done):
    for k in range(2):
        for t in range(n):
            last = pe.transpose(ps[:, k * 512 + t * P:k * 512 + (t + 1) * P],
                                h[:, t * D + k * P:t * D + (k + 1) * P], m.ident[:, :])
    last.then_inc(done, 1)


def logits(nc, sem, m):
    sA, sL, sF, _ = (m.big[:, k * EP:(k + 1) * EP] for k in range(4))
    cut = Carve(sF)
    gs, gd, ge = ([cut(GD) for _ in range(2)], [cut(GD) for _ in range(2)],
                  [cut(G * ED) for _ in range(2)])
    psE, psA, psZ = m.PS[0:ED, 1024:1536], m.PS[0:H, 1536:2048], m.PS[0:H, 2048:2560]
    psY = [m.PS[:, 3072:3584], m.PS[:, 3584:4096]]
    blank, staged, gate = sem("lo_blank"), sem("lo_staged"), sem("lo_gate")
    src_in, dst_in, ea_in = ([sem(f"lo_{k}_in{u}") for u in range(2)] for k in ("src", "dst", "ea"))
    stats, std, scales, hs = (sem("lo_stats"), sem("lo_std"), sem("lo_scales"), sem("lo_h"))
    kept, eturn = ([sem(f"lo_{k}{u}") for u in range(2)] for k in ("kept", "eturn"))
    turned, tout, eout = sem("lo_turned"), sem("lo_tout"), sem("lo_eout")
    prods, pout, logit, lout, dve_own = (sem("lo_prods"), sem("lo_pout"), sem("lo_logit"),
                                         sem("lo_lout"), sem("lo_dve"))

    def tiles(buf):
        return [buf[:, t * D:(t + 1) * D] for t in range(G)]

    with nc.Block() as block:
        @block.gpsimd
        def _(pool):
            for b in (*gs, *gd, *ge):
                pool.memset(b, 0.0).then_inc(blank, 1)
            pool.wait_ge(blank, 6)
            bx, be = pool.to_reg(N - 1), pool.to_reg(E - 1)
            with pool.Fori(0, EG // 2) as i:
                for u in range(2):
                    g = i * 2 + u
                    pool.wait_ge(src_in[u], i * (16 * G))
                    pool.wait_ge(dst_in[u], i * (16 * G))
                    pool.wait_ge(ea_in[u], i * (16 * G))
                    pool.tensor_copy(m.idx_s[u][:, :], m.srec[:, ds(g * (8 * G), 8 * G)])\
                        .then_inc(staged, 1)
                    pool.wait_ge(staged, g + 1)
                    pool.wait_ge(kept[u], i)
                    pool.wait_ge(eturn[u], i)
                    pool.sem_inc(gate, 1)
                    for t in range(G):
                        def row(c):
                            return bass.IndirectOffsetOnAxis(
                                ap=m.idx_s[u][:, 8 * t + c:8 * t + c + 1], axis=0)
                        pool.indirect_dma_start(gs[u][:, t * D:(t + 1) * D], None, m.x[:, :],
                                                row(0), bounds_check=bx, oob_is_err=False)\
                            .then_inc(src_in[u], 16)
                        pool.indirect_dma_start(gd[u][:, t * D:(t + 1) * D], None, m.x[:, :],
                                                row(1), bounds_check=bx, oob_is_err=False)\
                            .then_inc(dst_in[u], 16)
                        pool.indirect_dma_start(ge[u][:, t * ED:(t + 1) * ED], None, m.ea[:, :],
                                                row(4), bounds_check=be, oob_is_err=False)\
                            .then_inc(ea_in[u], 16)

        @block.vector
        def _(dve):
            link = Link(dve, dve_own)
            with dve.Fori(0, EG // 2) as i:
                link.enter(i, 24)
                for u in range(2):
                    g = i * 2 + u
                    for part, (buf, came) in enumerate(((gs, src_in), (gd, dst_in))):
                        dve.wait_ge(came[u], i * (16 * G) + 16 * G)
                        dve.wait_ge(hs, g * 2 + part)
                        ln_stats(dve, link, m, tiles(buf[u]), part, stats)
                        dve.wait_ge(std, g * 2 + (part + 1))
                        ln_scales(dve, link, m, part, G, scales)
                    dve.tensor_tensor(
                        m.xs[:, ds(g * GD, GD)].rearrange("p (t d) -> p t d", t=G),
                        gs[u].rearrange("p (t d) -> p t d", t=G),
                        m.bias0_b[:, :].unsqueeze(1).to_broadcast([P, G, D]), ALU.add)\
                        .then_inc(kept[u], 1)
                    for b in range(2):
                        dve.wait_ge(prods, g * 2 + (b + 1))
                        dve.tensor_copy(m.xh[:, ds(g * GD + b * 2 * D, 2 * D)], psY[b])\
                            .then_inc(pout, 1)
                link.leave(EG // 2)

        @block.scalar
        def _(act):
            with act.Fori(0, EG // 2) as i:
                for u in range(2):
                    g = i * 2 + u
                    for part, buf in enumerate((gs, gd)):
                        _, var, s = ln_parts(m, part, G)
                        act.wait_ge(stats, g * 2 + (part + 1))
                        act.activation(s[0], var, ACT.Sqrt, bias=m.eps[:, :]).then_inc(std, 1)
                        act.wait_ge(scales, g * 2 + (part + 1))
                        act.wait_ge(turned, g * 2 + part)
                        ln_apply(act, m, tiles(buf[u]), part, m.h[part], hs)
                        act.wait_ge(turned, g * 2 + (part + 1))
                        act.wait_ge(logit, g)
                        act.activation(m.hT[part][:, :], m.PS[:, 0:1024], ACT.Copy).then_inc(tout, 1)
                    act.wait_ge(eturn[u], i + 1)
                    act.activation(m.eaT[:, :], psE, ACT.Copy).then_inc(eout, 1)
                    act.wait_ge(logit, g + 1)
                    act.activation(sA[0:H, ds(g * 512, 512)], psA, ACT.Copy)
                    act.activation(sL[0:H, ds(g * 512, 512)], psZ, ACT.Identity,
                                   bias=m.amean[:, :]).then_inc(lout, 1)

        @block.tensor
        def _(pe):
            with pe.Fori(0, EG // 2) as i:
                for u in range(2):
                    g = i * 2 + u
                    for part in range(2):
                        pe.wait_ge(hs, g * 2 + (part + 1))
                        pe.wait_ge(tout, g * 2 + part)
                        turn(pe, m, m.h[part], m.PS[:, 0:1024], G, turned)
                    pe.wait_ge(ea_in[u], i * (16 * G) + 16 * G)
                    pe.wait_ge(eout, g)
                    pe.sem_inc(m.gate_pe, 1)
                    for t in range(G):
                        last = pe.transpose(psE[:, t * P:(t + 1) * P],
                                            ge[u][:, t * ED:(t + 1) * ED], m.ident[:, :])
                    last.then_inc(eturn[u], 1)
                    pe.wait_ge(tout, g * 2 + 1)
                    for b in range(2):
                        pe.wait_ge(pout, g * 2 + b)
                        for t in (2 * b, 2 * b + 1):
                            for k in range(2):
                                last = pe.matmul(psY[b][:, (t % 2) * D:(t % 2 + 1) * D],
                                                 m.hT[0][:, k * 512 + t * P:k * 512 + (t + 1) * P],
                                                 m.w0[:, k * D:(k + 1) * D],
                                                 start=(k == 0), stop=(k == 1))
                        last.then_inc(prods, 1)
                    pe.wait_ge(lout, g)
                    pe.wait_ge(tout, g * 2 + 2)
                    pe.wait_ge(eout, g + 1)
                    for k in range(2):
                        o = k * 3 * H
                        pe.matmul(psA, m.wa[:, o:o + H], m.hT[0][:, k * 512:(k + 1) * 512],
                                  start=(k == 0), stop=False)
                        pe.matmul(psA, m.wa[:, o + H:o + 2 * H], m.hT[1][:, k * 512:(k + 1) * 512],
                                  start=False, stop=False)
                        pe.matmul(psZ, m.wa[:, o + 2 * H:o + 3 * H],
                                  m.hT[1][:, k * 512:(k + 1) * 512], start=(k == 0), stop=(k == 1))
                    pe.matmul(psA, m.we8[:, :], m.eaT[:, :], start=False, stop=True)\
                        .then_inc(logit, 1)


def softmax(nc, sem, m):
    sA, sL, sF, sK = (m.big[0:H, k * EP:(k + 1) * EP] for k in range(4))
    new_next = m.big[0:H, 3 * EP + 1:4 * EP + 1]
    sub, exps, dve_own = sem("sm_sub"), sem("sm_exp"), sem("sm_dve")
    with nc.Block() as block:
        @block.vector
        def _(dve):
            link = Link(dve, dve_own)
            dve.scalar_tensor_tensor(sA, sA, SLOPE, sA, ALU.mult, ALU.max)
            link(dve.scalar_tensor_tensor(sL, sL, SLOPE, sL, ALU.mult, ALU.max))
            link(dve.tensor_tensor(sF, sA, sL, ALU.max))
            link(dve.tensor_tensor_scan(sF, sK, sF, -BIG, ALU.add, ALU.max))
            link(dve.tensor_tensor_scan(sF[:, ::-1], new_next[:, ::-1], sF[:, ::-1], -BIG,
                                        ALU.add, ALU.max))
            dve.tensor_tensor(sA, sA, sF, ALU.subtract).then_inc(sub, 1)
            dve.tensor_tensor(sL, sL, sF, ALU.subtract).then_inc(sub, 1)
            full = [m.big[:, k * EP:(k + 1) * EP] for k in range(3)]
            dve.wait_ge(sub, 2)
            dve.wait_ge(exps, 1)
            to_edge_major(dve, link, full[0], full[2], m.ex)
            dve.wait_ge(exps, 2)
            to_edge_major(dve, link, full[1], full[2], m.exs)

        @block.scalar
        def _(act):
            for k, s in enumerate((sA, sL)):
                act.wait_ge(sub, k + 1)
                act.activation(s, s, ACT.Exp).then_inc(exps, 1)


def weights(nc, sem, m):
    raw = m.h[0], m.h[1]
    loaded, raws, cleared, turned, dve_own = (sem("we_loaded"), sem("we_raws"), sem("we_cleared"),
                                              sem("we_turned"), sem("we_dve"))
    with nc.Block() as block:
        @block.gpsimd
        def _(pool):
            pool.memset(m.bd, 0.0).then_inc(cleared, 1)

        @block.sync
        def _(sp):
            for n, w in enumerate((m.W1, m.W2)):
                sp.dma_start(raw[n][:, 0:2 * D].rearrange("p (j c) -> p j c", j=2),
                             w.rearrange("(j p) c -> p j c", p=P)).then_inc(raws, 16)
            sp.dma_start(m.drow, m.row_d[0, 1:EP + 1].partition_broadcast(P)).then_inc(loaded, 16)
            for l in range(2):
                for k in range(2):
                    sp.dma_start(m.wb[l][:, k * NB * D:(k + 1) * NB * D].rearrange(
                        "p (b o) -> p b o", b=NB),
                        m.bases[l, :, k * P:(k + 1) * P, :].rearrange("b p o -> p b o"))\
                        .then_inc(loaded, 16)
                sp.dma_start(m.wr[l].rearrange("p (k o) -> p k o", k=2),
                             m.roots[l].rearrange("(k p) o -> p k o", p=P)).then_inc(loaded, 16)
            sp.wait_ge(cleared, 1)
            for k in range(2):
                for j in range(4):
                    b = 4 * k + j
                    sp.dma_start(
                        m.bd[C * j:C * (j + 1), k * R * P:(k + 1) * R * P].rearrange(
                            "i (r o) -> i r o", r=R)[:, :, C * j:C * (j + 1)],
                        m.L1w[:, b * C * C:(b + 1) * C * C].rearrange("r (i o) -> i r o", i=C))\
                        .then_inc(loaded, 16)
            sp.wait_ge(loaded, 16 * 15)

        @block.tensor
        def _(pe):
            pe.wait_ge(raws, 32)
            for n in range(2):
                for k in range(2):
                    for j in range(2):
                        last = pe.transpose(
                            m.PS[:, (n * 2 + k) * D + j * P:(n * 2 + k) * D + (j + 1) * P],
                            raw[n][:, j * D + k * P:j * D + (k + 1) * P], m.ident[:, :])
            last.then_inc(turned, 1)

        @block.vector
        def _(dve):
            dve.wait_ge(turned, 1)
            dve.tensor_copy(m.w1t, m.PS[:, 0:2 * D])
            dve.tensor_copy(m.w2t, m.PS[:, 2 * D:4 * D])
            dve.tensor_scalar(m.nmasks[:, :], m.masks[:, :], -1.0, 1.0, ALU.mult, ALU.add)
            dve.tensor_scalar(m.nmaskn[:, :], m.maskn[:, :], -1.0, 1.0, ALU.mult, ALU.add)


def each_group(eng, link, per, body):
    body(0, 0, 0, True, False)
    with eng.Fori(0, EG // 2 - 1) as i:
        if link is not None:
            link.enter(i, per)
        body(i * 2 + 1, 1, i, False, False)
        body(i * 2 + 2, 0, i + 1, False, False)
        if link is not None:
            link.leave(EG // 2 - 1)
    body(EG - 1, 1, EG // 2 - 1, False, True)


def equality(dve, m, row, col, tau, s, done):
    dve.tensor_scalar(m.eq[s][:, :], row[:, ds(tau * P, P)], col[:, ds(tau + 1, 1)], None,
                      ALU.is_equal)
    dve.tensor_scalar(m.carry[s][96:P, :], row[96:P, ds(tau * P, P)], col[96:P, ds(tau, 1)],
                      m.e127[96:P, :], ALU.is_equal, ALU.mult).then_inc(done, 1)


def edge_layer0(nc, sem, m):
    cut = Carve(m.work)
    msg = [cut(AW) for _ in range(2)]
    o = [cut(G * AW) for _ in range(2)]
    nrm = [cut(G * AW) for _ in range(2)]
    z = cut(2 * G * H)
    pss = [m.PS[:, 3072:3072 + AW], m.PS[:, 3584:3584 + AW]]
    made, summed, out_of, normed = sem("l0_made"), sem("l0_summed"), sem("l0_out"), sem("l0_norm")
    zeroed, dve_own = sem("l0_zeroed"), sem("l0_dve")
    stored = [sem(f"l0_stored{u}") for u in range(2)]

    with nc.Block() as block:
        @block.gpsimd
        def _(pool):
            pool.memset(o[1][:, 3 * AW:4 * AW], 0.0).then_inc(zeroed, 1)

        @block.vector
        def _(dve):
            link = Link(dve, dve_own)

            def norm(g, u, n):
                o4 = o[u].rearrange("p (t c) -> p t c", t=G)
                n4 = nrm[u].rearrange("p (t c) -> p t c", t=G)
                zu = z[:, u * G * H:(u + 1) * G * H].rearrange("p (t h) -> p t h", t=G)
                exs = m.exs[:, ds(g * (G * H), G * H)].rearrange("p (t h) -> p t h", t=G)
                dve.wait_ge(out_of, g * G + (G + 2))
                dve.wait_ge(stored[u], n * 32)
                link(dve.tensor_tensor(zu, o4[:, :, D:AW], exs, ALU.add))
                link(dve.tensor_scalar(zu, zu, 1e-16, None, ALU.add))
                link(dve.reciprocal(zu, zu))
                for t in range(G):
                    dve.tensor_tensor(n4[:, t, 0:D].rearrange("p (h c) -> p h c", c=C),
                                      o4[:, t, 0:D].rearrange("p (h c) -> p h c", c=C),
                                      bc(zu[:, t, :], C), ALU.mult)
                dve.tensor_tensor(n4[:, :, D:AW], exs, zu, ALU.mult).then_inc(normed, 1)

            def body(g, u, n, first, last):
                for t in range(G):
                    s = t % 2
                    tau = g * G + t
                    dve.wait_ge(summed, tau + 1)
                    dve.tensor_tensor(msg[s][:, 0:D].rearrange("p (h c) -> p h c", c=C),
                                      m.xh[:, ds(tau * D, D)].rearrange("p (h c) -> p h c", c=C),
                                      bc(m.ex[:, ds(tau * H, H)], C), ALU.mult)
                    dve.tensor_copy(msg[s][:, D:AW], m.ex[:, ds(tau * H, H)])
                    equality(dve, m, m.drow, m.dstc, tau, s, made)
                    if t == 1 and not first:
                        norm(g - 1, 1 - u, n - (1 - u))

            each_group(dve, link, 6, body)
            norm(EG - 1, 1, EG // 2 - 1)

        @block.tensor
        def _(pe):
            pe.sem_inc(summed, 2)
            pe.wait_ge(zeroed, 1)

            def body(g, u, n, first, last):
                for t in range(G):
                    s = t % 2
                    tau = g * G + t
                    prev = (o[u][96:P, (t - 1) * AW:t * AW] if t else o[1 - u][96:P, 3 * AW:4 * AW])
                    pe.wait_ge(made, tau + 1)
                    pe.wait_ge(out_of, tau + 1)
                    pe.matmul(pss[s], m.eq[s][:, :], msg[s], start=True, stop=False)
                    pe.wait_ge(out_of, tau + 2)
                    pe.matmul(pss[s], m.carry[s][96:P, :], prev, start=False, stop=True)\
                        .then_inc(summed, 1)
            each_group(pe, None, 0, body)

        @block.scalar
        def _(act):
            act.sem_inc(out_of, 2)

            def body(g, u, n, first, last):
                if not first:
                    act.wait_ge(normed, g - 1)
                for t in range(G):
                    act.wait_ge(summed, g * G + (t + 3))
                    act.activation(o[u][:, t * AW:(t + 1) * AW], pss[t % 2], ACT.Copy)\
                        .then_inc(out_of, 1)
            each_group(act, None, 0, body)

        @block.sync
        def _(sp):
            def body(g, u, n, first, last):
                sp.wait_ge(normed, g + 1)
                n4 = nrm[u].rearrange("p (t c) -> p t c", t=G)
                sp.dma_start(m.a_d[0].rearrange("(t q) c -> q t c", q=P)[:, ds(g * G, G), :], n4)\
                    .then_inc(stored[u], 16)
                sp.dma_start(m.tab_d.rearrange("(t q) c -> q t c", q=P)[:, ds(g * G, G), 0:H],
                             n4[:, :, D:AW]).then_inc(stored[u], 16)
            each_group(sp, None, 0, body)
            for u in range(2):
                sp.wait_ge(stored[u], EG // 2 * 32)


def edge_layer(nc, sem, m, k):
    halves = 2 if k == 1 else 1
    comps = 4
    co = {1: m.co1, 2: m.co2[0], 3: m.co2[1]}[k]
    nco = halves * comps
    root = k == 2
    gw = AW if k == 1 else D
    cut = Carve(m.work)
    msg = [cut(D) for _ in range(2)]
    o = [cut(GD) for _ in range(2)]
    rows = [cut(G * gw) for _ in range(2)]
    a0, a01 = (cut(GD), cut(GD)) if k == 1 else (None, None)
    psT = m.PS[:, 0:1024]
    psB = [m.PS[:, 1024:2048], m.PS[:, 2048:3072]]
    psR = m.PS[:, 3072:3072 + D]
    psS = [m.PS[:, (3584 if root else 3072):][:, 0:D], m.PS[:, 3584:3584 + D]]
    free = 2 if root else 1
    table = m.a_d[k - 1]
    col = H + (k - 1) * D
    tab = m.tab_d.rearrange("(t q) c -> q t c", q=P)[:, :, col:col + D]

    def s_(name):
        return sem(f"l{k}_{name}")

    blank, staged, gate, zeroed = s_("blank"), s_("staged"), s_("gate"), s_("zeroed")
    stats, std, scales, hs = s_("stats"), s_("std"), s_("scales"), s_("h")
    turned, tout = s_("turned"), s_("tout")
    prods, eaten, rooted, rout = s_("prods"), s_("eaten"), s_("rooted"), s_("rout")
    made, summed, out_of, dve_own = s_("made"), s_("summed"), s_("out"), s_("dve")
    rows_in, updated, o_sent, tab_sent = ([s_(f"{name}{u}") for u in range(2)] for name in
                                          ("rows_in", "updated", "o_sent", "tab_sent"))
    if k == 1:
        a0_in, joined, a01_sent = s_("a0_in"), s_("joined"), s_("a01_sent")

    with nc.Block() as block:
        @block.gpsimd
        def _(pool):
            for b in rows:
                pool.memset(b, 0.0).then_inc(blank, 1)
            pool.memset(o[1][:, 3 * D:4 * D], 0.0).then_inc(zeroed, 1)
            pool.wait_ge(blank, 2)
            bound = pool.to_reg(EP - 1)

            def gather(g, u, n):
                pool.wait_ge(rows_in[u], n * (16 * G))
                pool.wait_ge(updated[u], n)
                pool.tensor_copy(m.idx_s[u][:, 0:G], m.poss[:, ds(g * G, G)]).then_inc(staged, 1)
                pool.wait_ge(staged, g + 1)
                pool.sem_inc(gate, 1)
                for t in range(G):
                    pool.indirect_dma_start(
                        rows[u][:, t * gw:(t + 1) * gw], None, table,
                        bass.IndirectOffsetOnAxis(ap=m.idx_s[u][:, t:t + 1], axis=0),
                        bounds_check=bound, oob_is_err=False).then_inc(rows_in[u], 16)

            def body(g, u, n, first, last):
                if not last:
                    gather(g + 1, 1 - u, n + u)
                if k == 1:
                    pool.wait_ge(a0_in, g * 16 + 16)
                    pool.wait_ge(out_of, g * G + (G + 2))
                    pool.wait_ge(a01_sent, g * 16)
                    pool.sem_inc(gate, 1)
                    pool.tensor_tensor(a01, a0, o[u], ALU.add).then_inc(joined, 1)

            gather(0, 0, 0)
            each_group(pool, None, 0, body)

        @block.sync
        def _(sp):
            def body(g, u, n, first, last):
                if k == 1:
                    sp.wait_ge(joined, g)
                    sp.dma_start(a0.rearrange("p (t c) -> p t c", t=G),
                                 table.rearrange("(t q) c -> q t c", q=P)[:, ds(g * G, G), 0:D])\
                        .then_inc(a0_in, 16)
                sp.wait_ge(out_of, g * G + (G + 2))
                o4 = o[u].rearrange("p (t c) -> p t c", t=G)
                if k < 3:
                    sp.dma_start(m.a_d[k].rearrange("(t q) c -> q t c", q=P)[:, ds(g * G, G), :],
                                 o4).then_inc(o_sent[u], 16)
                if k > 1:
                    sp.dma_start(tab[:, ds(g * G, G), :], o4).then_inc(tab_sent[u], 16)
                else:
                    sp.wait_ge(joined, g + 1)
                    sp.dma_start(tab[:, ds(g * G, G), :], a01.rearrange("p (t c) -> p t c", t=G))\
                        .then_inc(a01_sent, 16)

            each_group(sp, None, 0, body)
            for u in range(2):
                if k < 3:
                    sp.wait_ge(o_sent[u], EG // 2 * 16)
                if k > 1:
                    sp.wait_ge(tab_sent[u], EG // 2 * 16)
            if k == 1:
                sp.wait_ge(a01_sent, EG * 16)

        @block.vector
        def _(dve):
            link = Link(dve, dve_own)

            def prepare(g, u, n):
                x4 = m.xs[:, ds(g * GD, GD)].rearrange("p (t d) -> p t d", t=G)
                r4 = rows[u].rearrange("p (t c) -> p t c", t=G)
                xt = [m.xs[:, ds(g * GD + t * D, D)] for t in range(G)]
                dve.wait_ge(rows_in[u], n * (16 * G) + 16 * G)
                dve.wait_ge(hs, g)
                if k == 3:
                    dve.wait_ge(turned, g)
                    for t in range(G):
                        last = dve.scalar_tensor_tensor(
                            m.h[u][:, t * D:(t + 1) * D], r4[:, t, 0:D],
                            m.masks[:, ds(g * G + t, 1)], m.xh[:, ds(g * GD + t * D, D)],
                            ALU.mult, ALU.add)
                    value = link.mark(last)
                    link.until(value)
                    dve.sem_inc(hs, 1)
                    dve.sem_inc(updated[u], 1)
                    return
                if k == 1:
                    xh8 = m.xh[:, ds(g * GD, GD)].rearrange("p (a c) -> p a c", c=C)
                    al = m.alpha[:, u * G * H:(u + 1) * G * H]
                    for t in range(G):
                        last = dve.scalar_tensor_tensor(
                            al[:, t * H:(t + 1) * H], r4[:, t, D:AW],
                            m.masks[:, ds(g * G + t, 1)],
                            m.nmasks[:, ds(g * G + t, 1)].to_broadcast([P, H]),
                            ALU.mult, ALU.add)
                    link(last)
                    link(dve.tensor_tensor(xh8, xh8, bc(al, C), ALU.mult))
                    link(dve.tensor_tensor(m.xs[:, ds(g * GD, GD)], m.xs[:, ds(g * GD, GD)],
                                           m.xh[:, ds(g * GD, GD)], ALU.add))
                for t in range(G):
                    last = dve.scalar_tensor_tensor(xt[t], r4[:, t, 0:D],
                                                    m.masks[:, ds(g * G + t, 1)], xt[t],
                                                    ALU.mult, ALU.add)
                link(last)
                dve.sem_inc(updated[u], 1)
                ln_stats(dve, link, m, xt, u, stats)
                dve.wait_ge(std, g + 1)
                ln_scales(dve, link, m, u, G, scales)

            def message(g, t):
                s, tau = t % 2, g * G + t
                dve.wait_ge(summed, tau + 1)
                for hf in range(halves):
                    q = tau * halves + hf
                    b = psB[hf if halves == 2 else s]
                    dve.wait_ge(prods, q + 1)
                    for c in range(comps):
                        if k == 1:
                            part = b.rearrange("p (k r o) -> p k r o", k=2, r=4)[:, :, c, :]
                            to = msg[s].rearrange("p (k o) -> p k o", k=2)
                        else:
                            part, to = b[:, c * D:(c + 1) * D], msg[s]
                        w = co[:, ds(tau * nco + hf * comps + c, 1)]
                        if hf == 0 and c == 0:
                            last = dve.tensor_scalar(to, part, w, None, ALU.mult)
                        else:
                            last = dve.scalar_tensor_tensor(to, part, w, to, ALU.mult, ALU.add)
                        link(last)
                    dve.sem_inc(eaten, 1)
                equality(dve, m, m.drow, m.dstc, tau, s, made)

            def body(g, u, n, first, last):
                for t in range(G):
                    message(g, t)
                    if t == 1 and not last:
                        prepare(g + 1, 1 - u, n + u)

            dve.sem_inc(eaten, 2)
            prepare(0, 0, 0)
            per = {1: 2 * (4 * 8 + 10), 2: 2 * (4 * 4 + 7), 3: 2 * (4 * 4 + 1)}[k]
            each_group(dve, link, per, body)

        @block.scalar
        def _(act):
            def normal(g, u, n):
                _, var, s = ln_parts(m, u, G)
                xt = [m.xs[:, ds(g * GD + t * D, D)] for t in range(G)]
                act.wait_ge(stats, g + 1)
                act.activation(s[0], var, ACT.Sqrt, bias=m.eps[:, :]).then_inc(std, 1)
                act.wait_ge(scales, g + 1)
                ln_apply(act, m, xt, u, m.h[u], hs)

            def turned_out(g, u):
                act.wait_ge(turned, g + 1)
                if k == 3:
                    for c in range(2):
                        last = act.activation(m.hT[u][:, c * 512:(c + 1) * 512],
                                              psT[:, c * 512:(c + 1) * 512], ACT.Relu,
                                              bias=m.b0col[:, c:c + 1])
                else:
                    last = act.activation(m.hT[u][:, :], psT, ACT.Copy)
                last.then_inc(tout, 1)

            def sum_out(tau, u, t):
                act.wait_ge(summed, tau + 3)
                act.activation(o[u][:, t * D:(t + 1) * D], psS[t % 2], ACT.Copy)\
                    .then_inc(out_of, 1)

            def root_out(g, t):
                if k == 2:
                    act.wait_ge(rooted, g * G + (t + 1))
                    act.activation(m.xh[:, ds((g * G + t) * D, D)], psR, ACT.Copy)\
                        .then_inc(rout, 1)

            def body(g, u, n, first, last):
                root_out(g, 0)
                if not first:
                    sum_out(g * G - 1, 1 - u, 3)
                if k < 3:
                    act.wait_ge(o_sent[u], n * 16)
                if k > 1:
                    act.wait_ge(tab_sent[u], n * 16)
                elif not first:
                    act.wait_ge(joined, g - 1)
                root_out(g, 1)
                sum_out(g * G, u, 0)
                if not last:
                    if k != 3:
                        normal(g + 1, 1 - u, n + u)
                root_out(g, 2)
                sum_out(g * G + 1, u, 1)
                root_out(g, 3)
                if not last:
                    turned_out(g + 1, 1 - u)
                sum_out(g * G + 2, u, 2)

            act.sem_inc(out_of, 2)
            if k == 2:
                act.sem_inc(rout, 1)
            if k != 3:
                normal(0, 0, 0)
            turned_out(0, 0)
            each_group(act, None, 0, body)
            sum_out(EP // P - 1, 1, 3)

        @block.tensor
        def _(pe):
            def products(g, u, t):
                tau = g * G + t
                s = t % 2
                hT = [m.hT[u][:, c * 512 + t * P:c * 512 + (t + 1) * P] for c in range(2)]
                pe.wait_ge(tout, g + 1)
                if root:
                    pe.wait_ge(rout, tau + 1)
                    for c in range(2):
                        last = pe.matmul(psR, hT[c], m.wr[0][:, c * D:(c + 1) * D],
                                         start=(c == 0), stop=(c == 1))
                    last.then_inc(rooted, 1)
                for hf in range(halves):
                    b = psB[hf if halves == 2 else s]
                    pe.wait_ge(eaten, tau * halves + (hf + 1))
                    if k == 1:
                        for c in range(2):
                            last = pe.matmul(b[:, c * 512:(c + 1) * 512], hT[c],
                                             m.bd[:, (c * 2 + hf) * 512:(c * 2 + hf + 1) * 512],
                                             start=True, stop=True)
                    else:
                        for j in range(2):
                            for c in range(2):
                                last = pe.matmul(
                                    b[:, j * 512:(j + 1) * 512], hT[c],
                                    m.wb[k - 2][:, (c * 2 + j) * 512:(c * 2 + j + 1) * 512],
                                    start=(c == 0), stop=(c == 1))
                    last.then_inc(prods, 1)

            def sums(tau, u, t):
                s = t % 2
                prev = (o[u][96:P, (t - 1) * D:t * D] if t else o[1 - u][96:P, 3 * D:4 * D])
                pe.wait_ge(made, tau + 1)
                pe.wait_ge(out_of, tau + free)
                pe.matmul(psS[s], m.eq[s][:, :], msg[s], start=True, stop=False)
                pe.wait_ge(out_of, tau + 2)
                pe.matmul(psS[s], m.carry[s][96:P, :], prev, start=False, stop=True)\
                    .then_inc(summed, 1)

            def turn_group(g, u):
                pe.wait_ge(hs, g + 1)
                pe.wait_ge(tout, g)
                turn(pe, m, m.h[u], psT, G, turned)

            def body(g, u, n, first, last):
                for t in range(G):
                    products(g, u, t)
                    if t == 3 and not last:
                        turn_group(g + 1, 1 - u)
                    if t:
                        sums(g * G + (t - 1), u, t - 1)
                    elif not first:
                        sums(g * G - 1, 1 - u, 3)

            pe.sem_inc(summed, 2)
            pe.wait_ge(zeroed, 1)
            turn_group(0, 0)
            each_group(pe, None, 0, body)
            sums(EP // P - 1, 1, 3)


def sage(nc, sem, m):
    MW = D + 2
    cut, cuth = Carve(m.xs), Carve(m.xh)
    srow = cuth(EP)
    rows, res = [cut(GD) for _ in range(2)], [cut(GD) for _ in range(2)]
    o, msg = [cut(G * MW) for _ in range(2)], [cut(MW) for _ in range(2)]
    inv = cut(2 * G)
    psT = m.PS[:, 0:1024]
    psB = [m.PS[:, 1024:1024 + D], m.PS[:, 1536:1536 + D]]
    psS = [m.PS[:, 2048:2048 + MW], m.PS[:, 2560:2560 + MW]]
    blank, staged, gate, ready, got_row = (sem("sg_blank"), sem("sg_staged"), sem("sg_gate"),
                                           sem("sg_ready"), sem("sg_row"))
    turned, tout, prods, made, summed, out_of, done = (
        sem("sg_turned"), sem("sg_tout"), sem("sg_prods"), sem("sg_made"), sem("sg_summed"),
        sem("sg_out"), sem("sg_done"))
    rows_in, res_in, sent = ([sem(f"sg_{k}{u}") for u in range(2)] for k in
                             ("rows_in", "res_in", "sent"))
    dve_own = sem("sg_dve")
    with nc.Block() as block:
        @block.sync
        def _(sp):
            sp.dma_start(srow, m.row2_d[0, 0:EP].partition_broadcast(P)).then_inc(got_row, 16)
            sp.wait_ge(got_row, 16)

        @block.gpsimd
        def _(pool):
            for b in (*rows, *res):
                pool.memset(b, 0.0).then_inc(blank, 1)
            pool.memset(o[1][:, 3 * MW:4 * MW], 0.0).then_inc(ready, 1)
            for b in msg:
                pool.memset(b[:, D:MW], 1.0).then_inc(ready, 1)
            pool.wait_ge(blank, 4)
            bound = pool.to_reg(N - 1)

            def gather(g, u, n):
                pool.wait_ge(rows_in[u], n * (16 * G))
                pool.wait_ge(sent[u], n * (16 * G))
                pool.tensor_copy(m.idx_s[u][:, :], m.srec2[:, ds(g * (8 * G), 8 * G)])\
                    .then_inc(staged, 1)
                pool.tensor_copy(m.idx_t[u][:, :], m.to_node[:, ds(g * G, G)]).then_inc(staged, 1)
                pool.wait_ge(staged, g * 2 + 2)
                pool.sem_inc(gate, 1)
                for t in range(G):
                    pool.indirect_dma_start(
                        rows[u][:, t * D:(t + 1) * D], None, m.h3_d[:, :],
                        bass.IndirectOffsetOnAxis(ap=m.idx_s[u][:, 8 * t + 1:8 * t + 2], axis=0),
                        bounds_check=bound, oob_is_err=False).then_inc(rows_in[u], 16)
                for t in range(G):
                    pool.indirect_dma_start(
                        res[u][:, t * D:(t + 1) * D], None, m.out[:, :],
                        bass.IndirectOffsetOnAxis(ap=m.idx_t[u][:, t:t + 1], axis=0),
                        bounds_check=bound, oob_is_err=False).then_inc(res_in[u], 16)

            def body(g, u, n, first, last):
                if not last:
                    gather(g + 1, 1 - u, n + u)
                pool.wait_ge(done, g + 1)
                pool.sem_inc(gate, 1)
                for t in range(G):
                    pool.indirect_dma_start(
                        m.out[:, :],
                        bass.IndirectOffsetOnAxis(ap=m.idx_t[u][:, t:t + 1], axis=0),
                        res[u][:, t * D:(t + 1) * D], None,
                        bounds_check=bound, oob_is_err=False).then_inc(sent[u], 16)

            gather(0, 0, 0)
            each_group(pool, None, 0, body)
            for u in range(2):
                pool.wait_ge(sent[u], EG // 2 * 16 * G)

        @block.vector
        def _(dve):
            link = Link(dve, dve_own)

            def result(g, u, n):
                o4 = o[u].rearrange("p (t c) -> p t c", t=G)
                iv = inv[:, u * G:(u + 1) * G]
                dve.wait_ge(out_of, g * G + (G + 2))
                link(dve.reciprocal(iv.unsqueeze(2), o4[:, :, D:D + 1]))
                dve.wait_ge(res_in[u], n * (16 * G) + 16 * G)
                for t in range(G):
                    r = res[u][:, t * D:(t + 1) * D]
                    last = dve.scalar_tensor_tensor(r, o4[:, t, 0:D], iv[:, t:t + 1], r,
                                                    ALU.mult, ALU.add)
                last.then_inc(done, 1)

            def body(g, u, n, first, last):
                for t in range(G):
                    s, tau = t % 2, g * G + t
                    dve.wait_ge(summed, tau + 1)
                    dve.wait_ge(prods, tau + 1)
                    dve.tensor_copy(msg[s][:, 0:D], psB[s])
                    equality(dve, m, srow, m.srcc, tau, s, made)
                    if t == 1 and not first:
                        result(g - 1, 1 - u, n - (1 - u))

            dve.wait_ge(got_row, 16)
            dve.wait_ge(ready, 3)
            each_group(dve, link, 2, body)
            result(EG - 1, 1, EG // 2 - 1)

        @block.scalar
        def _(act):
            def turned_out(g, u):
                act.wait_ge(turned, g + 1)
                act.activation(m.hT[u][:, :], psT, ACT.Copy).then_inc(tout, 1)

            def sum_out(tau, u, t):
                act.wait_ge(summed, tau + 3)
                act.activation(o[u][:, t * MW:(t + 1) * MW], psS[t % 2], ACT.Copy)\
                    .then_inc(out_of, 1)

            def body(g, u, n, first, last):
                if not first:
                    sum_out(g * G - 1, 1 - u, 3)
                    act.wait_ge(done, g - 1)
                sum_out(g * G, u, 0)
                sum_out(g * G + 1, u, 1)
                if not last:
                    turned_out(g + 1, 1 - u)
                sum_out(g * G + 2, u, 2)

            act.sem_inc(out_of, 2)
            turned_out(0, 0)
            each_group(act, None, 0, body)
            sum_out(ET - 1, 1, 3)

        @block.tensor
        def _(pe):
            def turn_group(g, u, n):
                pe.wait_ge(rows_in[u], n * (16 * G) + 16 * G)
                pe.wait_ge(tout, g)
                turn(pe, m, rows[u], psT, G, turned)

            def product(g, u, t):
                tau, s = g * G + t, t % 2
                pe.wait_ge(tout, g + 1)
                if not (isinstance(tau, int) and tau < 2):
                    pe.wait_ge(made, tau - 1)
                for c in range(2):
                    last = pe.matmul(psB[s], m.hT[u][:, c * 512 + t * P:c * 512 + (t + 1) * P],
                                     m.w2t[:, c * D:(c + 1) * D], start=(c == 0), stop=(c == 1))
                last.then_inc(prods, 1)

            def sums(tau, u, t):
                s = t % 2
                prev = (o[u][96:P, (t - 1) * MW:t * MW] if t else o[1 - u][96:P, 3 * MW:4 * MW])
                pe.wait_ge(made, tau + 1)
                pe.wait_ge(out_of, tau + 1)
                pe.matmul(psS[s], m.eq[s][:, :], msg[s], start=True, stop=False)
                pe.wait_ge(out_of, tau + 2)
                pe.matmul(psS[s], m.carry[s][96:P, :], prev, start=False, stop=True)\
                    .then_inc(summed, 1)

            def body(g, u, n, first, last):
                for t in range(G):
                    product(g, u, t)
                    if t == 3 and not last:
                        turn_group(g + 1, 1 - u, n + u)
                    if t:
                        sums(g * G + (t - 1), u, t - 1)
                    elif not first:
                        sums(g * G - 1, 1 - u, 3)

            pe.sem_inc(summed, 2)
            pe.wait_ge(ready, 3)
            turn_group(0, 0, 0)
            each_group(pe, None, 0, body)
            sums(ET - 1, 1, 3)


def at_least(eng, sem, value):
    if not (isinstance(value, int) and value <= 0):
        eng.wait_ge(sem, value)


def nodes(nc, sem, m):
    STAGES = 4
    NQI = STAGES * NG
    cut, cuth = Carve(m.xs), Carve(m.xh)
    xin, xw, y = ([cut(GD) for _ in range(NG)] for _ in range(3))
    rows = [cuth(G * TW), cuth(G * TW), m.big[:, 0:G * TW]]
    psT = [m.PS[:, 0:1024], m.PS[:, 1024:2048]]
    psY = [m.PS[:, 2048:3072], m.PS[:, 3072:4096]]
    wts = [m.w0[:, :], m.wr[0], m.wr[1], m.w1t]
    x_v = m.x[0:NT * P, :].rearrange("(p t) d -> p (t d)", p=P)
    out_v = m.out[0:NT * P, :].rearrange("(p t) d -> p (t d)", p=P)
    xin_in, rows_in, stored, h_sent = ([sem(f"n_{k}{g}") for g in range(NG)] for k in
                                       ("xin", "rows", "stored", "h_sent"))
    h3_v = m.h3_d[0:NT * P, :].rearrange("(p t) d -> p (t d)", p=P)
    blank, staged, gate = sem("n_blank"), sem("n_staged"), sem("n_gate")
    biased = [sem(f"n_biased{k}") for k in range(3)]
    stats, std, scales, hs, ys = (sem("n_stats"), sem("n_std"), sem("n_scales"), sem("n_h"),
                                  sem("n_y"))
    turned, tout, prods, eaten, final = (sem("n_turned"), sem("n_tout"), sem("n_prods"),
                                         sem("n_eaten"), sem("n_final"))
    dve_own = sem("n_dve")
    LN_AT = {0: 0, 1: NG, 3: 2 * NG}

    def where(i, q):
        if isinstance(i, int) and i == NI:
            return i, q, 0, 1
        return i + q // NQI, q % NQI // NG, q % NG, G

    def ln_no(i, q):
        i, s, g, _ = where(i, q)
        if isinstance(i, int) and i == NI:
            return i * (3 * NG) + {0: 0, 1: 1, 3: 2}[s]
        return i * (3 * NG) + (LN_AT[s] + g)

    def rows_to_use(i, s, g, n):
        src = xin[g] if s == 0 else xw[g]
        return [src[:, t * D:(t + 1) * D] for t in range(n)]

    def run(eng, link, per, body):
        with eng.Fori(0, NI - 1) as i:
            if link is not None:
                link.enter(i, per)
            body(i, True)
            if link is not None:
                link.leave(NI - 1)
        body(NI - 1, False)

    with nc.Block() as block:
        @block.sync
        def _(sp):
            def load(i, g):
                sp.dma_start(xin[g], x_v[:, ds((i * NG + g) * GD, GD)]).then_inc(xin_in[g], 16)

            def store_h(i, g):
                sp.wait_ge(hs, ln_no(i, 3 * NG + g) + 1)
                sp.dma_start(h3_v[:, ds((i * NG + g) * GD, GD)], y[g]).then_inc(h_sent[g], 16)

            def store(i, g):
                sp.wait_ge(final, i * NG + (g + 1))
                sp.dma_start(out_v[:, ds((i * NG + g) * GD, GD)], xw[g]).then_inc(stored[g], 16)

            def free(i, g):
                sp.wait_ge(biased[0], i * NG + (g + 1))
                sp.sem_inc(m.gate_sp, 1)
                sp.wait_ge(hs, ln_no(i, g) + 1)
                sp.sem_inc(m.gate_sp, 1)

            def body(i, whole):
                for g in range(NG):
                    if whole:
                        free(i, g)
                        load(i + 1, g)
                    elif g == 0:
                        free(i, g)
                        sp.dma_start(xin[0][0:REM, 0:D], m.x[NT * P:N, :]).then_inc(xin_in[0], 16)
                for g in range(NG):
                    store_h(i, g)
                for g in range(NG):
                    store(i, g)

            for g in range(NG):
                load(0, g)
            run(sp, None, 0, body)
            sp.wait_ge(hs, ln_no(NI, 3) + 1)
            sp.dma_start(m.h3_d[NT * P:N, :], y[0][0:REM, 0:D]).then_inc(h_sent[0], 16)
            sp.wait_ge(final, NI * NG + 1)
            sp.dma_start(m.out[NT * P:N, :], xw[0][0:REM, 0:D]).then_inc(stored[0], 16)
            for g in range(NG):
                sp.wait_ge(stored[g], 16 * (NI + (g == 0)))
                sp.wait_ge(h_sent[g], 16 * (NI + (g == 0)))

        @block.gpsimd
        def _(pool):
            bound = pool.to_reg(EP - 1)

            def add_bias(g, n, to, frm, bias, k):
                pool.tensor_tensor(to[:, 0:n * D].rearrange("p (t d) -> p t d", t=n),
                                   frm[:, 0:n * D].rearrange("p (t d) -> p t d", t=n),
                                   bias[:, :].unsqueeze(1).to_broadcast([P, n, D]), ALU.add)\
                    .then_inc(biased[k], 1)

            def begin(i, g, n):
                j = i * NG + g
                pool.wait_ge(xin_in[g], i * 16 + 16)
                at_least(pool, stored[g], i * 16)
                pool.sem_inc(gate, 1)
                add_bias(g, n, xw[g], xin[g], m.bias0_b, 0)
                at_least(pool, rows_in[g], i * (16 * G))
                at_least(pool, final, (i - 1) * NG + (g + 1))
                pool.sem_inc(gate, 1)
                pool.tensor_copy(m.idx_n[g][:, 0:n], m.posn[:, ds(j * G, n)]).then_inc(staged, 1)
                pool.wait_ge(staged, j + 1)
                pool.sem_inc(gate, 1)
                for t in range(n):
                    pool.indirect_dma_start(
                        rows[g][:, t * TW:(t + 1) * TW], None, m.tab_d[:, :],
                        bass.IndirectOffsetOnAxis(ap=m.idx_n[g][:, t:t + 1], axis=0),
                        bounds_check=bound, oob_is_err=False).then_inc(rows_in[g], 16)

            def middle(i, g, n, s):
                q = s if isinstance(i, int) and i == NI else s * NG + g
                pool.wait_ge(hs, ln_no(i, q) + 1)
                pool.sem_inc(gate, 1)
                add_bias(g, n, xw[g], xw[g], m.bias1_b if s == 1 else m.b12_b, 1 if s == 1 else 2)

            def body(i, whole):
                for s in (1, 3):
                    for g in range(NG):
                        middle(i, g, G, s)
                if whole:
                    for g in range(NG):
                        begin(i + 1, g, G)

            for b in rows:
                pool.memset(b, 0.0).then_inc(blank, 1)
            pool.wait_ge(blank, NG)
            for g in range(NG):
                begin(0, g, G)
            run(pool, None, 0, body)
            begin(NI, 0, 1)
            middle(NI, 0, 1, 1)
            middle(NI, 0, 1, 3)

        @block.vector
        def _(dve):
            link = Link(dve, dve_own)

            def prepare(i, q):
                u, Q = q % 2, i * NQI + q
                no = ln_no(i, q) if where(i, q)[1] != 2 else None
                i, s, g, n = where(i, q)
                if s == 2:
                    return
                if s == 0:
                    dve.wait_ge(xin_in[g], i * 16 + 16)
                at_least(dve, turned, Q - 1)
                ln_stats(dve, link, m, rows_to_use(i, s, g, n), u, stats)
                dve.wait_ge(std, no + 1)
                ln_scales(dve, link, m, u, n, scales)

            def consume(i, q):
                u = q % 2
                Q = i * NQI + q
                i, s, g, n = where(i, q)
                r4 = rows[g].rearrange("p (t c) -> p t c", t=G)
                j = i * NG + g
                ps, x = psY[u][:, 0:n * D], xw[g][:, 0:n * D]
                mask = [m.maskn[:, ds(j * G + t, 1)] for t in range(n)]
                if s == 0:
                    dve.wait_ge(rows_in[g], i * (16 * G) + 16 * n)
                    al = m.alpha[:, 0:n * H]
                    for t in range(n):
                        last = dve.scalar_tensor_tensor(
                            al[:, t * H:(t + 1) * H], r4[:, t, 0:H], mask[t],
                            m.nmaskn[:, ds(j * G + t, 1)].to_broadcast([P, H]),
                            ALU.mult, ALU.add)
                    link(last)
                dve.wait_ge(prods, Q + 1)
                if s == 0:
                    at_least(dve, h_sent[g], i * 16)
                    link(dve.tensor_tensor(y[g][:, 0:n * D].rearrange("p (a c) -> p a c", c=C),
                                           ps.rearrange("p (a c) -> p a c", c=C), bc(al, C),
                                           ALU.mult))
                    dve.sem_inc(eaten, 1)
                    dve.wait_ge(biased[0], j + 1)
                    link(dve.tensor_tensor(x, x, y[g][:, 0:n * D], ALU.add))
                elif s == 1:
                    for t in range(n):
                        last = dve.scalar_tensor_tensor(
                            y[g][:, t * D:(t + 1) * D], r4[:, t, H + D:H + 2 * D], mask[t],
                            ps[:, t * D:(t + 1) * D], ALU.mult, ALU.add)
                    link(last)
                    dve.sem_inc(eaten, 1)
                    dve.sem_inc(ys, 1)
                    return
                else:
                    dve.wait_ge(biased[1 if s == 2 else 2], j + 1)
                    link(dve.tensor_tensor(x, x, ps, ALU.add))
                    dve.sem_inc(eaten, 1)
                if s == 3:
                    dve.sem_inc(final, 1)
                    return
                c = {0: H, 2: H + 2 * D}[s]
                for t in range(n):
                    xt = x[:, t * D:(t + 1) * D]
                    last = dve.scalar_tensor_tensor(xt, r4[:, t, c:c + D], mask[t], xt,
                                                    ALU.mult, ALU.add)
                link(last)

            def body(i, whole):
                for q in range(NQI):
                    if whole or q + 2 < NQI:
                        prepare(i, q + 2)
                    consume(i, q)

            dve.sem_inc(eaten, 2)
            prepare(0, 0)
            prepare(0, 1)
            run(dve, link, NG * (3 * 6 + 4 + 1 + 2 + 1), body)
            for s in range(STAGES):
                prepare(NI, s)
                consume(NI, s)

        @block.scalar
        def _(act):
            def normal(i, q):
                u, Q = q % 2, i * NQI + q
                no = ln_no(i, q) if where(i, q)[1] != 2 else None
                i, s, g, n = where(i, q)
                if s == 2:
                    return
                _, var, sc = ln_parts(m, u, n)
                act.wait_ge(stats, no + 1)
                act.activation(sc[0], var, ACT.Sqrt, bias=m.eps[:, :]).then_inc(std, 1)
                act.wait_ge(scales, no + 1)
                at_least(act, turned, Q - 1)
                ln_apply(act, m, rows_to_use(i, s, g, n), u, y[g] if s == 3 else m.h[u], hs)

            def turned_out(i, q):
                u, Q = q % 2, i * NQI + q
                i, s, g, n = where(i, q)
                act.wait_ge(turned, Q + 1)
                at_least(act, prods, Q - 1)
                ps3 = psT[u].rearrange("p (k e) -> p k e", k=2)[:, :, 0:n * P]
                to3 = m.hT[u][:, :].rearrange("p (k e) -> p k e", k=2)[:, :, 0:n * P]
                if s == 2:
                    for c in range(2):
                        last = act.activation(to3[:, c, :], ps3[:, c, :], ACT.Relu,
                                              bias=m.b0col[:, c:c + 1])
                else:
                    last = act.activation(to3, ps3, ACT.Copy)
                last.then_inc(tout, 1)

            def body(i, whole):
                for q in range(NQI):
                    if whole or q + 2 < NQI:
                        normal(i, q + 2)
                    if whole or q + 1 < NQI:
                        turned_out(i, q + 1)

            normal(0, 0)
            normal(0, 1)
            turned_out(0, 0)
            run(act, None, 0, body)
            for s in range(STAGES):
                normal(NI, s)
                turned_out(NI, s)

        @block.tensor
        def _(pe):
            def turn_rows(i, q):
                u, Q = q % 2, i * NQI + q
                no = ln_no(i, q) if where(i, q)[1] != 2 else None
                i, s, g, n = where(i, q)
                if s == 2:
                    pe.wait_ge(ys, i * NG + (g + 1))
                else:
                    pe.wait_ge(hs, no + 1)
                at_least(pe, tout, Q - 1)
                turn(pe, m, y[g] if s in (2, 3) else m.h[u], psT[u], n, turned)

            def product(i, q):
                u, Q = q % 2, i * NQI + q
                i, s, g, n = where(i, q)
                pe.wait_ge(tout, Q + 1)
                pe.wait_ge(eaten, Q + 1)
                for t in range(n):
                    for c in range(2):
                        last = pe.matmul(psY[u][:, t * D:(t + 1) * D],
                                         m.hT[u][:, c * 512 + t * P:c * 512 + (t + 1) * P],
                                         wts[s][:, c * D:(c + 1) * D],
                                         start=(c == 0), stop=(c == 1))
                last.then_inc(prods, 1)

            def body(i, whole):
                for q in range(NQI):
                    if whole or q + 1 < NQI:
                        turn_rows(i, q + 1)
                    product(i, q)

            turn_rows(0, 0)
            run(pe, None, 0, body)
            for s in range(STAGES):
                turn_rows(NI, s)
                product(NI, s)


def build(nc, x, src, dst, ea, rel, ew, W0, Wedge, att_src, att_dst, att_edge, bias0, L1w,
          comps, bases, roots, biases, W1, b1, W2, b2, out):
    ctx = ExitStack()
    m = Store()
    (m.x, m.src, m.dst, m.ea, m.rel, m.ew, m.W0, m.Wedge, m.att_src, m.att_dst, m.att_edge,
     m.bias0, m.L1w, m.comps, m.bases, m.roots, m.biases, m.W1, m.b1, m.W2, m.b2, m.out) = (
         x, src, dst, ea, rel, ew, W0, Wedge, att_src, att_dst, att_edge, bias0, L1w, comps,
         bases, roots, biases, W1, b1, W2, b2, out)
    with ctx:
        def sb(name, shape, dt=F32):
            return ctx.enter_context(nc.sbuf_tensor(name, shape, dt))

        def sem(name):
            return ctx.enter_context(nc.semaphore(name))

        def dram(name, shape, dt=F32):
            return nc.dram_tensor(name, shape, dt, kind="Internal").ap()

        m.rec_d = dram("rec_d", [EP, 8], I32)
        m.row_d = dram("row_d", [3, EP + 2])
        m.pos_d = dram("pos_d", [N, 1], I32)
        m.a_d = [dram("a0_d", [EP, AW])] + [dram(f"a{k}_d", [EP, D]) for k in (1, 2)]
        m.rec2_d = dram("rec2_d", [EP, 8], I32)
        m.row2_d = dram("row2_d", [1, EP + 1])
        m.h3_d = dram("h3_d", [N, D])
        m.tab_d = dram("tab_d", [EP, TW])

        m.xs = sb("xs", [P, ET * D])
        m.xh = sb("xh", [P, ET * D])
        m.big = sb("big", [P, 4 * EP + 1])
        m.w0 = sb("w0", [P, 2 * D])
        m.ident = sb("ident", [P, P])
        m.identb = sb("identb", [P, P], BF16)
        m.ones = sb("ones", [P, HI])
        m.onesf = sb("onesf", [P, P])
        m.iota = sb("iota", [P, HI])
        m.part = sb("part", [P, 1])
        m.e127 = sb("e127", [P, 1])
        m.tri = sb("tri", [P, P])
        m.triu = sb("triu", [P, P])
        m.eps = sb("eps", [P, 1])
        m.bias0_b = sb("bias0_b", [P, D])
        m.bias1_b = sb("bias1_b", [P, D])
        m.b12_b = sb("b12_b", [P, D])
        m.b0col = sb("b0col", [P, 2])
        m.srec = sb("srec", [P, ET * 8], I32)
        m.dstc = sb("dstc", [P, ET + 1])
        m.relc = sb("relc", [P, ET])
        m.srec2 = sb("srec2", [P, ET * 8], I32)
        m.srcc = sb("srcc", [P, ET + 1])
        m.to_node = sb("to_node", [P, ET], I32)
        m.poss = sb("poss", [P, ET], I32)
        m.masks = sb("masks", [P, ET])
        m.posn = sb("posn", [P, NT + 1], I32)
        m.maskn = sb("maskn", [P, NT + 1])
        m.co1 = sb("co1", [P, ET * R])
        m.co2 = [sb(f"co2_{l}", [P, ET * NB]) for l in range(2)]
        m.co3 = sb("co3", [P, ET])
        m.ex = sb("ex", [P, ET * H])
        m.exs = sb("exs", [P, ET * H])
        m.h = [sb(f"h{u}", [P, GD]) for u in range(2)]
        m.hT = [sb(f"hT{u}", [P, GD]) for u in range(2)]
        m.st = sb("st", [P, 2 * G * 6])
        m.mv = sb("mv", [P, 2 * G * 2])
        m.ln = sb("ln", [P, 2 * 4 * G])
        m.PS = ctx.enter_context(nc.psum_tensor("PS", [P, 4096], F32))
        m.comps_b = sb("comps_b", [P, 2 * R * NB])
        m.wa = sb("wa", [P, 2 * 3 * H])
        m.we8 = sb("we8", [ED, H])
        m.emean = sb("emean", [ED, 1])
        m.amean = sb("amean", [H, 1])
        m.eaT = sb("eaT", [ED, 512])
        m.idx_s = [sb(f"idx_s{u}", [P, 8 * G], I32) for u in range(2)]
        m.gate_dve, m.gate_pe, m.gate_sp = sem("gate_dve"), sem("gate_pe"), sem("gate_sp")
        m.drow = m.big[:, 0:EP]
        wbig = Carve(m.big[:, EP:])
        m.wb = [wbig(2 * NB * D) for _ in range(2)]
        m.wr = [wbig(2 * D) for _ in range(2)]
        m.w1t, m.w2t = wbig(2 * D), wbig(2 * D)
        m.bd = wbig(2 * R * P)
        m.work = m.big[:, EP + wbig.at:]
        m.eq = [sb(f"eq{u}", [P, P]) for u in range(2)]
        m.carry = [sb(f"carry{u}", [P, P]) for u in range(2)]
        m.alpha = sb("alpha", [P, 2 * G * H])
        m.nmasks = sb("nmasks", [P, ET])
        m.nmaskn = sb("nmaskn", [P, NT + 1])
        m.idx_n = [sb(f"idx_n{g}", [P, G], I32) for g in range(NG)]
        m.idx_t = [sb(f"idx_t{u}", [P, G], I32) for u in range(2)]

        for key, rec_d in ((1, m.rec_d), (0, m.rec2_d)):
            if key == 1:
                with step(nc) as own:
                    constants(nc, own, m)
            with step(nc) as own:
                sort_edges(nc, own, m, key, rec_d)
        for one in (records, records_by_src, small_weights, counts, logits, softmax, weights,
                    edge_layer0):
            with step(nc) as own:
                one(nc, own, m)
        for k in (1, 2, 3):
            with step(nc) as own:
                edge_layer(nc, own, m, k)
        for one in (nodes, sage):
            with step(nc) as own:
                one(nc, own, m)


_INS = ["x", "src", "dst", "edge_attr_64", "edge_type_8", "edge_weight", "L0_gnn_W",
        "L0_gnn_W_edge", "L0_gnn_att_src", "L0_gnn_att_dst", "L0_gnn_att_edge", "L0_gnn_bias",
        "L1_gnn_weight", "L2_gnn_comps", "L2_gnn_bases", "L2_gnn_roots", "L2_gnn_biases",
        "L3_gnn_W1", "L3_gnn_b1", "L3_gnn_W2", "L3_gnn_b2"]


def kernel(**inputs):
    import numpy as _np
    import concourse.bacc as _bacc
    from concourse import mybir as _mybir
    from concourse.bass_utils import run_bass_kernel_spmd as _run

    nc = _bacc.Bacc("TRN2", target_bir_lowering=False, num_devices=1)
    arrays, args = {}, []
    for name in _INS:
        a = _np.ascontiguousarray(inputs[name])
        arrays[f"in_{name}"] = a
        args.append(nc.dram_tensor(f"in_{name}", a.shape, _mybir.dt.from_np(a.dtype),
                                   kind="ExternalInput").ap())
    args.append(nc.dram_tensor("out_0", (N, D), F32, kind="ExternalOutput").ap())
    build(nc, *args)
    r = _run(nc, [arrays], core_ids=[0])
    return r.results[0]["out_0"]
```

```python
from contextlib import ExitStack, contextmanager

import concourse.bass as bass
from concourse import mybir

F32 = mybir.dt.float32
BF16 = mybir.dt.bfloat16
I32 = mybir.dt.int32
ALU = mybir.AluOpType
ACT = mybir.ActivationFunctionType
AX_X = mybir.AxisListType.X
ONE = 1
ds = bass.ds

P = 128
N, D, E = 20000, 256, 5000
H, C = 8, 32
R = 8
NB = 4
ED = 64
ET = -(-E // P)
EP = ET * P
EQ = E // ET
NQ = 125
G = 4
EG = ET // G
NT = N // P
REM = N - NT * P
NG = 4
NI = -(-NT // (G * NG))
HI = 160
PAD_KEY = 156 * 128 + 127
FAR = 1 << 20
EPS = 1e-5
BIG = 1e30
SLOPE = 0.2
GD = G * D
AW = D + H
TW = H + 3 * D
assert EQ * ET == E and EG % 2 == 0 and N % NQ == 0
assert NI * G * NG == NT + G and 0 < REM <= P


class Link:

    def __init__(self, eng, sem):
        self.eng, self.sem, self.base, self.i, self.per, self.c = eng, sem, 0, None, 0, 0

    def enter(self, i, per):
        self.i, self.per, self.c = i, per, 0

    def leave(self, times):
        assert self.c == self.per, ("increments of the loop's body", self.c, self.per)
        self.base, self.i, self.c = self.base + times * self.per, None, 0

    def mark(self, ins):
        ins.then_inc(self.sem, 1)
        if self.i is None:
            self.base += 1
            return self.base
        self.c += 1
        return self.i * self.per + (self.base + self.c)

    def until(self, value):
        self.eng.wait_ge(self.sem, value + ONE)

    def __call__(self, ins):
        self.until(self.mark(ins))


class Carve:

    def __init__(self, buf):
        self.buf, self.at = buf, 0

    def __call__(self, n):
        self.at += n
        return self.buf[:, self.at - n:self.at]


@contextmanager
def step(nc):
    mine = []

    def sem(name, start=ONE):
        mine.append(nc.alloc_semaphore(name=name))
        if start:
            nc.scalar.sem_inc(mine[-1], start)
        return mine[-1]

    yield sem
    nc.clear_and_free_semaphores(mine)
    nc.all_engine_barrier()


class Store:
    pass


def bc(ap, n):
    return ap.unsqueeze(2).to_broadcast([ap.shape[0], ap.shape[1], n])


def at_least(eng, sem, value):
    if not (isinstance(value, int) and value <= 0):
        eng.wait_ge(sem, value + ONE)


def each_group(eng, link, per, body):
    body(0, 0, 0, True, False)
    with eng.Fori(0, EG // 2 - 1) as i:
        if link is not None:
            link.enter(i, per)
        body(i * 2 + 1, 1, i, False, False)
        body(i * 2 + 2, 0, i + 1, False, False)
        if link is not None:
            link.leave(EG // 2 - 1)
    body(EG - 1, 1, EG // 2 - 1, False, True)


def constants(nc, sem, m):
    done = sem("const_done")
    nc.all_engine_barrier()
    with nc.Block() as block:
        @block.gpsimd
        def _(pool):
            link = Link(pool, done)
            pool.memset(m.ident[:, :], 0.0).then_inc(done, 1)
            pool.memset(m.ones[:, :], 1.0).then_inc(done, 1)
            pool.memset(m.onesf[:, :], 1.0).then_inc(done, 1)
            pool.memset(m.eps[:, :], EPS).then_inc(done, 1)
            pool.memset(m.e127[:, :], 0.0).then_inc(done, 1)
            pool.iota(m.iota[:, :], pattern=[[1, HI]], base=0, channel_multiplier=0,
                      allow_small_or_imprecise_dtypes=True).then_inc(done, 1)
            pool.iota(m.part[:, :], pattern=[[0, 1]], base=0, channel_multiplier=1,
                      allow_small_or_imprecise_dtypes=True).then_inc(done, 1)
            pool.wait_ge(done, 7 + ONE)
            link.base = 7
            link(pool.affine_select(out=m.ident[:, :], in_=m.ident[:, :], compare_op=ALU.not_equal,
                                    fill=1.0, base=0, pattern=[[-1, P]], channel_multiplier=1))
            link(pool.affine_select(out=m.tri[:, :], in_=m.onesf[:, :], compare_op=ALU.is_gt,
                                    fill=0.0, base=0, pattern=[[-1, P]], channel_multiplier=1))
            link(pool.affine_select(out=m.triu[:, :], in_=m.onesf[:, :], compare_op=ALU.is_gt,
                                    fill=0.0, base=0, pattern=[[1, P]], channel_multiplier=-1))
            link(pool.affine_select(out=m.e127[:, :], in_=m.e127[:, :], compare_op=ALU.not_equal,
                                    fill=1.0, base=1 - P, pattern=[[0, 1]], channel_multiplier=1))
            link(pool.tensor_copy(m.identb[:, :], m.ident[:, :]))


KEYS = (1, 0)


def drain(sp, landed, drained):
    with sp.Fori(0, EG // 2) as i:
        for u in range(2):
            sp.wait_ge(landed[u], i * (16 * G) + 16 * G)
            sp.sem_inc(drained[u], 1)


def scatter_records(pool, m, j, sent, drained, staged, gate, rec_d):
    ranks, recs = m.ranks[j], m.recs[j]
    cut = Carve(m.hT[j])
    rank_s = [cut(G).bitcast(I32) for _ in range(2)]
    rec_s = [cut(8 * G).bitcast(I32) for _ in range(2)]
    with pool.Fori(0, EG // 2) as i:
        for u in range(2):
            pool.wait_ge(drained[u], i + ONE)
            pool.tensor_copy(rank_s[u], ranks[:, ds((i * 2 + u) * G, G)]).then_inc(staged, 1)
            pool.tensor_copy(rec_s[u], recs[:, ds((i * 2 + u) * (8 * G), 8 * G)])\
                .then_inc(staged, 1)
            pool.wait_ge(staged, i * 4 + (2 * u + 2) + ONE)
            pool.sem_inc(gate, 1)
            for t in range(G):
                pool.indirect_dma_start(
                    rec_d[:, :], bass.IndirectOffsetOnAxis(ap=rank_s[u][:, t:t + 1], axis=0),
                    rec_s[u][:, 8 * t:8 * t + 8], None).then_inc(sent[u], 16)
    for u in range(2):
        pool.wait_ge(sent[u], EG // 2 * 16 * G)


def sort_edges(nc, sem, m):
    cut = Carve(m.xs)
    lin = cut(7 * ET).bitcast(I32)
    hilo_i = cut(4 * ET).bitcast(I32)
    keyf, hif, lof, before, inside, rank = ([cut(ET) for _ in range(2)] for _ in range(6))
    oh_loT = [cut(2 * P) for _ in range(2)]
    junk1, junk2 = [cut(P) for _ in range(2)], [cut(HI) for _ in range(2)]
    count, total, upto, table = cut(2 * HI), cut(2 * HI), cut(2 * HI), cut(2 * HI)
    zero = cut(HI // 2).bitcast(BF16)
    wide = Carve(m.big)
    keyrow = [wide(EP).bitcast(I32) for _ in range(2)]
    oh_hi = [wide(ET * HI // 2).bitcast(BF16) for _ in range(2)]
    widest = Carve(m.xh)
    oh_lo = [widest(ET * P // 2).bitcast(BF16) for _ in range(2)]
    psC = [m.PS[:, 0:HI], m.PS[:, 512:512 + HI]]
    psW, psX = m.PS[:, 1024:1024 + 2 * HI], m.PS[:, 1536:1536 + 2 * HI]
    psG = [m.PS[:, 512 * b:512 * b + 2 * HI] for b in (0, 1)]
    psN = [m.PS[:, 512 * b:512 * b + 2 * HI] for b in (4, 5)]
    psLT = [m.PS[:, b:b + P].bitcast(BF16) for b in (3072, 3584)]
    U = 8

    def of(buf, j):
        return buf[:, j * HI:(j + 1) * HI]

    def lo(t, j):
        return oh_lo[j][:, ds(t * P, P)]

    def hi(t, j):
        return oh_hi[j][:, ds(t * HI, HI)]

    cleared, loaded, numbered, keys_in = (sem("so_cleared"), sem("so_loaded"),
                                          sem("so_numbered"), sem("so_keys"))
    hot, counted, summed, split = sem("so_hot"), sem("so_counted"), sem("so_summed"), sem("so_split")
    turned, turned_out, next_in, looked = (sem("so_turned"), sem("so_turned_out"),
                                           sem("so_next"), sem("so_looked"))
    added, used, dve_own = sem("so_added"), sem("so_used"), sem("so_dve")
    nc.all_engine_barrier()
    with nc.Block() as block:
        @block.sync
        def _(sp):
            sp.wait_ge(cleared, 9 + ONE)
            for k, a in ((5, m.dst), (6, m.src), (0, m.src), (1, m.dst), (2, m.rel), (3, m.ew)):
                sp.dma_start(lin[0:EQ, k * ET:(k + 1) * ET],
                             a.rearrange("(p t) -> p t", t=ET).bitcast(I32)).then_inc(loaded, 16)
            for j, a in enumerate((m.dst, m.src)):
                sp.dma_start(keyrow[j][:, 0:E], a.partition_broadcast(P)).then_inc(keys_in, 16)
            sp.wait_ge(loaded, 96 + ONE)
            sp.wait_ge(keys_in, 32 + ONE)

        @block.gpsimd
        def _(pool):
            for k, v in ((5, PAD_KEY), (6, PAD_KEY), (0, 0), (1, 0), (2, 0), (3, 0)):
                pool.memset(lin[:, k * ET:(k + 1) * ET], v).then_inc(cleared, 1)
            pool.memset(zero, 0.0).then_inc(cleared, 1)
            for j in range(2):
                pool.memset(keyrow[j][:, E:EP], PAD_KEY).then_inc(cleared, 1)
            pool.iota(lin[:, 4 * ET:5 * ET], pattern=[[1, ET]], base=0,
                      channel_multiplier=ET).then_inc(numbered, 1)

        @block.vector
        def _(dve):
            link = Link(dve, dve_own)
            dve.wait_ge(loaded, 96 + ONE)
            dve.wait_ge(numbered, 1 + ONE)
            keys = lin[:, 5 * ET:7 * ET]
            dve.tensor_scalar(hilo_i[:, 0:2 * ET], keys, 7, None, ALU.arith_shift_right)
            link(dve.tensor_scalar(hilo_i[:, 2 * ET:], keys, P - 1, None, ALU.bitwise_and))
            for j in range(2):
                dve.tensor_copy(keyf[j], keys[:, j * ET:(j + 1) * ET])
                dve.tensor_copy(hif[j], hilo_i[:, j * ET:(j + 1) * ET])
                last = dve.tensor_copy(lof[j], hilo_i[:, (2 + j) * ET:(3 + j) * ET])
            link(last)
            with dve.Fori(0, ET // U) as i:
                for t in (i * U + v for v in range(U)):
                    for j in range(2):
                        dve.tensor_scalar(lo(t, j), m.iota[:, 0:P], lof[j][:, ds(t, 1)], None,
                                          ALU.is_equal)
                        last = dve.tensor_scalar(hi(t, j), m.iota[:, :], hif[j][:, ds(t, 1)], None,
                                                 ALU.is_equal)
                    last.then_inc(hot, 1)
            dve.wait_ge(counted, 1 + ONE)
            dve.tensor_copy(of(count, 0), psC[0])
            dve.tensor_copy(of(count, 1), psC[1]).then_inc(split, 1)
            dve.wait_ge(summed, 1 + ONE)
            link(dve.tensor_copy(total, psX))
            for j in range(2):
                last = dve.tensor_tensor_scan(of(upto, j), m.ones[:, 0:HI], of(total, j), 0.0,
                                              ALU.mult, ALU.add)
            link(last)
            link(dve.tensor_tensor(upto, upto, total, ALU.subtract))
            dve.tensor_tensor(table, upto, psW, ALU.add).then_inc(added, 1)
            dve.wait_ge(keys_in, 32 + ONE)
            with dve.Fori(0, ET // U) as i:
                for v in range(U):
                    t, u = i * U + v, v % 2
                    dve.wait_ge(looked, t + 1 + ONE)
                    dve.wait_ge(next_in, t + 1 + ONE)
                    dve.wait_ge(used, t + ONE)
                    dve.tensor_tensor(table, table, psN[u], ALU.add).then_inc(added, 1)
                    for j in range(2):
                        dve.scalar_tensor_tensor(
                            junk1[j], keyrow[j].rearrange("p (q t) -> p q t", t=ET)[:, :, ds(t, 1)]
                            .squeeze(2), keyf[j][:, ds(t, 1)], m.tri[:, :],
                            ALU.is_equal, ALU.mult, accum_out=inside[j][:, ds(t, 1)])
                    for j in range(2):
                        last = dve.scalar_tensor_tensor(
                            junk2[j], m.iota[:, :], hif[j][:, ds(t, 1)], of(psG[u], j),
                            ALU.is_equal, ALU.mult, accum_out=before[j][:, ds(t, 1)])
                    last.then_inc(used, 1)
            dve.wait_ge(used, ET + ONE)
            for j in range(2):
                link(dve.tensor_tensor(rank[j], before[j], inside[j], ALU.add))
                dve.tensor_copy(m.ranks[j], rank[j])
                rec3 = m.recs[j].rearrange("p (t c) -> p t c", c=8)
                for k in range(8):
                    c = 5 + j if k == KEYS[j] else k if k < 5 else 0
                    dve.tensor_copy(rec3[:, :, k], lin[:, c * ET:(c + 1) * ET])

        @block.scalar
        def _(act):
            with act.Fori(0, ET // U) as i:
                for v in range(U):
                    act.wait_ge(turned, i * U + (v + 1) + ONE)
                    if v > 1:
                        act.wait_ge(looked, i * U + (v - 1) + ONE)
                    act.activation(oh_loT[v % 2], psLT[v % 2], ACT.Copy).then_inc(turned_out, 1)
                act.wait_ge(looked, i * U + U + ONE)

        @block.tensor
        def _(pe):
            pe.wait_ge(cleared, 9 + ONE)
            pe.matmul(psC[0], zero[:, 0:P], zero, start=True, stop=False)
            pe.matmul(psC[1], zero[:, 0:P], zero, start=True, stop=False)
            with pe.Fori(0, ET // U) as i:
                for v in range(U):
                    t = i * U + v
                    pe.wait_ge(hot, t + 1 + ONE)
                    for j in range(2):
                        pe.matmul(psC[j], lo(t, j), hi(t, j), start=False, stop=False)
            pe.matmul(psC[0], zero[:, 0:P], zero, start=False, stop=True)
            pe.matmul(psC[1], zero[:, 0:P], zero, start=False, stop=True).then_inc(counted, 1)
            pe.wait_ge(split, 1 + ONE)
            pe.matmul(psW, m.triu[:, :], count, start=True, stop=True)
            pe.matmul(psX, m.onesf[:, :], count, start=True, stop=True).then_inc(summed, 1)
            with pe.Fori(0, ET // U) as i:
                for v in range(U):
                    t, u = i * U + v, v % 2
                    for j in range(2):
                        last = pe.transpose(psLT[u][:, j * P:(j + 1) * P], lo(t, j),
                                            m.identb[:, :])
                    last.then_inc(turned, 1)
                    for j in range(2):
                        last = pe.matmul(of(psN[u], j), lo(t, j), hi(t, j), start=True, stop=True)
                    last.then_inc(next_in, 1)
                    pe.wait_ge(turned_out, t + 1 + ONE)
                    pe.wait_ge(added, t + 1 + ONE)
                    for j in range(2):
                        last = pe.matmul(of(psG[u], j), oh_loT[u][:, j * P:(j + 1) * P],
                                         of(table, j), start=True, stop=True)
                    last.then_inc(looked, 1)


def records(nc, sem, m):
    cut = Carve(m.xs)
    lastc, far = cut(ET), cut(ET)
    clear = cut(N // NQ).bitcast(I32)
    row, prev, nxt = cut(2 * P), cut(P), cut(P)
    keep, last = cut(P), cut(P)
    ends = cut(4)
    psA, psL = m.PS[0:ET, 0:2 * P], m.PS[:, 512:512 + ET]
    srec3 = m.srec[:, :].rearrange("p (t c) -> p t c", c=8)
    loaded, filled, cleared, turned, rowed = (sem("re_loaded"), sem("re_filled"), sem("re_cleared"),
                                              sem("re_turned"), sem("re_rowed"))
    cols, wrote, back, flags, flipped = (sem("re_cols"), sem("re_wrote"), sem("re_back"),
                                         sem("re_flags"), sem("re_flipped"))
    kept, dve_own = sem("re_kept"), sem("re_dve")
    nc.all_engine_barrier()
    with nc.Block() as block:
        @block.sync
        def _(sp):
            sp.dma_start(srec3, m.rec_d.rearrange("(t q) c -> q t c", q=P)).then_inc(loaded, 16)
            sp.wait_ge(filled, 4 + ONE)
            sp.dma_start(m.pos_d.rearrange("(p t) c -> p (t c)", p=NQ), clear[0:NQ, :])\
                .then_inc(cleared, 16)
            sp.dma_start(m.row_d[0:1, 0:1], ends[0:1, 0:1]).then_inc(wrote, 16)
            sp.dma_start(m.row_d[0:1, EP + 1:EP + 2], ends[0:1, 1:2]).then_inc(wrote, 16)
            sp.dma_start(m.row_d[2:3, EP:EP + 1], ends[0:1, 2:3]).then_inc(wrote, 16)
            sp.wait_ge(rowed, 1 + ONE)
            sp.dma_start(m.row_d[0, 1:EP + 1].rearrange("(t q) -> t q", q=P), row[0:ET, 0:P])\
                .then_inc(wrote, 16)
            sp.dma_start(m.row_d[1, 0:EP].rearrange("(t q) -> t q", q=P), row[0:ET, P:2 * P])\
                .then_inc(wrote, 16)
            sp.wait_ge(wrote, 80 + ONE)
            sp.dma_start(prev[0:ET, :], m.row_d[0, 0:EP].rearrange("(t q) -> t q", q=P))\
                .then_inc(back, 16)
            sp.dma_start(nxt[0:ET, :], m.row_d[0, 2:EP + 2].rearrange("(t q) -> t q", q=P))\
                .then_inc(back, 16)
            sp.wait_ge(flags, 1 + ONE)
            sp.dma_start(m.row_d[2, 0:EP].rearrange("(t q) -> t q", q=P), keep[0:ET, :])\
                .then_inc(kept, 16)
            sp.wait_ge(kept, 16 + ONE)
            sp.wait_ge(cleared, 16 + ONE)

        @block.gpsimd
        def _(pool):
            pool.memset(clear, FAR).then_inc(filled, 1)
            pool.memset(m.posn[:, :], FAR).then_inc(filled, 1)
            pool.memset(ends[:, 0:2], -5.0).then_inc(filled, 1)
            pool.memset(ends[:, 2:4], 0.0).then_inc(filled, 1)
            pool.iota(m.place[:, :], pattern=[[P, ET]], base=0, channel_multiplier=1).then_inc(filled, 1)

        @block.vector
        def _(dve):
            link = Link(dve, dve_own)
            dve.wait_ge(loaded, 16 + ONE)
            dve.memset(m.dstc[:, 0:1], -5.0)
            dve.tensor_copy(m.dstc[:, 1:ET + 1], srec3[:, :, 1])
            dve.tensor_copy(m.relc[:, :], srec3[:, :, 2]).then_inc(cols, 1)
            dve.wait_ge(back, 32 + ONE)
            dve.tensor_tensor(keep[0:ET, :], row[0:ET, 0:P], prev[0:ET, :], ALU.is_equal)
            dve.tensor_tensor(last[0:ET, :], row[0:ET, 0:P], nxt[0:ET, :], ALU.not_equal)\
                .then_inc(flags, 1)
            dve.wait_ge(flipped, 1 + ONE)
            link(dve.tensor_copy(lastc, psL))
            link(dve.tensor_scalar(far, lastc, -float(FAR), float(FAR), ALU.mult, ALU.add))
            link(dve.tensor_tensor(lastc, lastc, m.dstc[:, 1:ET + 1], ALU.mult))
            link(dve.tensor_tensor(lastc, lastc, far, ALU.add))
            dve.tensor_copy(m.posidx[:, :], lastc)

        @block.scalar
        def _(act):
            act.wait_ge(turned, 1 + ONE)
            act.activation(row[0:ET, :], psA, ACT.Copy).then_inc(rowed, 1)

        @block.tensor
        def _(pe):
            pe.wait_ge(cols, 1 + ONE)
            pe.transpose(psA[:, 0:P], m.dstc[:, 1:ET + 1], m.ident[:, :])
            pe.transpose(psA[:, P:2 * P], m.relc[:, :], m.ident[:, :]).then_inc(turned, 1)
            pe.wait_ge(flags, 1 + ONE)
            pe.transpose(psL, last[0:ET, :], m.ident[0:ET, 0:ET]).then_inc(flipped, 1)


def records_by_src(nc, sem, m):
    cut = Carve(m.xs)
    lastc, far = cut(ET), cut(ET)
    row, nxt, last, ends = cut(P), cut(P), cut(P), cut(4)
    psA, psL = m.PS[0:ET, 0:P], m.PS[:, 512:512 + ET]
    loaded, cleared, cols, turned, rowed = (sem("rs_loaded"), sem("rs_cleared"), sem("rs_cols"),
                                            sem("rs_turned"), sem("rs_rowed"))
    wrote, back, flags, flipped, dve_own = (sem("rs_wrote"), sem("rs_back"), sem("rs_flags"),
                                            sem("rs_flipped"), sem("rs_dve"))
    srec3 = m.srec2[:, :].rearrange("p (t c) -> p t c", c=8)
    nc.all_engine_barrier()
    with nc.Block() as block:
        @block.gpsimd
        def _(pool):
            pool.memset(ends, -5.0).then_inc(cleared, 1)

        @block.sync
        def _(sp):
            sp.dma_start(srec3, m.rec2_d.rearrange("(t q) c -> q t c", q=P)).then_inc(loaded, 16)
            sp.wait_ge(cleared, 1 + ONE)
            sp.dma_start(m.row2_d[0:1, EP:EP + 1], ends[0:1, 0:1]).then_inc(wrote, 16)
            sp.wait_ge(rowed, 1 + ONE)
            sp.dma_start(m.row2_d[0, 0:EP].rearrange("(t q) -> t q", q=P), row[0:ET, :])\
                .then_inc(wrote, 16)
            sp.wait_ge(wrote, 32 + ONE)
            sp.dma_start(nxt[0:ET, :], m.row2_d[0, 1:EP + 1].rearrange("(t q) -> t q", q=P))\
                .then_inc(back, 16)
            sp.wait_ge(back, 16 + ONE)

        @block.vector
        def _(dve):
            link = Link(dve, dve_own)
            dve.wait_ge(loaded, 16 + ONE)
            dve.memset(m.srcc[:, 0:1], -5.0)
            dve.tensor_copy(m.srcc[:, 1:ET + 1], srec3[:, :, 0]).then_inc(cols, 1)
            dve.wait_ge(back, 16 + ONE)
            dve.tensor_tensor(last[0:ET, :], row[0:ET, :], nxt[0:ET, :], ALU.not_equal)\
                .then_inc(flags, 1)
            dve.wait_ge(flipped, 1 + ONE)
            link(dve.tensor_copy(lastc, psL))
            link(dve.tensor_scalar(far, lastc, -float(FAR), float(FAR), ALU.mult, ALU.add))
            link(dve.tensor_tensor(lastc, lastc, m.srcc[:, 1:ET + 1], ALU.mult))
            link(dve.tensor_tensor(lastc, lastc, far, ALU.add))
            dve.tensor_copy(m.to_node[:, :], lastc)

        @block.scalar
        def _(act):
            act.wait_ge(turned, 1 + ONE)
            act.activation(row[0:ET, :], psA, ACT.Copy).then_inc(rowed, 1)

        @block.tensor
        def _(pe):
            pe.wait_ge(cols, 1 + ONE)
            pe.transpose(psA, m.srcc[:, 1:ET + 1], m.ident[:, :]).then_inc(turned, 1)
            pe.wait_ge(flags, 1 + ONE)
            pe.transpose(psL, last[0:ET, :], m.ident[0:ET, 0:ET]).then_inc(flipped, 1)


def small_weights(nc, sem, m):
    cut = Carve(m.xs)
    att = [cut(D) for _ in range(3)]
    we, tmp, eas, b2_b = cut(D), cut(2 * D), cut(ED), cut(D)
    ea_all = m.xh[0:EQ, 0:ET * ED]
    meane = m.PS[0:ED, 0:1]
    loaded, eas_in, rowsum, summed, mean, drawn, dve_own = (
        sem("sw_loaded"), sem("sw_eas_in"), sem("sw_rowsum"), sem("sw_summed"), sem("sw_mean"),
        sem("sw_drawn"), sem("sw_dve"))
    staged, gate, sent = sem("sw_staged"), sem("sw_gate"), [sem(f"sw_sent{u}", 0) for u in range(2)]
    drained = [sem(f"sw_drained{u}") for u in range(2)]
    nc.all_engine_barrier()
    with nc.Block() as block:
        @block.gpsimd
        def _(pool):
            scatter_records(pool, m, 0, sent, drained, staged, gate, m.rec_d)

        @block.sync
        def _(sp):
            sp.dma_start(ea_all, m.ea.rearrange("(p t) c -> p (t c)", t=ET)).then_inc(eas_in, 16)
            sp.dma_start(m.w0[:, :].rearrange("p (k n) -> p k n", k=2),
                         m.W0.rearrange("(k p) n -> p k n", p=P)).then_inc(loaded, 16)
            sp.dma_start(we[0:ED, :], m.Wedge).then_inc(loaded, 16)
            for a, dest in ((m.att_src, att[0]), (m.att_dst, att[1]), (m.att_edge, att[2])):
                sp.dma_start(dest, a.rearrange("h c -> (h c)").partition_broadcast(P))\
                    .then_inc(loaded, 16)
            sp.dma_start(m.bias0_b, m.bias0.partition_broadcast(P)).then_inc(loaded, 16)
            sp.dma_start(m.bias1_b, m.biases[1, :].partition_broadcast(P)).then_inc(loaded, 16)
            sp.dma_start(m.b12_b[:, :], m.b1.partition_broadcast(P)).then_inc(loaded, 16)
            sp.dma_start(b2_b, m.b2.partition_broadcast(P)).then_inc(loaded, 16)
            sp.dma_start(m.comps_b[:, :],
                         m.comps[0:2].rearrange("l r b -> (l r b)").partition_broadcast(P))\
                .then_inc(loaded, 16)
            for k in range(2):
                sp.dma_start(m.b0col[:, k:k + 1], m.biases[0, k * P:(k + 1) * P].unsqueeze(1))\
                    .then_inc(loaded, 16)
            drain(sp, sent, drained)
            sp.wait_ge(loaded, 192 + ONE)
            sp.wait_ge(eas_in, 16 + ONE)

        @block.vector
        def _(dve):
            link = Link(dve, dve_own)
            dve.wait_ge(eas_in, 16 + ONE)
            dve.tensor_reduce(eas[0:EQ, :], ea_all.rearrange("p (t c) -> p c t", c=ED), AX_X,
                              ALU.add).then_inc(rowsum, 1)
            dve.wait_ge(loaded, 192 + ONE)
            for j in range(2):
                for k in range(2):
                    link(dve.tensor_tensor(tmp[:, k * D:(k + 1) * D], m.w0[:, k * D:(k + 1) * D],
                                           att[j], ALU.mult))
                for k in range(2):
                    link(dve.tensor_reduce(m.wa[:, k * 3 * H + j * H:k * 3 * H + (j + 1) * H],
                                           tmp[:, k * D:(k + 1) * D].rearrange(
                                               "p (h c) -> p h c", c=C), AX_X, ALU.add))
            for k in range(2):
                o = k * 3 * H
                dve.tensor_tensor(m.wa[:, o + 2 * H:o + 3 * H], m.wa[:, o:o + H],
                                  m.wa[:, o + H:o + 2 * H], ALU.add)
            dve.tensor_tensor(m.b12_b[:, :], m.b12_b[:, :], b2_b, ALU.add)
            dve.memset(m.pre[:, 0:H], 1.0)
            dve.memset(m.pre[:, H + D:H + 2 * D], 0.0)
            link(dve.tensor_tensor(tmp[0:ED, 0:D], we[0:ED, :], att[2][0:ED, :], ALU.mult))
            link(dve.tensor_reduce(m.we8[:, :], tmp[0:ED, 0:D].rearrange("p (h c) -> p h c", c=C),
                                   AX_X, ALU.add))
            dve.wait_ge(summed, 1 + ONE)
            dve.tensor_scalar(m.emean[:, :], meane, 1.0 / E, None, ALU.mult).then_inc(mean, 1)
            dve.wait_ge(drawn, 1 + ONE)
            dve.tensor_copy(m.amean[:, :], m.PS[0:H, 512:513])

        @block.tensor
        def _(pe):
            pe.wait_ge(rowsum, 1 + ONE)
            pe.matmul(meane, eas[0:EQ, :], m.onesf[0:EQ, 0:1], start=True, stop=True)\
                .then_inc(summed, 1)
            pe.wait_ge(mean, 1 + ONE)
            pe.matmul(m.PS[0:H, 512:513], m.we8[:, :], m.emean[:, :], start=True, stop=True)\
                .then_inc(drawn, 1)


def to_edge_major(dve, link, heads, scratch, out):
    link(dve.transpose(scratch[0:32, :], heads[0:32, :]))
    blocks = scratch[0:32, :].rearrange("p (t j c) -> p t j c", j=4, c=32)
    for j in range(4):
        last = dve.tensor_copy(out[32 * j:32 * j + 32, :].rearrange("p (t c) -> p t c", c=8),
                               blocks[:, :, j, 0:8])
    link(last)


def counts(nc, sem, m):
    sA, sL, sF, sK = (m.big[:, k * EP:(k + 1) * EP] for k in range(4))
    keep_next = m.big[0:R, 3 * EP + 1:4 * EP + 1]
    cut = Carve(m.xs)
    cnt, oh, tmp, sel, w = cut(ET * R), cut(ET * R), cut(ET * R), cut(ET), cut(ET)
    cleared, keeps, rels, dve_own = sem("co_cleared"), sem("co_keeps"), sem("co_rels"), sem("co_dve")
    staged, gate, sent = sem("co_staged"), sem("co_gate"), [sem(f"co_sent{u}", 0) for u in range(2)]
    drained = [sem(f"co_drained{u}") for u in range(2)]

    def by8(ap):
        return ap.rearrange("p (t r) -> p t r", r=R)

    nc.all_engine_barrier()
    with nc.Block() as block:
        @block.gpsimd
        def _(pool):
            pool.memset(sA[0:32, :], 0.0).then_inc(cleared, 1)
            pool.memset(sL[0:32, :], 0.0).then_inc(cleared, 1)
            scatter_records(pool, m, 1, sent, drained, staged, gate, m.rec2_d)

        @block.sync
        def _(sp):
            sp.dma_start(m.big[0:R, 3 * EP:4 * EP + 1],
                         m.row_d[2, 0:EP + 1].partition_broadcast(R)).then_inc(keeps, 16)
            sp.wait_ge(cleared, 2 + ONE)
            sp.dma_start(sL[0:R, :], m.row_d[1, 0:EP].partition_broadcast(R)).then_inc(rels, 16)
            drain(sp, sent, drained)
            sp.wait_ge(rels, 16 + ONE)
            sp.wait_ge(keeps, 16 + ONE)

        @block.vector
        def _(dve):
            link = Link(dve, dve_own)
            dve.wait_ge(rels, 16 + ONE)
            dve.wait_ge(cleared, 2 + ONE)
            link(dve.tensor_scalar(sA[0:R, :], sL[0:R, :], m.part[0:R, :], None, ALU.is_equal))
            dve.wait_ge(keeps, 16 + ONE)
            link(dve.tensor_tensor_scan(sF[0:R, :], sK[0:R, :], sA[0:R, :], 0.0, ALU.mult, ALU.add))
            link(dve.tensor_tensor_scan(sA[0:R, ::-1], keep_next[:, ::-1], sF[0:R, ::-1], 0.0,
                                        ALU.mult, ALU.max))
            to_edge_major(dve, link, sA, sF, cnt)
            dve.tensor_scalar(m.big[0:R, 3 * EP:4 * EP + 1], m.big[0:R, 3 * EP:4 * EP + 1], -1.0,
                              BIG, ALU.add, ALU.mult)
            dve.tensor_copy(w, m.srec[:, :].bitcast(F32).rearrange("p (t c) -> p t c", c=8)[:, :, 3])
            link(dve.tensor_tensor(by8(oh), m.iota[:, 0:R].unsqueeze(1).to_broadcast([P, ET, R]),
                                   bc(m.relc[:, :], R), ALU.is_equal))
            dve.tensor_tensor(by8(m.co1[:, :]), by8(oh), bc(w, R), ALU.mult)
            link(dve.tensor_tensor(tmp, oh, cnt, ALU.mult))
            link(dve.tensor_reduce(sel, by8(tmp), AX_X, ALU.add))
            link(dve.tensor_scalar(sel, sel, 1.0, None, ALU.max))
            link(dve.reciprocal(sel, sel))
            for l in range(2):
                for b in range(NB):
                    comp = m.comps_b[:, l * R * NB:(l + 1) * R * NB].rearrange(
                        "p (r b) -> p b r", b=NB)[:, b:b + 1, :].to_broadcast([P, ET, R])
                    link(dve.tensor_tensor(by8(tmp), by8(oh), comp, ALU.mult))
                    col = m.co2[l][:, :].rearrange("p (t b) -> p t b", b=NB)[:, :, b:b + 1]
                    link(dve.tensor_reduce(col, by8(tmp), AX_X, ALU.add))
                    link(dve.tensor_tensor(col, col, sel.unsqueeze(2), ALU.mult))


def ln_stats(dve, link, m, rows, u, done):
    n = len(rows)
    for t, r in enumerate(rows):
        last = dve.bn_stats(m.st[:, (u * G + t) * 6:(u * G + t + 1) * 6], r)
    link(last)
    dve.sem_inc(m.gate_dve, 1)
    for t in range(n):
        last = dve.bn_aggr(m.mv[:, (u * G + t) * 2:(u * G + t + 1) * 2],
                           m.st[:, (u * G + t) * 6:(u * G + t + 1) * 6])
    last.then_inc(done, 1)


def ln_parts(m, u, n):
    mv = m.mv[:, u * G * 2:(u * G + n) * 2].rearrange("p (t c) -> p t c", c=2)
    s = [m.ln[:, (u * 4 + k) * G:(u * 4 + k) * G + n] for k in range(4)]
    return mv[:, :, 0], mv[:, :, 1], s


def ln_scales(dve, link, m, u, n, done):
    mean, var, (std, nmr, a, r) = ln_parts(m, u, n)
    link(dve.reciprocal(r, std))
    link(dve.scalar_tensor_tensor(a, var, EPS, r, ALU.add, ALU.mult))
    link(dve.scalar_tensor_tensor(a, a, -0.5, r, ALU.mult, ALU.mult))
    link(dve.scalar_tensor_tensor(std, a, 1.5, r, ALU.add, ALU.mult))
    dve.scalar_tensor_tensor(nmr, mean, -1.0, std, ALU.mult, ALU.mult).then_inc(done, 1)


def ln_apply(act, m, rows, u, h, done):
    _, _, (rstd, nmr, _, _) = ln_parts(m, u, len(rows))
    for t, r in enumerate(rows):
        last = act.activation(h[:, t * D:(t + 1) * D], r, ACT.Relu, scale=rstd[:, t:t + 1],
                              bias=nmr[:, t:t + 1])
    last.then_inc(done, 1)


def turn(pe, m, h, ps, n, done):
    for k in range(2):
        for t in range(n):
            last = pe.transpose(ps[:, k * 512 + t * P:k * 512 + (t + 1) * P],
                                h[:, t * D + k * P:t * D + (k + 1) * P], m.ident[:, :])
    last.then_inc(done, 1)


def logits(nc, sem, m):
    sA, sL, sF, _ = (m.big[:, k * EP:(k + 1) * EP] for k in range(4))
    cut = Carve(sF)
    gs, gd, ge = ([cut(GD) for _ in range(2)], [cut(GD) for _ in range(2)],
                  [cut(G * ED) for _ in range(2)])
    psE, psA, psZ = m.PS[0:ED, 1024:1536], m.PS[0:H, 1536:2048], m.PS[0:H, 2048:2560]
    psY = [m.PS[:, 3072:3584], m.PS[:, 3584:4096]]
    blank, staged, gate = sem("lo_blank"), sem("lo_staged"), sem("lo_gate")
    src_in, dst_in, ea_in = ([sem(f"lo_{k}_in{u}", 0) for u in range(2)] for k in ("src", "dst", "ea"))
    stats, std, scales, hs = (sem("lo_stats"), sem("lo_std"), sem("lo_scales"), sem("lo_h"))
    kept, eturn = ([sem(f"lo_{k}{u}") for u in range(2)] for k in ("kept", "eturn"))
    turned, tout, eout = sem("lo_turned"), sem("lo_tout"), sem("lo_eout")
    prods, pout, logit, lout, dve_own = (sem("lo_prods"), sem("lo_pout"), sem("lo_logit"),
                                         sem("lo_lout"), sem("lo_dve"))

    def tiles(buf):
        return [buf[:, t * D:(t + 1) * D] for t in range(G)]

    nc.all_engine_barrier()
    with nc.Block() as block:
        @block.gpsimd
        def _(pool):
            for b in (*gs, *gd, *ge):
                pool.memset(b, 0.0).then_inc(blank, 1)
            pool.wait_ge(blank, 6 + ONE)
            bx, be = pool.to_reg(N - 1), pool.to_reg(E - 1)
            with pool.Fori(0, EG // 2) as i:
                for u in range(2):
                    g = i * 2 + u
                    pool.wait_ge(kept[u], i + ONE)
                    pool.wait_ge(eturn[u], i + ONE)
                    pool.sem_inc(gate, 1)
                    pool.tensor_copy(m.idx_s[u][:, :], m.srec[:, ds(g * (8 * G), 8 * G)])\
                        .then_inc(staged, 1)
                    pool.wait_ge(staged, g + 1 + ONE)
                    pool.sem_inc(gate, 1)
                    for buf, table, c, bound, came in (
                            (gs, m.x, 0, bx, src_in), (gd, m.x, 1, bx, dst_in),
                            (ge, m.ea, 4, be, ea_in)):
                        w = ED if buf is ge else D
                        for t in range(G):
                            row = bass.IndirectOffsetOnAxis(
                                ap=m.idx_s[u][:, 8 * t + c:8 * t + c + 1], axis=0)
                            pool.indirect_dma_start(buf[u][:, t * w:(t + 1) * w], None,
                                                    table[:, :], row, bounds_check=bound,
                                                    oob_is_err=False).then_inc(came[u], 16)

        @block.vector
        def _(dve):
            link = Link(dve, dve_own)

            def prepare(g, u, n):
                for part, (buf, came) in enumerate(((gs, src_in), (gd, dst_in))):
                    dve.wait_ge(came[u], n * (16 * G) + 16 * G)
                    at_least(dve, hs, g * 2)
                    ln_stats(dve, link, m, tiles(buf[u]), part, stats)
                for part in range(2):
                    dve.wait_ge(std, g * 2 + (part + 1) + ONE)
                    ln_scales(dve, link, m, part, G, scales)
                dve.tensor_tensor(
                    m.xs[:, ds(g * GD, GD)].rearrange("p (t d) -> p t d", t=G),
                    gs[u].rearrange("p (t d) -> p t d", t=G),
                    m.bias0_b.unsqueeze(1).to_broadcast([P, G, D]), ALU.add).then_inc(kept[u], 1)

            def body(g, u, n, first, last):
                if not last:
                    prepare(g + 1, 1 - u, n + u)
                for b in range(2):
                    dve.wait_ge(prods, g * 2 + (b + 1) + ONE)
                    dve.tensor_copy(m.xh[:, ds(g * GD + b * 2 * D, 2 * D)], psY[b])\
                        .then_inc(pout, 1)

            prepare(0, 0, 0)
            each_group(dve, link, 20, body)

        @block.scalar
        def _(act):
            def normal(g, u):
                for part in range(2):
                    _, var, s = ln_parts(m, part, G)
                    act.wait_ge(stats, g * 2 + (part + 1) + ONE)
                    act.activation(s[0], var, ACT.Sqrt, bias=m.eps[:, :]).then_inc(std, 1)
                for part, buf in enumerate((gs, gd)):
                    act.wait_ge(scales, g * 2 + (part + 1) + ONE)
                    at_least(act, turned, g * 2)
                    ln_apply(act, m, tiles(buf[u]), part, m.h[part], hs)

            def body(g, u, n, first, last):
                for part in range(2):
                    act.wait_ge(turned, g * 2 + (part + 1) + ONE)
                    at_least(act, logit, g)
                    act.activation(m.hT[part][:, :], m.PS[:, 0:1024], ACT.Copy).then_inc(tout, 1)
                act.wait_ge(eturn[u], n + 1 + ONE)
                act.activation(m.eaT[:, :], psE, ACT.Copy).then_inc(eout, 1)
                if not last:
                    normal(g + 1, 1 - u)
                act.wait_ge(logit, g + 1 + ONE)
                act.activation(sA[0:H, ds(g * 512, 512)], psA, ACT.Copy)
                act.activation(sL[0:H, ds(g * 512, 512)], psZ, ACT.Identity,
                               bias=m.amean[:, :]).then_inc(lout, 1)

            normal(0, 0)
            each_group(act, None, 0, body)

        @block.tensor
        def _(pe):
            with pe.Fori(0, EG // 2) as i:
                for u in range(2):
                    g = i * 2 + u
                    for part in range(2):
                        pe.wait_ge(hs, g * 2 + (part + 1) + ONE)
                        pe.wait_ge(tout, g * 2 + part + ONE)
                        turn(pe, m, m.h[part], m.PS[:, 0:1024], G, turned)
                    pe.wait_ge(ea_in[u], i * (16 * G) + 16 * G)
                    pe.wait_ge(eout, g + ONE)
                    pe.sem_inc(m.gate_pe, 1)
                    for t in range(G):
                        last = pe.transpose(psE[:, t * P:(t + 1) * P],
                                            ge[u][:, t * ED:(t + 1) * ED], m.ident[:, :])
                    last.then_inc(eturn[u], 1)
                    pe.wait_ge(tout, g * 2 + 1 + ONE)
                    for b in range(2):
                        pe.wait_ge(pout, g * 2 + b + ONE)
                        for t in (2 * b, 2 * b + 1):
                            for k in range(2):
                                last = pe.matmul(psY[b][:, (t % 2) * D:(t % 2 + 1) * D],
                                                 m.hT[0][:, k * 512 + t * P:k * 512 + (t + 1) * P],
                                                 m.w0[:, k * D:(k + 1) * D],
                                                 start=(k == 0), stop=(k == 1))
                        last.then_inc(prods, 1)
                    pe.wait_ge(lout, g + ONE)
                    pe.wait_ge(tout, g * 2 + 2 + ONE)
                    pe.wait_ge(eout, g + 1 + ONE)
                    for k in range(2):
                        o = k * 3 * H
                        pe.matmul(psA, m.wa[:, o:o + H], m.hT[0][:, k * 512:(k + 1) * 512],
                                  start=(k == 0), stop=False)
                        pe.matmul(psA, m.wa[:, o + H:o + 2 * H], m.hT[1][:, k * 512:(k + 1) * 512],
                                  start=False, stop=False)
                        pe.matmul(psZ, m.wa[:, o + 2 * H:o + 3 * H],
                                  m.hT[1][:, k * 512:(k + 1) * 512], start=(k == 0), stop=(k == 1))
                    pe.matmul(psA, m.we8[:, :], m.eaT[:, :], start=False, stop=True)\
                        .then_inc(logit, 1)


def softmax(nc, sem, m):
    sA, sL, sF, sK = (m.big[0:H, k * EP:(k + 1) * EP] for k in range(4))
    new_next = m.big[0:H, 3 * EP + 1:4 * EP + 1]
    idx_s, val_s = m.idx_t, m.val_t
    staged, gate, posted = sem("sm_staged"), sem("sm_gate"), [sem(f"sm_posted{u}", 0) for u in range(2)]
    drained = [sem(f"sm_drained{u}") for u in range(2)]
    sub, exps, dve_own = sem("sm_sub"), sem("sm_exp"), sem("sm_dve")
    nc.all_engine_barrier()
    with nc.Block() as block:
        @block.sync
        def _(sp):
            drain(sp, posted, drained)

        @block.gpsimd
        def _(pool):
            bound = pool.to_reg(N - 1)
            with pool.Fori(0, EG // 2) as i:
                for u in range(2):
                    pool.wait_ge(drained[u], i + ONE)
                    pool.tensor_copy(idx_s[u][:, :], m.posidx[:, ds((i * 2 + u) * G, G)])\
                        .then_inc(staged, 1)
                    pool.tensor_copy(val_s[u][:, :], m.place[:, ds((i * 2 + u) * G, G)])\
                        .then_inc(staged, 1)
                    pool.wait_ge(staged, i * 4 + (2 * u + 2) + ONE)
                    pool.sem_inc(gate, 1)
                    for t in range(G):
                        pool.indirect_dma_start(
                            m.pos_d[:, :],
                            bass.IndirectOffsetOnAxis(ap=idx_s[u][:, t:t + 1], axis=0),
                            val_s[u][:, t:t + 1], None, bounds_check=bound,
                            oob_is_err=False).then_inc(posted[u], 16)
            for u in range(2):
                pool.wait_ge(posted[u], EG // 2 * 16 * G)

        @block.vector
        def _(dve):
            link = Link(dve, dve_own)
            dve.scalar_tensor_tensor(sA, sA, SLOPE, sA, ALU.mult, ALU.max)
            link(dve.scalar_tensor_tensor(sL, sL, SLOPE, sL, ALU.mult, ALU.max))
            link(dve.tensor_tensor(sF, sA, sL, ALU.max))
            link(dve.tensor_tensor_scan(sF, sK, sF, -BIG, ALU.add, ALU.max))
            link(dve.tensor_tensor_scan(sF[:, ::-1], new_next[:, ::-1], sF[:, ::-1], -BIG,
                                        ALU.add, ALU.max))
            dve.tensor_tensor(sA, sA, sF, ALU.subtract).then_inc(sub, 1)
            dve.tensor_tensor(sL, sL, sF, ALU.subtract).then_inc(sub, 1)
            full = [m.big[:, k * EP:(k + 1) * EP] for k in range(3)]
            dve.wait_ge(sub, 2 + ONE)
            dve.wait_ge(exps, 1 + ONE)
            to_edge_major(dve, link, full[0], full[2], m.ex)
            dve.wait_ge(exps, 2 + ONE)
            to_edge_major(dve, link, full[1], full[2], m.exs)

        @block.scalar
        def _(act):
            for k, s in enumerate((sA, sL)):
                act.wait_ge(sub, k + 1 + ONE)
                act.activation(s, s, ACT.Exp).then_inc(exps, 1)


def weights(nc, sem, m):
    raw = m.h[0], m.h[1]
    loaded, raws, cleared, turned, dve_own = (sem("we_loaded"), sem("we_raws"), sem("we_cleared"),
                                              sem("we_turned"), sem("we_dve"))
    nc.all_engine_barrier()
    with nc.Block() as block:
        @block.gpsimd
        def _(pool):
            pool.memset(m.bd, 0.0).then_inc(cleared, 1)

        @block.sync
        def _(sp):
            for n, w in enumerate((m.W1, m.W2)):
                sp.dma_start(raw[n][:, 0:2 * D].rearrange("p (j c) -> p j c", j=2),
                             w.rearrange("(j p) c -> p j c", p=P)).then_inc(raws, 16)
            sp.dma_start(m.drow, m.row_d[0, 1:EP + 1].partition_broadcast(P)).then_inc(loaded, 16)
            for l in range(2):
                for k in range(2):
                    sp.dma_start(m.wb[l][:, k * NB * D:(k + 1) * NB * D].rearrange(
                        "p (b o) -> p b o", b=NB),
                        m.bases[l, :, k * P:(k + 1) * P, :].rearrange("b p o -> p b o"))\
                        .then_inc(loaded, 16)
                sp.dma_start(m.wr[l].rearrange("p (k o) -> p k o", k=2),
                             m.roots[l].rearrange("(k p) o -> p k o", p=P)).then_inc(loaded, 16)
            sp.wait_ge(cleared, 1 + ONE)
            for k in range(2):
                for j in range(4):
                    b = 4 * k + j
                    sp.dma_start(
                        m.bd[C * j:C * (j + 1), k * R * P:(k + 1) * R * P].rearrange(
                            "i (r o) -> i r o", r=R)[:, :, C * j:C * (j + 1)],
                        m.L1w[:, b * C * C:(b + 1) * C * C].rearrange("r (i o) -> i r o", i=C))\
                        .then_inc(loaded, 16)
            sp.wait_ge(loaded, 16 * 15 + ONE)

        @block.tensor
        def _(pe):
            pe.wait_ge(raws, 32 + ONE)
            for n in range(2):
                for k in range(2):
                    for j in range(2):
                        last = pe.transpose(
                            m.PS[:, (n * 2 + k) * D + j * P:(n * 2 + k) * D + (j + 1) * P],
                            raw[n][:, j * D + k * P:j * D + (k + 1) * P], m.ident[:, :])
            last.then_inc(turned, 1)

        @block.vector
        def _(dve):
            dve.wait_ge(turned, 1 + ONE)
            dve.tensor_copy(m.w1t, m.PS[:, 0:2 * D])
            dve.tensor_copy(m.w2t, m.PS[:, 2 * D:4 * D])


def equality(dve, m, row, col, tau, s, done):
    dve.tensor_scalar(m.eq[s][:, :], row[:, ds(tau * P, P)], col[:, ds(tau + 1, 1)], None,
                      ALU.is_equal)
    dve.tensor_scalar(m.carry[s][96:P, :], row[96:P, ds(tau * P, P)], col[96:P, ds(tau, 1)],
                      m.e127[96:P, :], ALU.is_equal, ALU.mult).then_inc(done, 1)


def edge_layer0(nc, sem, m):
    cut = Carve(m.work)
    msg = [cut(AW) for _ in range(2)]
    o = [cut(G * AW) for _ in range(2)]
    nrm = [cut(G * AW) for _ in range(2)]
    z = cut(2 * G * H)
    pss = [m.PS[:, 3072:3072 + AW], m.PS[:, 3584:3584 + AW]]
    made, summed, out_of, normed = sem("l0_made"), sem("l0_summed"), sem("l0_out"), sem("l0_norm")
    zeroed, dve_own = sem("l0_zeroed"), sem("l0_dve")
    stored = [sem(f"l0_stored{u}") for u in range(2)]
    idx_s, val_s = m.idx_t, m.val_t
    staged, gate, looked, nodes_in = (sem("l0_staged"), sem("l0_gate"), sem("l0_looked"),
                                      sem("l0_nodes"))
    found = [sem(f"l0_found{u}", 0) for u in range(2)]

    nc.all_engine_barrier()
    with nc.Block() as block:
        @block.gpsimd
        def _(pool):
            pool.memset(o[1][:, 3 * AW:4 * AW], 0.0).then_inc(zeroed, 1)
            with pool.Fori(0, EG // 2) as i:
                for u in range(2):
                    pool.wait_ge(looked, i * 2 + ONE)
                    pool.tensor_copy(idx_s[u][:, :], m.srec[:, ds((i * 2 + u) * (8 * G), 8 * G)]
                                     .rearrange("p (t c) -> p t c", c=8)[:, :, 0])\
                        .then_inc(staged, 1)
                    pool.wait_ge(staged, i * 2 + (u + 1) + ONE)
                    pool.sem_inc(gate, 1)
                    for t in range(G):
                        pool.indirect_dma_start(
                            val_s[u][:, t:t + 1], None, m.pos_d[:, :],
                            bass.IndirectOffsetOnAxis(ap=idx_s[u][:, t:t + 1], axis=0))\
                            .then_inc(found[u], 16)
                    if u == 1:
                        for v in range(2):
                            pool.wait_ge(found[v], i * (16 * G) + 16 * G)
                            pool.tensor_copy(m.poss[:, ds((i * 2 + v) * G, G)], val_s[v][:, :])\
                                .then_inc(looked, 1)

        @block.vector
        def _(dve):
            link = Link(dve, dve_own)

            def norm(g, u, n):
                o4 = o[u].rearrange("p (t c) -> p t c", t=G)
                n4 = nrm[u].rearrange("p (t c) -> p t c", t=G)
                zu = z[:, u * G * H:(u + 1) * G * H].rearrange("p (t h) -> p t h", t=G)
                exs = m.exs[:, ds(g * (G * H), G * H)].rearrange("p (t h) -> p t h", t=G)
                dve.wait_ge(out_of, g * G + (G + 2) + ONE)
                dve.wait_ge(stored[u], n * 32 + ONE)
                link(dve.tensor_tensor(zu, o4[:, :, D:AW], exs, ALU.add))
                link(dve.tensor_scalar(zu, zu, 1e-16, None, ALU.add))
                link(dve.reciprocal(zu, zu))
                for t in range(G):
                    dve.tensor_tensor(n4[:, t, 0:D].rearrange("p (h c) -> p h c", c=C),
                                      o4[:, t, 0:D].rearrange("p (h c) -> p h c", c=C),
                                      bc(zu[:, t, :], C), ALU.mult)
                dve.tensor_tensor(n4[:, :, D:AW], exs, zu, ALU.mult).then_inc(normed, 1)

            def body(g, u, n, first, last):
                for t in range(G):
                    s = t % 2
                    tau = g * G + t
                    dve.wait_ge(summed, tau + 1 + ONE)
                    dve.tensor_tensor(msg[s][:, 0:D].rearrange("p (h c) -> p h c", c=C),
                                      m.xh[:, ds(tau * D, D)].rearrange("p (h c) -> p h c", c=C),
                                      bc(m.ex[:, ds(tau * H, H)], C), ALU.mult)
                    dve.tensor_copy(msg[s][:, D:AW], m.ex[:, ds(tau * H, H)])
                    equality(dve, m, m.drow, m.dstc, tau, s, made)
                    if t == 1 and not first:
                        norm(g - 1, 1 - u, n - (1 - u))

            each_group(dve, link, 6, body)
            norm(EG - 1, 1, EG // 2 - 1)
            dve.wait_ge(looked, EG + ONE)
            link(dve.tensor_scalar(m.masks[:, :], m.poss[:, :], float(EP), None, ALU.is_lt))
            dve.tensor_scalar(m.nmasks[:, :], m.masks[:, :], -1.0, 1.0, ALU.mult, ALU.add)

        @block.tensor
        def _(pe):
            pe.sem_inc(summed, 2)
            pe.wait_ge(zeroed, 1 + ONE)

            def body(g, u, n, first, last):
                for t in range(G):
                    s = t % 2
                    tau = g * G + t
                    prev = (o[u][96:P, (t - 1) * AW:t * AW] if t else o[1 - u][96:P, 3 * AW:4 * AW])
                    pe.wait_ge(made, tau + 1 + ONE)
                    pe.wait_ge(out_of, tau + 1 + ONE)
                    pe.matmul(pss[s], m.eq[s][:, :], msg[s], start=True, stop=False)
                    pe.wait_ge(out_of, tau + 2 + ONE)
                    pe.matmul(pss[s], m.carry[s][96:P, :], prev, start=False, stop=True)\
                        .then_inc(summed, 1)
            each_group(pe, None, 0, body)

        @block.scalar
        def _(act):
            act.sem_inc(out_of, 2)

            def body(g, u, n, first, last):
                if not first:
                    act.wait_ge(normed, g - 1 + ONE)
                for t in range(G):
                    act.wait_ge(summed, g * G + (t + 3) + ONE)
                    act.activation(o[u][:, t * AW:(t + 1) * AW], pss[t % 2], ACT.Copy)\
                        .then_inc(out_of, 1)
            each_group(act, None, 0, body)

        @block.sync
        def _(sp):
            def body(g, u, n, first, last):
                sp.wait_ge(normed, g + 1 + ONE)
                n4 = nrm[u].rearrange("p (t c) -> p t c", t=G)
                sp.dma_start(m.a_d[0].rearrange("(t q) c -> q t c", q=P)[:, ds(g * G, G), :], n4)\
                    .then_inc(stored[u], 16)
                sp.dma_start(m.tab_d.rearrange("(t q) c -> q t c", q=P)[:, ds(g * G, G), 0:H],
                             n4[:, :, D:AW]).then_inc(stored[u], 16)
            sp.dma_start(m.posn[:, 0:NT],
                         m.pos_d[0:NT * P, :].rearrange("(p t) c -> p (t c)", p=P))\
                .then_inc(nodes_in, 16)
            sp.dma_start(m.posn[0:REM, NT:NT + 1], m.pos_d[NT * P:N, :]).then_inc(nodes_in, 16)
            sp.wait_ge(nodes_in, 32 + ONE)
            each_group(sp, None, 0, body)
            for u in range(2):
                sp.wait_ge(stored[u], EG // 2 * 32 + ONE)


def edge_layer(nc, sem, m, k):
    halves = 2 if k == 1 else 1
    comps = 4
    co = {1: m.co1, 2: m.co2[0], 3: m.co2[1]}[k]
    nco = halves * comps
    root = k == 2
    gw = AW if k == 1 else D
    cut = Carve(m.work)
    msg, other = [cut(D) for _ in range(2)], cut(D)
    o = [cut(GD) for _ in range(2)]
    rows = [cut(G * gw) for _ in range(2)]
    a0 = cut(GD) if k == 1 else None
    whole = cut(GD) if k != 2 else None
    psT = m.PS[:, 0:1024]
    psB = [m.PS[:, 1024:2048], m.PS[:, 2048:3072]]
    psR = m.PS[:, 3072:3072 + D]
    psS = [m.PS[:, (3584 if root else 3072):][:, 0:D], m.PS[:, 3584:3584 + D]]
    free = 2 if root else 1
    table = m.a_d[k - 1]
    col = H + (k - 1) * D
    tab = m.tab_d.rearrange("(t q) c -> q t c", q=P)[:, :, col:col + D]

    def s_(name):
        return sem(f"l{k}_{name}")

    blank, staged, gate, zeroed = s_("blank"), s_("staged"), s_("gate"), s_("zeroed")
    stats, std, scales, hs = s_("stats"), s_("std"), s_("scales"), s_("h")
    turned, tout = s_("turned"), s_("tout")
    prods, eaten, rooted, rout = s_("prods"), s_("eaten"), s_("rooted"), s_("rout")
    made, summed, out_of, dve_own = s_("made"), s_("summed"), s_("out"), s_("dve")
    updated, o_sent, tab_sent = ([s_(f"{name}{u}") for u in range(2)] for name in
                                 ("updated", "o_sent", "tab_sent"))
    rows_in = [sem(f"l{k}_rows_in{u}", 0) for u in range(2)]
    a0_in, joined, whole_sent, pool_own = (s_("a0_in"), s_("joined"), s_("whole_sent"),
                                           s_("pool"))

    nc.all_engine_barrier()
    with nc.Block() as block:
        @block.gpsimd
        def _(pool):
            for b in rows:
                pool.memset(b, 0.0).then_inc(blank, 1)
            pool.memset(o[1][:, 3 * D:4 * D], 0.0).then_inc(zeroed, 1)
            pool.wait_ge(blank, 2 + ONE)
            bound = pool.to_reg(EP - 1)

            def gather(g, u, n):
                pool.wait_ge(updated[u], n + ONE)
                pool.tensor_copy(m.idx_s[u][:, 0:G], m.poss[:, ds(g * G, G)]).then_inc(staged, 1)
                pool.wait_ge(staged, g + 1 + ONE)
                pool.sem_inc(gate, 1)
                for t in range(G):
                    pool.indirect_dma_start(
                        rows[u][:, t * gw:(t + 1) * gw], None, table,
                        bass.IndirectOffsetOnAxis(ap=m.idx_s[u][:, t:t + 1], axis=0),
                        bounds_check=bound, oob_is_err=False).then_inc(rows_in[u], 16)

            def join(g, u):
                bias = (m.bias0_b if k == 1 else m.bias1_b).unsqueeze(1).to_broadcast([P, G, D])
                w3, o3 = (b.rearrange("p (t d) -> p t d", t=G) for b in (whole, o[u]))
                pool.wait_ge(out_of, g * G + (G + 2) + ONE)
                at_least(pool, whole_sent, g * 16)
                pool.sem_inc(gate, 1)
                added = pool.tensor_tensor(w3, o3, bias, ALU.add)
                if k == 1:
                    added.then_inc(pool_own, 1)
                    pool.wait_ge(pool_own, g + 1 + ONE)
                    pool.wait_ge(a0_in, g * 16 + 16 + ONE)
                    pool.sem_inc(gate, 1)
                    added = pool.tensor_tensor(whole, whole, a0, ALU.add)
                added.then_inc(joined, 1)

            def body(g, u, n, first, last):
                if not last:
                    gather(g + 1, 1 - u, n + u)
                if k != 2 and not first:
                    join(g - 1, 1 - u)

            gather(0, 0, 0)
            each_group(pool, None, 0, body)
            if k != 2:
                join(EG - 1, 1)

        @block.sync
        def _(sp):
            def body(g, u, n, first, last):
                if k == 1:
                    sp.wait_ge(joined, g + ONE)
                    sp.dma_start(a0.rearrange("p (t c) -> p t c", t=G),
                                 table.rearrange("(t q) c -> q t c", q=P)[:, ds(g * G, G), 0:D])\
                        .then_inc(a0_in, 16)
                sp.wait_ge(out_of, g * G + (G + 2) + ONE)
                o4 = o[u].rearrange("p (t c) -> p t c", t=G)
                if k < 3:
                    sp.dma_start(m.a_d[k].rearrange("(t q) c -> q t c", q=P)[:, ds(g * G, G), :],
                                 o4).then_inc(o_sent[u], 16)
                if k == 2:
                    sp.dma_start(tab[:, ds(g * G, G), :], o4).then_inc(tab_sent[u], 16)
                else:
                    if k == 3:
                        sp.sem_inc(m.gate_sp, 1)
                    sp.wait_ge(joined, g + 1 + ONE)
                    sp.sem_inc(m.gate_sp, 1)
                    sp.dma_start(tab[:, ds(g * G, G), :], whole.rearrange("p (t c) -> p t c", t=G))\
                        .then_inc(whole_sent, 16)

            each_group(sp, None, 0, body)
            for u in range(2):
                if k < 3:
                    sp.wait_ge(o_sent[u], EG // 2 * 16 + ONE)
                if k == 2:
                    sp.wait_ge(tab_sent[u], EG // 2 * 16 + ONE)
            if k != 2:
                sp.wait_ge(whole_sent, EG * 16 + ONE)

        @block.vector
        def _(dve):
            link = Link(dve, dve_own)

            def prepare(g, u, n):
                x4 = m.xs[:, ds(g * GD, GD)].rearrange("p (t d) -> p t d", t=G)
                r4 = rows[u].rearrange("p (t c) -> p t c", t=G)
                xt = [m.xs[:, ds(g * GD + t * D, D)] for t in range(G)]
                dve.wait_ge(rows_in[u], n * (16 * G) + 16 * G)
                dve.wait_ge(hs, g + ONE)
                if k == 3:
                    dve.wait_ge(turned, g + ONE)
                    for t in range(G):
                        last = dve.scalar_tensor_tensor(
                            m.h[u][:, t * D:(t + 1) * D], r4[:, t, 0:D],
                            m.masks[:, ds(g * G + t, 1)], m.xh[:, ds(g * GD + t * D, D)],
                            ALU.mult, ALU.add)
                    value = link.mark(last)
                    link.until(value)
                    dve.sem_inc(hs, 1)
                    dve.sem_inc(updated[u], 1)
                    return
                if k == 1:
                    xh8 = m.xh[:, ds(g * GD, GD)].rearrange("p (a c) -> p a c", c=C)
                    al = m.alpha[:, u * G * H:(u + 1) * G * H]
                    for t in range(G):
                        last = dve.scalar_tensor_tensor(
                            al[:, t * H:(t + 1) * H], r4[:, t, D:AW],
                            m.masks[:, ds(g * G + t, 1)],
                            m.nmasks[:, ds(g * G + t, 1)].to_broadcast([P, H]),
                            ALU.mult, ALU.add)
                    link(last)
                    link(dve.tensor_tensor(xh8, xh8, bc(al, C), ALU.mult))
                    link(dve.tensor_tensor(m.xs[:, ds(g * GD, GD)], m.xs[:, ds(g * GD, GD)],
                                           m.xh[:, ds(g * GD, GD)], ALU.add))
                for t in range(G):
                    last = dve.scalar_tensor_tensor(xt[t], r4[:, t, 0:D],
                                                    m.masks[:, ds(g * G + t, 1)], xt[t],
                                                    ALU.mult, ALU.add)
                link(last)
                dve.sem_inc(updated[u], 1)

            def measure(g, u):
                ln_stats(dve, link, m, [m.xs[:, ds(g * GD + t * D, D)] for t in range(G)], u,
                         stats)
                dve.wait_ge(std, g + 1 + ONE)
                ln_scales(dve, link, m, u, G, scales)

            def message(g, t):
                s, tau = t % 2, g * G + t
                dve.wait_ge(summed, tau + 1 + ONE)
                at_least(dve, made, tau)
                sums, ended = (msg[s], other), [None, None]
                for hf in range(halves):
                    dve.wait_ge(prods, tau * halves + (hf + 1) + ONE)
                    b = psB[hf if halves == 2 else s]
                    for c in range(comps):
                        to = sums[c % 2]
                        if k == 1:
                            part = b.rearrange("p (k r o) -> p k r o", k=2, r=4)[:, :, c, :]
                            to = to.rearrange("p (k o) -> p k o", k=2)
                        else:
                            part = b[:, c * D:(c + 1) * D]
                        w = co[:, ds(tau * nco + hf * comps + c, 1)]
                        if ended[c % 2] is None:
                            last = dve.tensor_scalar(to, part, w, None, ALU.mult)
                        else:
                            link.until(ended[c % 2])
                            last = dve.scalar_tensor_tensor(to, part, w, to, ALU.mult, ALU.add)
                        ended[c % 2] = link.mark(last)
                    link.until(ended[1])
                    dve.sem_inc(eaten, 1)
                dve.tensor_tensor(msg[s], msg[s], other, ALU.add)
                equality(dve, m, m.drow, m.dstc, tau, s, made)

            def body(g, u, n, first, last):
                for t in range(G):
                    message(g, t)
                    if t == 0 and not last:
                        prepare(g + 1, 1 - u, n + u)
                    if t == 1 and not last and k < 3:
                        measure(g + 1, 1 - u)

            dve.sem_inc(eaten, 2)
            prepare(0, 0, 0)
            if k < 3:
                measure(0, 0)
            per = {1: 2 * (4 * 8 + 9), 2: 2 * (4 * 4 + 6), 3: 2 * (4 * 4 + 1)}[k]
            each_group(dve, link, per, body)

        @block.scalar
        def _(act):
            def normal(g, u, n):
                _, var, s = ln_parts(m, u, G)
                xt = [m.xs[:, ds(g * GD + t * D, D)] for t in range(G)]
                act.wait_ge(stats, g + 1 + ONE)
                act.activation(s[0], var, ACT.Sqrt, bias=m.eps[:, :]).then_inc(std, 1)
                act.wait_ge(scales, g + 1 + ONE)
                ln_apply(act, m, xt, u, m.h[u], hs)

            def turned_out(g, u):
                act.wait_ge(turned, g + 1 + ONE)
                if k == 3:
                    for c in range(2):
                        last = act.activation(m.hT[u][:, c * 512:(c + 1) * 512],
                                              psT[:, c * 512:(c + 1) * 512], ACT.Relu,
                                              bias=m.b0col[:, c:c + 1])
                else:
                    last = act.activation(m.hT[u][:, :], psT, ACT.Copy)
                last.then_inc(tout, 1)

            def sum_out(tau, u, t):
                act.wait_ge(summed, tau + 3 + ONE)
                act.activation(o[u][:, t * D:(t + 1) * D], psS[t % 2], ACT.Copy)\
                    .then_inc(out_of, 1)

            def root_out(g, t):
                if k == 2:
                    act.wait_ge(rooted, g * G + (t + 1) + ONE)
                    act.activation(m.xh[:, ds((g * G + t) * D, D)], psR, ACT.Copy)\
                        .then_inc(rout, 1)

            def body(g, u, n, first, last):
                root_out(g, 0)
                if not first:
                    sum_out(g * G - 1, 1 - u, 3)
                if k < 3:
                    act.wait_ge(o_sent[u], n * 16 + ONE)
                if k == 2:
                    act.wait_ge(tab_sent[u], n * 16 + ONE)
                elif not first:
                    act.wait_ge(joined, g - 1 + ONE)
                root_out(g, 1)
                sum_out(g * G, u, 0)
                if not last:
                    if k != 3:
                        normal(g + 1, 1 - u, n + u)
                root_out(g, 2)
                sum_out(g * G + 1, u, 1)
                root_out(g, 3)
                if not last:
                    turned_out(g + 1, 1 - u)
                sum_out(g * G + 2, u, 2)

            act.sem_inc(out_of, 2)
            if k == 2:
                act.sem_inc(rout, 1)
            if k != 3:
                normal(0, 0, 0)
            turned_out(0, 0)
            each_group(act, None, 0, body)
            sum_out(EP // P - 1, 1, 3)

        @block.tensor
        def _(pe):
            def products(g, u, t):
                tau = g * G + t
                s = t % 2
                hT = [m.hT[u][:, c * 512 + t * P:c * 512 + (t + 1) * P] for c in range(2)]
                pe.wait_ge(tout, g + 1 + ONE)
                if root:
                    pe.wait_ge(rout, tau + 1 + ONE)
                    for c in range(2):
                        last = pe.matmul(psR, hT[c], m.wr[0][:, c * D:(c + 1) * D],
                                         start=(c == 0), stop=(c == 1))
                    last.then_inc(rooted, 1)
                for hf in range(halves):
                    b = psB[hf if halves == 2 else s]
                    pe.wait_ge(eaten, tau * halves + (hf + 1) + ONE)
                    if k == 1:
                        for c in range(2):
                            last = pe.matmul(b[:, c * 512:(c + 1) * 512], hT[c],
                                             m.bd[:, (c * 2 + hf) * 512:(c * 2 + hf + 1) * 512],
                                             start=True, stop=True)
                    else:
                        for j in range(2):
                            for c in range(2):
                                last = pe.matmul(
                                    b[:, j * 512:(j + 1) * 512], hT[c],
                                    m.wb[k - 2][:, (c * 2 + j) * 512:(c * 2 + j + 1) * 512],
                                    start=(c == 0), stop=(c == 1))
                    last.then_inc(prods, 1)

            def sums(tau, u, t):
                s = t % 2
                prev = (o[u][96:P, (t - 1) * D:t * D] if t else o[1 - u][96:P, 3 * D:4 * D])
                pe.wait_ge(made, tau + 1 + ONE)
                pe.wait_ge(out_of, tau + free + ONE)
                pe.matmul(psS[s], m.eq[s][:, :], msg[s], start=True, stop=False)
                pe.wait_ge(out_of, tau + 2 + ONE)
                pe.matmul(psS[s], m.carry[s][96:P, :], prev, start=False, stop=True)\
                    .then_inc(summed, 1)

            def turn_group(g, u):
                pe.wait_ge(hs, g + 1 + ONE)
                pe.wait_ge(tout, g + ONE)
                turn(pe, m, m.h[u], psT, G, turned)

            def body(g, u, n, first, last):
                for t in range(G):
                    products(g, u, t)
                    if t == 3 and not last:
                        turn_group(g + 1, 1 - u)
                    if t:
                        sums(g * G + (t - 1), u, t - 1)
                    elif not first:
                        sums(g * G - 1, 1 - u, 3)

            pe.sem_inc(summed, 2)
            pe.wait_ge(zeroed, 1 + ONE)
            turn_group(0, 0)
            each_group(pe, None, 0, body)
            sums(EP // P - 1, 1, 3)


def sage(nc, sem, m):
    MW = D + 2
    cut, cuth = Carve(m.xs), Carve(m.xh)
    srow = cuth(EP)
    rows, res = [cut(GD) for _ in range(2)], [cut(GD) for _ in range(2)]
    o, msg = [cut(G * MW) for _ in range(2)], [cut(MW) for _ in range(2)]
    inv = cut(2 * G)
    psT = m.PS[:, 0:1024]
    psB = [m.PS[:, 1024:1024 + D], m.PS[:, 1536:1536 + D]]
    psS = [m.PS[:, 2048:2048 + MW], m.PS[:, 2560:2560 + MW]]
    blank, staged, gate, ready, got_row = (sem("sg_blank"), sem("sg_staged"), sem("sg_gate"),
                                           sem("sg_ready"), sem("sg_row"))
    turned, tout, prods, made, summed, out_of, done = (
        sem("sg_turned"), sem("sg_tout"), sem("sg_prods"), sem("sg_made"), sem("sg_summed"),
        sem("sg_out"), sem("sg_done"))
    rows_in, res_in, sent = ([sem(f"sg_{k}{u}", 0) for u in range(2)] for k in
                             ("rows_in", "res_in", "sent"))
    drained = [sem(f"sg_drained{u}") for u in range(2)]
    dve_own, put = sem("sg_dve"), sem("sg_put")
    nc.all_engine_barrier()
    with nc.Block() as block:
        @block.sync
        def _(sp):
            sp.dma_start(srow, m.row2_d[0, 0:EP].partition_broadcast(P)).then_inc(got_row, 16)
            sp.wait_ge(got_row, 16 + ONE)
            drain(sp, sent, drained)

        @block.gpsimd
        def _(pool):
            for b in (*rows, *res):
                pool.memset(b, 0.0).then_inc(blank, 1)
            pool.memset(o[1][:, 3 * MW:4 * MW], 0.0).then_inc(ready, 1)
            for b in msg:
                pool.memset(b[:, D:MW], 1.0).then_inc(ready, 1)
            pool.wait_ge(blank, 4 + ONE)
            bound = pool.to_reg(N - 1)

            def heads(g, u, n):
                at_least(pool, turned, g - 1)
                pool.tensor_copy(m.idx_s[u][:, :], m.srec2[:, ds(g * (8 * G), 8 * G)])\
                    .then_inc(staged, 1)
                pool.wait_ge(staged, g + 1 + ONE)
                pool.sem_inc(gate, 1)
                for t in range(G):
                    pool.indirect_dma_start(
                        rows[u][:, t * D:(t + 1) * D], None, m.h3_d[:, :],
                        bass.IndirectOffsetOnAxis(ap=m.idx_s[u][:, 8 * t + 1:8 * t + 2], axis=0),
                        bounds_check=bound, oob_is_err=False).then_inc(rows_in[u], 16)

            def fetch(g, u, n):
                at_least(pool, drained[u], n)
                pool.sem_inc(gate, 1)
                pool.tensor_copy(m.idx_t[u][:, :], m.to_node[:, ds(g * G, G)]).then_inc(put, 1)
                pool.wait_ge(put, g + 1 + ONE)
                pool.sem_inc(gate, 1)
                for t in range(G):
                    pool.indirect_dma_start(
                        res[u][:, t * D:(t + 1) * D], None, m.out[:, :],
                        bass.IndirectOffsetOnAxis(ap=m.idx_t[u][:, t:t + 1], axis=0),
                        bounds_check=bound, oob_is_err=False).then_inc(res_in[u], 16)

            def scatter(g, u):
                pool.wait_ge(done, g + 1 + ONE)
                pool.sem_inc(gate, 1)
                for t in range(G):
                    pool.indirect_dma_start(
                        m.out[:, :],
                        bass.IndirectOffsetOnAxis(ap=m.idx_t[u][:, t:t + 1], axis=0),
                        res[u][:, t * D:(t + 1) * D], None,
                        bounds_check=bound, oob_is_err=False).then_inc(sent[u], 16)

            def body(g, u, n, first, last):
                if not last:
                    heads(g + 1, 1 - u, n + u)
                if not first:
                    scatter(g - 1, 1 - u)
                if not last:
                    fetch(g + 1, 1 - u, n + u)

            heads(0, 0, 0)
            fetch(0, 0, 0)
            each_group(pool, None, 0, body)
            scatter(EG - 1, 1)
            for u in range(2):
                pool.wait_ge(sent[u], EG // 2 * 16 * G)

        @block.vector
        def _(dve):
            link = Link(dve, dve_own)

            def result(g, u, n):
                o4 = o[u].rearrange("p (t c) -> p t c", t=G)
                iv = inv[:, u * G:(u + 1) * G]
                dve.wait_ge(out_of, g * G + (G + 2) + ONE)
                link(dve.reciprocal(iv.unsqueeze(2), o4[:, :, D:D + 1]))
                dve.wait_ge(res_in[u], n * (16 * G) + 16 * G)
                for t in range(G):
                    r = res[u][:, t * D:(t + 1) * D]
                    last = dve.scalar_tensor_tensor(r, o4[:, t, 0:D], iv[:, t:t + 1], r,
                                                    ALU.mult, ALU.add)
                last.then_inc(done, 1)

            def body(g, u, n, first, last):
                for t in range(G):
                    s, tau = t % 2, g * G + t
                    dve.wait_ge(summed, tau + 1 + ONE)
                    dve.wait_ge(prods, tau + 1 + ONE)
                    dve.tensor_copy(msg[s][:, 0:D], psB[s])
                    equality(dve, m, srow, m.srcc, tau, s, made)
                    if t == 1 and not first:
                        result(g - 1, 1 - u, n - (1 - u))

            dve.wait_ge(got_row, 16 + ONE)
            dve.wait_ge(ready, 3 + ONE)
            each_group(dve, link, 2, body)
            result(EG - 1, 1, EG // 2 - 1)

        @block.scalar
        def _(act):
            def turned_out(g, u):
                act.wait_ge(turned, g + 1 + ONE)
                act.activation(m.hT[u][:, :], psT, ACT.Copy).then_inc(tout, 1)

            def sum_out(tau, u, t):
                act.wait_ge(summed, tau + 3 + ONE)
                act.activation(o[u][:, t * MW:(t + 1) * MW], psS[t % 2], ACT.Copy)\
                    .then_inc(out_of, 1)

            def body(g, u, n, first, last):
                if not first:
                    sum_out(g * G - 1, 1 - u, 3)
                    act.wait_ge(done, g - 1 + ONE)
                sum_out(g * G, u, 0)
                sum_out(g * G + 1, u, 1)
                if not last:
                    turned_out(g + 1, 1 - u)
                sum_out(g * G + 2, u, 2)

            act.sem_inc(out_of, 2)
            turned_out(0, 0)
            each_group(act, None, 0, body)
            sum_out(ET - 1, 1, 3)

        @block.tensor
        def _(pe):
            def turn_group(g, u, n):
                pe.wait_ge(rows_in[u], n * (16 * G) + 16 * G)
                pe.wait_ge(tout, g + ONE)
                turn(pe, m, rows[u], psT, G, turned)

            def product(g, u, t):
                tau, s = g * G + t, t % 2
                pe.wait_ge(tout, g + 1 + ONE)
                if not (isinstance(tau, int) and tau < 2):
                    pe.wait_ge(made, tau - 1 + ONE)
                for c in range(2):
                    last = pe.matmul(psB[s], m.hT[u][:, c * 512 + t * P:c * 512 + (t + 1) * P],
                                     m.w2t[:, c * D:(c + 1) * D], start=(c == 0), stop=(c == 1))
                last.then_inc(prods, 1)

            def sums(tau, u, t):
                s = t % 2
                prev = (o[u][96:P, (t - 1) * MW:t * MW] if t else o[1 - u][96:P, 3 * MW:4 * MW])
                pe.wait_ge(made, tau + 1 + ONE)
                pe.wait_ge(out_of, tau + 1 + ONE)
                pe.matmul(psS[s], m.eq[s][:, :], msg[s], start=True, stop=False)
                pe.wait_ge(out_of, tau + 2 + ONE)
                pe.matmul(psS[s], m.carry[s][96:P, :], prev, start=False, stop=True)\
                    .then_inc(summed, 1)

            def body(g, u, n, first, last):
                for t in range(G):
                    product(g, u, t)
                    if t == 3 and not last:
                        turn_group(g + 1, 1 - u, n + u)
                    if t:
                        sums(g * G + (t - 1), u, t - 1)
                    elif not first:
                        sums(g * G - 1, 1 - u, 3)

            pe.sem_inc(summed, 2)
            pe.wait_ge(ready, 3 + ONE)
            turn_group(0, 0, 0)
            each_group(pe, None, 0, body)
            sums(ET - 1, 1, 3)


def nodes(nc, sem, m):
    STAGES = 3
    NQI = STAGES * NG
    cut, cuth = Carve(m.xs), Carve(m.xh)
    work = Carve(m.work)
    xin, xw = ([cut(GD) for _ in range(NG)] for _ in range(2))
    y = [cut(GD), cut(GD), work(GD), work(GD)]
    rows = [cuth(G * TW), cuth(G * TW), cuth(G * TW), m.big[:, 0:G * TW]]
    psT = [m.PS[:, 0:1024], m.PS[:, 1024:2048]]
    psY = [m.PS[:, 2048:3072], m.PS[:, 3072:4096]]
    wts = [m.w0[:, :], m.wr[1], m.w1t]
    x_v = m.x[0:NT * P, :].rearrange("(p t) d -> p (t d)", p=P)
    out_v = m.out[0:NT * P, :].rearrange("(p t) d -> p (t d)", p=P)
    h3_v = m.h3_d[0:NT * P, :].rearrange("(p t) d -> p (t d)", p=P)
    xin_in, stored, h_sent = ([sem(f"n_{k}{g}") for g in range(NG)] for k in
                              ("xin", "stored", "h_sent"))
    rows_in = [sem(f"n_rows{g}", 0) for g in range(NG)]
    filled, staged, gate = sem("n_filled"), sem("n_staged"), sem("n_gate")
    added = [sem(f"n_added{k}") for k in range(3)]
    stats, std, scales, hs = sem("n_stats"), sem("n_std"), sem("n_scales"), sem("n_h")
    first_done, relus = sem("n_first"), sem("n_relus")
    turned, tout, prods, eaten, final = (sem("n_turned"), sem("n_tout"), sem("n_prods"),
                                         sem("n_eaten"), sem("n_final"))
    dve_own = sem("n_dve")

    def size(i, g):
        return 1 if isinstance(i, int) and i == NI - 1 and g == NG - 1 else G

    def where(i, q):
        i, s, g = i + q // NQI, q % NQI // NG, q % NG
        return i, s, g, size(i, g)

    def rows_to_use(i, s, g, n):
        src = xin[g] if s == 0 else xw[g]
        return [src[:, t * D:(t + 1) * D] for t in range(n)]

    def run(eng, link, per, body):
        with eng.Fori(0, NI - 2) as i:
            if link is not None:
                link.enter(i, per)
            body(i, False)
            if link is not None:
                link.leave(NI - 2)
        body(NI - 2, False)
        body(NI - 1, True)

    nc.all_engine_barrier()
    with nc.Block() as block:
        @block.sync
        def _(sp):
            def load(i, g):
                if size(i, g) == G:
                    sp.dma_start(xin[g], x_v[:, ds((i * NG + g) * GD, GD)]).then_inc(xin_in[g], 16)
                else:
                    sp.dma_start(xin[g][0:REM, 0:D], m.x[NT * P:N, :]).then_inc(xin_in[g], 16)

            def store_h(i, g):
                sp.wait_ge(hs, i * NQI + (2 * NG + g + 1) + ONE)
                sp.sem_inc(m.gate_sp, 1)
                if size(i, g) == G:
                    sp.dma_start(h3_v[:, ds((i * NG + g) * GD, GD)], y[g])\
                        .then_inc(h_sent[g], 16)
                else:
                    sp.dma_start(m.h3_d[NT * P:N, :], y[g][0:REM, 0:D]).then_inc(h_sent[g], 16)

            def store(i, g):
                sp.wait_ge(final, i * NG + (g + 1) + ONE)
                if size(i, g) == G:
                    sp.dma_start(out_v[:, ds((i * NG + g) * GD, GD)], xw[g])\
                        .then_inc(stored[g], 16)
                else:
                    sp.dma_start(m.out[NT * P:N, :], xw[g][0:REM, 0:D]).then_inc(stored[g], 16)

            def body(i, last):
                if not last:
                    for g in range(NG):
                        sp.wait_ge(added[0], i * NG + (g + 1) + ONE)
                        sp.sem_inc(m.gate_sp, 1)
                        sp.wait_ge(hs, i * NQI + (g + 1) + ONE)
                        sp.sem_inc(m.gate_sp, 1)
                        load(i + 1, g)
                for g in range(NG):
                    store_h(i, g)
                for g in range(NG):
                    store(i, g)

            for g in range(NG):
                load(0, g)
            run(sp, None, 0, body)
            for g in range(NG):
                sp.wait_ge(stored[g], 16 * NI + ONE)
                sp.wait_ge(h_sent[g], 16 * NI + ONE)

        @block.gpsimd
        def _(pool):
            bound = pool.to_reg(EP - 1)

            def add(g, n, frm, more, k):
                pool.tensor_tensor(xw[g][:, 0:n * D].rearrange("p (t d) -> p t d", t=n),
                                   frm[:, 0:n * D].rearrange("p (t d) -> p t d", t=n),
                                   more, ALU.add).then_inc(added[k], 1)

            def table(g, n, c):
                return rows[g].rearrange("p (t c) -> p t c", t=G)[:, 0:n, c:c + D]

            def gather(i, g, n):
                j = i * NG + g
                pool.wait_ge(filled, j + 1 + ONE)
                pool.sem_inc(gate, 1)
                pool.tensor_copy(m.idx_n[g][:, 0:n], m.posn[:, ds(j * G, n)]).then_inc(staged, 1)
                pool.wait_ge(staged, j + 1 + ONE)
                pool.sem_inc(gate, 1)
                for t in range(n):
                    pool.indirect_dma_start(
                        rows[g][:, t * TW:(t + 1) * TW], None, m.tab_d[:, :],
                        bass.IndirectOffsetOnAxis(ap=m.idx_n[g][:, t:t + 1], axis=0),
                        bounds_check=bound, oob_is_err=False).then_inc(rows_in[g], 16)

            def begin(i, g, n):
                pool.wait_ge(xin_in[g], i * 16 + 16 + ONE)
                at_least(pool, stored[g], i * 16)
                pool.wait_ge(rows_in[g], i * (16 * G) + 16 * n)
                pool.sem_inc(gate, 1)
                add(g, n, xin[g], table(g, n, H), 0)

            def middle(i, g, n, s):
                pool.wait_ge(hs, i * NQI + (s * NG + g + 1) + ONE)
                pool.sem_inc(gate, 1)
                add(g, n, xw[g], table(g, n, H + 2 * D) if s == 1 else
                    m.b12_b[:, :].unsqueeze(1).to_broadcast([P, n, D]), s)

            def body(i, last):
                for g in range(NG):
                    middle(i, g, size(i, g), 1)
                for g in range(NG):
                    middle(i, g, size(i, g), 2)
                    if not last:
                        gather(i + 1, g, size(i + 1, g))
                if not last:
                    for g in range(NG):
                        begin(i + 1, g, size(i + 1, g))

            for g in range(NG):
                gather(0, g, G)
            for g in range(NG):
                begin(0, g, G)
            run(pool, None, 0, body)

        @block.vector
        def _(dve):
            link = Link(dve, dve_own)

            def prepare(i, q):
                u, Q = q % 2, i * NQI + q
                i, s, g, n = where(i, q)
                if s == 0:
                    dve.wait_ge(xin_in[g], i * 16 + 16 + ONE)
                at_least(dve, turned, Q - 1)
                ln_stats(dve, link, m, rows_to_use(i, s, g, n), u, stats)
                dve.wait_ge(std, Q + 1 + ONE)
                ln_scales(dve, link, m, u, n, scales)

            def consume(i, q):
                u, Q = q % 2, i * NQI + q
                i, s, g, n = where(i, q)
                j = i * NG + g
                ps, x = psY[u][:, 0:n * D], xw[g][:, 0:n * D]
                dve.wait_ge(prods, Q + 1 + ONE)
                if s == 0:
                    al = rows[g].rearrange("p (t c) -> p t c", t=G)[:, 0:n, 0:H]\
                        .unsqueeze(3).to_broadcast([P, n, H, C])
                    at_least(dve, h_sent[g], i * 16)
                    dve.wait_ge(rows_in[g], i * (16 * G) + 16 * n)
                    link(dve.tensor_tensor(
                        y[g][:, 0:n * D].rearrange("p (t h c) -> p t h c", h=H, c=C),
                        ps.rearrange("p (t h c) -> p t h c", h=H, c=C), al, ALU.mult))
                    dve.sem_inc(eaten, 1)
                    ps = y[g][:, 0:n * D]
                dve.wait_ge(added[s], j + 1 + ONE)
                link(dve.tensor_tensor(x, x, ps, ALU.add))
                if s > 0:
                    dve.sem_inc(eaten, 1)
                if s == 2:
                    dve.sem_inc(final, 1)

            def body(i, last):
                for q in range(NQI):
                    if not last or q + 3 < NQI:
                        prepare(i, q + 3)
                    consume(i, q)

            dve.sem_inc(eaten, 2)
            for q in range(3):
                prepare(0, q)
            run(dve, link, NG * (STAGES * 5 + 4), body)

        @block.scalar
        def _(act):
            def normal(i, q):
                u, Q = q % 2, i * NQI + q
                i, s, g, n = where(i, q)
                _, var, sc = ln_parts(m, u, n)
                act.wait_ge(stats, Q + 1 + ONE)
                act.activation(sc[0], var, ACT.Sqrt, bias=m.eps[:, :]).then_inc(std, 1)
                act.wait_ge(scales, Q + 1 + ONE)
                at_least(act, turned, Q - 1)
                ln_apply(act, m, rows_to_use(i, s, g, n), u, y[g] if s == 2 else m.h[u], hs)

            def part(ap, n):
                return ap.rearrange("p (k e) -> p k e", k=2)[:, :, 0:n * P]

            def turned_out(i, q):
                u, Q = q % 2, i * NQI + q
                i, s, g, n = where(i, q)
                act.wait_ge(turned, Q + 1 + ONE)
                at_least(act, prods, Q - 1)
                act.activation(part(m.hT[u][:, :], n), part(psT[u], n), ACT.Copy)\
                    .then_inc(tout, 1)

            def relu(i, q):
                u = q % 2
                i, s, g, n = where(i, q)
                act.wait_ge(first_done, i * NG + (g + 1) + ONE)
                for c in range(2):
                    last = act.activation(part(m.hT[u][:, :], n)[:, c, :], part(psY[u], n)[:, c, :],
                                          ACT.Relu, bias=m.b0col[:, c:c + 1])
                last.then_inc(relus, 1)

            def fill(i, g, n):
                if not (isinstance(i, int) and i == 0):
                    act.wait_ge(added[1], (i - 1) * NG + (g + 1) + ONE)
                    act.wait_ge(first_done, (i - 1) * NG + (g + 1) + ONE)
                act.activation(rows[g].rearrange("p (t c) -> p t c", t=G)[:, 0:n, :],
                               m.pre[:, :].unsqueeze(1).to_broadcast([P, n, TW]), ACT.Copy)\
                    .then_inc(filled, 1)

            def body(i, last):
                for q in range(NQI):
                    if q // NG == 1:
                        relu(i, q)
                    if not last or q + 1 < NQI:
                        turned_out(i, q + 1)
                    if not last or q + 3 < NQI:
                        normal(i, q + 3)
                    g = q - NG - 2
                    if 0 <= g < NG and not last:
                        fill(i + 1, g, size(i + 1, g))

            for g in range(NG):
                fill(0, g, G)
            normal(0, 0)
            normal(0, 1)
            turned_out(0, 0)
            normal(0, 2)
            run(act, None, 0, body)

        @block.tensor
        def _(pe):
            def turn_rows(i, q):
                u, Q = q % 2, i * NQI + q
                i, s, g, n = where(i, q)
                pe.wait_ge(hs, Q + 1 + ONE)
                at_least(pe, tout, Q - 1)
                turn(pe, m, y[g] if s == 2 else m.h[u], psT[u], n, turned)

            def first(i, q):
                u, Q = q % 2, i * NQI + q
                i, s, g, n = where(i, q)
                pe.wait_ge(tout, Q + 1 + ONE)
                pe.wait_ge(eaten, Q + 1 + ONE)
                for f in range(2):
                    to = psY[u][:, f * 512:f * 512 + n * P]
                    for c in range(2):
                        pe.matmul(to, m.wr[0][:, c * D + f * P:c * D + (f + 1) * P],
                                  m.hT[u][:, c * 512:c * 512 + n * P], start=(c == 0), stop=False)
                    for t in range(n):
                        at = t * TW + H + D + f * P
                        last = pe.matmul(to[:, t * P:(t + 1) * P], rows[g][:, at:at + P],
                                         m.ident[:, :], start=False, stop=(t == n - 1))
                last.then_inc(first_done, 1)

            def product(i, q):
                u, Q = q % 2, i * NQI + q
                i, s, g, n = where(i, q)
                if s == 1:
                    pe.wait_ge(relus, i * NG + (g + 1) + ONE)
                else:
                    pe.wait_ge(tout, Q + 1 + ONE)
                    pe.wait_ge(eaten, Q + 1 + ONE)
                for t in range(n):
                    for c in range(2):
                        last = pe.matmul(psY[u][:, t * D:(t + 1) * D],
                                         m.hT[u][:, c * 512 + t * P:c * 512 + (t + 1) * P],
                                         wts[s][:, c * D:(c + 1) * D],
                                         start=(c == 0), stop=(c == 1))
                last.then_inc(prods, 1)

            def body(i, last):
                for q in range(NQI):
                    if q // NG == 1:
                        first(i, q)
                    if not last or q + 1 < NQI:
                        turn_rows(i, q + 1)
                    product(i, q)

            turn_rows(0, 0)
            run(pe, None, 0, body)


def build(nc, x, src, dst, ea, rel, ew, W0, Wedge, att_src, att_dst, att_edge, bias0, L1w,
          comps, bases, roots, biases, W1, b1, W2, b2, out):
    ctx = ExitStack()
    m = Store()
    (m.x, m.src, m.dst, m.ea, m.rel, m.ew, m.W0, m.Wedge, m.att_src, m.att_dst, m.att_edge,
     m.bias0, m.L1w, m.comps, m.bases, m.roots, m.biases, m.W1, m.b1, m.W2, m.b2, m.out) = (
         x, src, dst, ea, rel, ew, W0, Wedge, att_src, att_dst, att_edge, bias0, L1w, comps,
         bases, roots, biases, W1, b1, W2, b2, out)
    with ctx:
        def sb(name, shape, dt=F32):
            return ctx.enter_context(nc.sbuf_tensor(name, shape, dt))

        def sem(name):
            return ctx.enter_context(nc.semaphore(name))

        def dram(name, shape, dt=F32):
            return nc.dram_tensor(name, shape, dt, kind="Internal").ap()

        m.rec_d = dram("rec_d", [EP, 8], I32)
        m.row_d = dram("row_d", [3, EP + 2])
        m.pos_d = dram("pos_d", [N, 1], I32)
        m.a_d = [dram("a0_d", [EP, AW])] + [dram(f"a{k}_d", [EP, D]) for k in (1, 2)]
        m.rec2_d = dram("rec2_d", [EP, 8], I32)
        m.row2_d = dram("row2_d", [1, EP + 1])
        m.h3_d = dram("h3_d", [N, D])
        m.tab_d = dram("tab_d", [EP, TW])

        m.xs = sb("xs", [P, ET * D])
        m.xh = sb("xh", [P, ET * D])
        m.big = sb("big", [P, 4 * EP + 1])
        m.w0 = sb("w0", [P, 2 * D])
        m.ident = sb("ident", [P, P])
        m.identb = sb("identb", [P, P], BF16)
        m.ones = sb("ones", [P, HI])
        m.onesf = sb("onesf", [P, P])
        m.iota = sb("iota", [P, HI])
        m.part = sb("part", [P, 1])
        m.e127 = sb("e127", [P, 1])
        m.tri = sb("tri", [P, P])
        m.triu = sb("triu", [P, P])
        m.eps = sb("eps", [P, 1])
        m.pre = sb("pre", [P, TW])
        m.bias0_b, m.bias1_b = m.pre[:, H:H + D], m.pre[:, H + 2 * D:TW]
        m.b12_b = sb("b12_b", [P, D])
        m.b0col = sb("b0col", [P, 2])
        m.srec = sb("srec", [P, ET * 8], I32)
        m.dstc = sb("dstc", [P, ET + 1])
        m.relc = sb("relc", [P, ET])
        m.srec2 = sb("srec2", [P, ET * 8], I32)
        m.srcc = sb("srcc", [P, ET + 1])
        m.to_node = sb("to_node", [P, ET], I32)
        m.ranks = [sb(f"rank{j}", [P, ET], I32)[:, :] for j in range(2)]
        m.posidx = sb("posidx", [P, ET], I32)
        m.place = sb("place", [P, ET], I32)
        m.poss = sb("poss", [P, ET], I32)
        m.masks = sb("masks", [P, ET])
        m.posn = sb("posn", [P, NT + 1], I32)
        m.co1 = sb("co1", [P, ET * R])
        m.co2 = [sb(f"co2_{l}", [P, ET * NB]) for l in range(2)]
        m.ex = sb("ex", [P, ET * H])
        m.exs = sb("exs", [P, ET * H])
        m.h = [sb(f"h{u}", [P, GD]) for u in range(2)]
        m.hT = [sb(f"hT{u}", [P, GD]) for u in range(2)]
        m.st = sb("st", [P, 2 * G * 6])
        m.mv = sb("mv", [P, 2 * G * 2])
        m.ln = sb("ln", [P, 2 * 4 * G])
        m.PS = ctx.enter_context(nc.psum_tensor("PS", [P, 4096], F32))
        m.comps_b = sb("comps_b", [P, 2 * R * NB])
        m.wa = sb("wa", [P, 2 * 3 * H])
        m.we8 = sb("we8", [ED, H])
        m.emean = sb("emean", [ED, 1])
        m.amean = sb("amean", [H, 1])
        m.eaT = sb("eaT", [ED, 512])
        m.idx_s = [sb(f"idx_s{u}", [P, 8 * G], I32) for u in range(2)]
        m.gate_dve, m.gate_pe, m.gate_sp = sem("gate_dve"), sem("gate_pe"), sem("gate_sp")
        m.drow = m.big[:, 0:EP]
        wbig = Carve(m.big[:, EP:])
        m.wb = [wbig(2 * NB * D) for _ in range(2)]
        m.wr = [wbig(2 * D) for _ in range(2)]
        m.w1t, m.w2t = wbig(2 * D), wbig(2 * D)
        m.bd = wbig(2 * R * P)
        m.work = m.big[:, EP + wbig.at:]
        m.eq = [sb(f"eq{u}", [P, P]) for u in range(2)]
        m.carry = [sb(f"carry{u}", [P, P]) for u in range(2)]
        m.alpha = sb("alpha", [P, 2 * G * H])
        m.nmasks = sb("nmasks", [P, ET])
        m.idx_n = [sb(f"idx_n{g}", [P, G], I32) for g in range(NG)]
        m.idx_t = [sb(f"idx_t{u}", [P, G], I32) for u in range(2)]
        m.val_t = [sb(f"val_t{u}", [P, G], I32) for u in range(2)]
        m.recs = [m.h[j][:, 0:8 * ET].bitcast(I32) for j in range(2)]

        for one in (constants, sort_edges, small_weights, records, counts, records_by_src, logits,
                    softmax, weights, edge_layer0):
            with step(nc) as own:
                one(nc, own, m)
        for k in (1, 2, 3):
            with step(nc) as own:
                edge_layer(nc, own, m, k)
        for one in (nodes, sage):
            with step(nc) as own:
                one(nc, own, m)


_INS = ["x", "src", "dst", "edge_attr_64", "edge_type_8", "edge_weight", "L0_gnn_W",
        "L0_gnn_W_edge", "L0_gnn_att_src", "L0_gnn_att_dst", "L0_gnn_att_edge", "L0_gnn_bias",
        "L1_gnn_weight", "L2_gnn_comps", "L2_gnn_bases", "L2_gnn_roots", "L2_gnn_biases",
        "L3_gnn_W1", "L3_gnn_b1", "L3_gnn_W2", "L3_gnn_b2"]


def kernel(**inputs):
    import numpy as _np
    import concourse.bacc as _bacc
    from concourse import mybir as _mybir
    from concourse.bass_utils import run_bass_kernel_spmd as _run

    nc = _bacc.Bacc("TRN2", target_bir_lowering=False, num_devices=1)
    arrays, args = {}, []
    for name in _INS:
        a = _np.ascontiguousarray(inputs[name])
        arrays[f"in_{name}"] = a
        args.append(nc.dram_tensor(f"in_{name}", a.shape, _mybir.dt.from_np(a.dtype),
                                   kind="ExternalInput").ap())
    args.append(nc.dram_tensor("out_0", (N, D), F32, kind="ExternalOutput").ap())
    build(nc, *args)
    r = _run(nc, [arrays], core_ids=[0])
    return r.results[0]["out_0"]
```

```python
from contextlib import ExitStack, contextmanager

import concourse.bass as bass
from concourse import mybir

F32 = mybir.dt.float32
BF16 = mybir.dt.bfloat16
I32 = mybir.dt.int32
ALU = mybir.AluOpType
ACT = mybir.ActivationFunctionType
AX_X = mybir.AxisListType.X
ONE = 1
ds = bass.ds

P = 128
N, D, E = 20000, 256, 5000
H, C = 8, 32
R = 8
NB = 4
ED = 64
ET = -(-E // P)
EP = ET * P
EQ = E // ET
NQ = 125
G = 4
EG = ET // G
NT = N // P
REM = N - NT * P
NG = 4
NGRP = NT // G + 1
NI = NGRP // NG
HI = 160
PAD_KEY = 156 * 128 + 127
FAR = 1 << 20
EPS = 1e-5
BIG = 1e30
SLOPE = 0.2
GD = G * D
AW = D + H
TW = H + 3 * D
assert EQ * ET == E and EG % 2 == 0 and N % NQ == 0
assert NT % G == 0 and 0 < REM <= P and NGRP % NG == 0 and NG == 4


class Link:

    def __init__(self, eng, sem):
        self.eng, self.sem, self.base, self.i, self.per, self.c = eng, sem, 0, None, 0, 0

    def enter(self, i, per):
        self.i, self.per, self.c = i, per, 0

    def leave(self, times):
        assert self.c == self.per, ("increments of the loop's body", self.c, self.per)
        self.base, self.i, self.c = self.base + times * self.per, None, 0

    def mark(self, ins):
        ins.then_inc(self.sem, 1)
        if self.i is None:
            self.base += 1
            return self.base
        self.c += 1
        return self.i * self.per + (self.base + self.c)

    def until(self, value):
        self.eng.wait_ge(self.sem, value + ONE)

    def __call__(self, ins):
        self.until(self.mark(ins))


class Carve:

    def __init__(self, buf):
        self.buf, self.at = buf, 0

    def __call__(self, n):
        self.at += n
        return self.buf[:, self.at - n:self.at]


@contextmanager
def step(nc):
    mine = []

    def sem(name, start=ONE):
        mine.append(nc.alloc_semaphore(name=name))
        if start:
            nc.scalar.sem_inc(mine[-1], start)
        return mine[-1]

    yield sem
    nc.clear_and_free_semaphores(mine)
    nc.all_engine_barrier()


class Store:
    pass


def bc(ap, n):
    return ap.unsqueeze(2).to_broadcast([ap.shape[0], ap.shape[1], n])


def at_least(eng, sem, value):
    if not (isinstance(value, int) and value <= 0):
        eng.wait_ge(sem, value + ONE)


def each_group(eng, link, per, body):
    body(0, 0, 0, True, False)
    with eng.Fori(0, EG // 2 - 1) as i:
        if link is not None:
            link.enter(i, per)
        body(i * 2 + 1, 1, i, False, False)
        body(i * 2 + 2, 0, i + 1, False, False)
        if link is not None:
            link.leave(EG // 2 - 1)
    body(EG - 1, 1, EG // 2 - 1, False, True)


def constants(nc, sem, m):
    done = sem("const_done")
    nc.all_engine_barrier()
    with nc.Block() as block:
        @block.gpsimd
        def _(pool):
            link = Link(pool, done)
            pool.memset(m.ident[:, :], 0.0).then_inc(done, 1)
            pool.memset(m.ones[:, :], 1.0).then_inc(done, 1)
            pool.memset(m.onesf[:, :], 1.0).then_inc(done, 1)
            pool.memset(m.eps[:, :], EPS).then_inc(done, 1)
            pool.memset(m.e127[:, :], 0.0).then_inc(done, 1)
            pool.iota(m.iota[:, :], pattern=[[1, HI]], base=0, channel_multiplier=0,
                      allow_small_or_imprecise_dtypes=True).then_inc(done, 1)
            pool.iota(m.part[:, :], pattern=[[0, 1]], base=0, channel_multiplier=1,
                      allow_small_or_imprecise_dtypes=True).then_inc(done, 1)
            pool.wait_ge(done, 7 + ONE)
            link.base = 7
            link(pool.affine_select(out=m.ident[:, :], in_=m.ident[:, :], compare_op=ALU.not_equal,
                                    fill=1.0, base=0, pattern=[[-1, P]], channel_multiplier=1))
            link(pool.affine_select(out=m.tri[:, :], in_=m.onesf[:, :], compare_op=ALU.is_gt,
                                    fill=0.0, base=0, pattern=[[-1, P]], channel_multiplier=1))
            link(pool.affine_select(out=m.triu[:, :], in_=m.onesf[:, :], compare_op=ALU.is_gt,
                                    fill=0.0, base=0, pattern=[[1, P]], channel_multiplier=-1))
            link(pool.affine_select(out=m.e127[:, :], in_=m.e127[:, :], compare_op=ALU.not_equal,
                                    fill=1.0, base=1 - P, pattern=[[0, 1]], channel_multiplier=1))
            link(pool.tensor_copy(m.identb[:, :], m.ident[:, :]))


KEYS = (1, 0)


def drain(sp, landed, drained):
    with sp.Fori(0, EG // 2) as i:
        for u in range(2):
            sp.wait_ge(landed[u], i * (16 * G) + 16 * G)
            sp.sem_inc(drained[u], 1)


def scatter_group(pool, m, j, g, u, k, bufs, sent, staged, gate, rec_d):
    rank_s, rec_s = bufs
    pool.tensor_copy(rank_s[u], m.ranks[j][:, ds(g * G, G)]).then_inc(staged, 1)
    pool.tensor_copy(rec_s[u], m.recs[j][:, ds(g * (8 * G), 8 * G)]).then_inc(staged, 1)
    pool.wait_ge(staged, k * 2 + 2 + ONE)
    pool.sem_inc(gate, 1)
    for t in range(G):
        pool.indirect_dma_start(
            rec_d[:, :], bass.IndirectOffsetOnAxis(ap=rank_s[u][:, t:t + 1], axis=0),
            rec_s[u][:, 8 * t:8 * t + 8], None).then_inc(sent[u], 16)


def sort_edges(nc, sem, m):
    cut = Carve(m.xs)
    lin = cut(7 * ET).bitcast(I32)
    hilo_i = cut(4 * ET).bitcast(I32)
    keyf, hif, lof, before, inside, rank = ([cut(ET) for _ in range(2)] for _ in range(6))
    oh_loT = [cut(2 * P) for _ in range(2)]
    junk1, junk2 = [cut(P) for _ in range(2)], [cut(HI) for _ in range(2)]
    count, total, upto, table = cut(2 * HI), cut(2 * HI), cut(2 * HI), cut(2 * HI)
    zero = cut(HI // 2).bitcast(BF16)
    wide = Carve(m.big)
    keyrow = [wide(EP).bitcast(I32) for _ in range(2)]
    oh_hi = [wide(ET * HI // 2).bitcast(BF16) for _ in range(2)]
    widest = Carve(m.xh)
    oh_lo = [widest(ET * P // 2).bitcast(BF16) for _ in range(2)]
    psC = [m.PS[:, 0:HI], m.PS[:, 512:512 + HI]]
    psW, psX = m.PS[:, 1024:1024 + 2 * HI], m.PS[:, 1536:1536 + 2 * HI]
    psG = [m.PS[:, 512 * b:512 * b + 2 * HI] for b in (0, 1)]
    psN = [m.PS[:, 512 * b:512 * b + 2 * HI] for b in (4, 5)]
    psLT = [m.PS[:, b:b + P].bitcast(BF16) for b in (3072, 3584)]
    U = 8

    def of(buf, j):
        return buf[:, j * HI:(j + 1) * HI]

    def lo(t, j):
        return oh_lo[j][:, ds(t * P, P)]

    def hi(t, j):
        return oh_hi[j][:, ds(t * HI, HI)]

    cleared, loaded, numbered, keys_in = (sem("so_cleared"), sem("so_loaded"),
                                          sem("so_numbered"), sem("so_keys"))
    hot, counted, summed, split = sem("so_hot"), sem("so_counted"), sem("so_summed"), sem("so_split")
    turned, turned_out, next_in, looked = (sem("so_turned"), sem("so_turned_out"),
                                           sem("so_next"), sem("so_looked"))
    added, used, dve_own = sem("so_added"), sem("so_used"), sem("so_dve")
    nc.all_engine_barrier()
    with nc.Block() as block:
        @block.sync
        def _(sp):
            sp.wait_ge(cleared, 9 + ONE)
            for k, a in ((5, m.dst), (6, m.src), (0, m.src), (1, m.dst), (2, m.rel), (3, m.ew)):
                sp.dma_start(lin[0:EQ, k * ET:(k + 1) * ET],
                             a.rearrange("(p t) -> p t", t=ET).bitcast(I32)).then_inc(loaded, 16)
            for j, a in enumerate((m.dst, m.src)):
                sp.dma_start(keyrow[j][:, 0:E], a.partition_broadcast(P)).then_inc(keys_in, 16)
            sp.wait_ge(loaded, 96 + ONE)
            sp.wait_ge(keys_in, 32 + ONE)

        @block.gpsimd
        def _(pool):
            for k, v in ((5, PAD_KEY), (6, PAD_KEY), (0, 0), (1, 0), (2, 0), (3, 0)):
                pool.memset(lin[:, k * ET:(k + 1) * ET], v).then_inc(cleared, 1)
            pool.memset(zero, 0.0).then_inc(cleared, 1)
            for j in range(2):
                pool.memset(keyrow[j][:, E:EP], PAD_KEY).then_inc(cleared, 1)
            pool.iota(lin[:, 4 * ET:5 * ET], pattern=[[1, ET]], base=0,
                      channel_multiplier=ET).then_inc(numbered, 1)

        @block.vector
        def _(dve):
            link = Link(dve, dve_own)
            dve.wait_ge(loaded, 96 + ONE)
            dve.wait_ge(numbered, 1 + ONE)
            keys = lin[:, 5 * ET:7 * ET]
            dve.tensor_scalar(hilo_i[:, 0:2 * ET], keys, 7, None, ALU.arith_shift_right)
            link(dve.tensor_scalar(hilo_i[:, 2 * ET:], keys, P - 1, None, ALU.bitwise_and))
            for j in range(2):
                dve.tensor_copy(keyf[j], keys[:, j * ET:(j + 1) * ET])
                dve.tensor_copy(hif[j], hilo_i[:, j * ET:(j + 1) * ET])
                last = dve.tensor_copy(lof[j], hilo_i[:, (2 + j) * ET:(3 + j) * ET])
            link(last)
            with dve.Fori(0, ET // U) as i:
                for t in (i * U + v for v in range(U)):
                    for j in range(2):
                        dve.tensor_scalar(lo(t, j), m.iota[:, 0:P], lof[j][:, ds(t, 1)], None,
                                          ALU.is_equal)
                        last = dve.tensor_scalar(hi(t, j), m.iota[:, :], hif[j][:, ds(t, 1)], None,
                                                 ALU.is_equal)
                    last.then_inc(hot, 1)
            dve.wait_ge(counted, 1 + ONE)
            dve.tensor_copy(of(count, 0), psC[0])
            dve.tensor_copy(of(count, 1), psC[1]).then_inc(split, 1)
            dve.wait_ge(summed, 1 + ONE)
            link(dve.tensor_copy(total, psX))
            for j in range(2):
                last = dve.tensor_tensor_scan(of(upto, j), m.ones[:, 0:HI], of(total, j), 0.0,
                                              ALU.mult, ALU.add)
            link(last)
            link(dve.tensor_tensor(upto, upto, total, ALU.subtract))
            dve.tensor_tensor(table, upto, psW, ALU.add).then_inc(added, 1)
            dve.wait_ge(keys_in, 32 + ONE)
            with dve.Fori(0, ET // U) as i:
                for v in range(U):
                    t, u = i * U + v, v % 2
                    dve.wait_ge(looked, t + 1 + ONE)
                    dve.wait_ge(next_in, t + 1 + ONE)
                    dve.wait_ge(used, t + ONE)
                    dve.tensor_tensor(table, table, psN[u], ALU.add).then_inc(added, 1)
                    for j in range(2):
                        dve.scalar_tensor_tensor(
                            junk1[j], keyrow[j].rearrange("p (q t) -> p q t", t=ET)[:, :, ds(t, 1)]
                            .squeeze(2), keyf[j][:, ds(t, 1)], m.tri[:, :],
                            ALU.is_equal, ALU.mult, accum_out=inside[j][:, ds(t, 1)])
                    for j in range(2):
                        last = dve.scalar_tensor_tensor(
                            junk2[j], m.iota[:, :], hif[j][:, ds(t, 1)], of(psG[u], j),
                            ALU.is_equal, ALU.mult, accum_out=before[j][:, ds(t, 1)])
                    last.then_inc(used, 1)
            dve.wait_ge(used, ET + ONE)
            for j in range(2):
                link(dve.tensor_tensor(rank[j], before[j], inside[j], ALU.add))
                dve.tensor_copy(m.ranks[j], rank[j])
                rec3 = m.recs[j].rearrange("p (t c) -> p t c", c=8)
                for k in range(8):
                    c = 5 + j if k == KEYS[j] else k if k < 5 else 0
                    dve.tensor_copy(rec3[:, :, k], lin[:, c * ET:(c + 1) * ET])

        @block.scalar
        def _(act):
            with act.Fori(0, ET // U) as i:
                for v in range(U):
                    act.wait_ge(turned, i * U + (v + 1) + ONE)
                    if v > 1:
                        act.wait_ge(looked, i * U + (v - 1) + ONE)
                    act.activation(oh_loT[v % 2], psLT[v % 2], ACT.Copy).then_inc(turned_out, 1)
                act.wait_ge(looked, i * U + U + ONE)

        @block.tensor
        def _(pe):
            pe.wait_ge(cleared, 9 + ONE)
            pe.matmul(psC[0], zero[:, 0:P], zero, start=True, stop=False)
            pe.matmul(psC[1], zero[:, 0:P], zero, start=True, stop=False)
            with pe.Fori(0, ET // U) as i:
                for v in range(U):
                    t = i * U + v
                    pe.wait_ge(hot, t + 1 + ONE)
                    for j in range(2):
                        pe.matmul(psC[j], lo(t, j), hi(t, j), start=False, stop=False)
            pe.matmul(psC[0], zero[:, 0:P], zero, start=False, stop=True)
            pe.matmul(psC[1], zero[:, 0:P], zero, start=False, stop=True).then_inc(counted, 1)
            pe.wait_ge(split, 1 + ONE)
            pe.matmul(psW, m.triu[:, :], count, start=True, stop=True)
            pe.matmul(psX, m.onesf[:, :], count, start=True, stop=True).then_inc(summed, 1)
            with pe.Fori(0, ET // U) as i:
                for v in range(U):
                    t, u = i * U + v, v % 2
                    for j in range(2):
                        last = pe.transpose(psLT[u][:, j * P:(j + 1) * P], lo(t, j),
                                            m.identb[:, :])
                    last.then_inc(turned, 1)
                    for j in range(2):
                        last = pe.matmul(of(psN[u], j), lo(t, j), hi(t, j), start=True, stop=True)
                    last.then_inc(next_in, 1)
                    pe.wait_ge(turned_out, t + 1 + ONE)
                    pe.wait_ge(added, t + 1 + ONE)
                    for j in range(2):
                        last = pe.matmul(of(psG[u], j), oh_loT[u][:, j * P:(j + 1) * P],
                                         of(table, j), start=True, stop=True)
                    last.then_inc(looked, 1)


def records(nc, sem, m):
    cut = Carve(m.xs)
    lastc, far = cut(ET), cut(ET)
    clear = cut(N // NQ).bitcast(I32)
    row, prev, nxt = cut(2 * P), cut(P), cut(P)
    keep, last = cut(P), cut(P)
    ends = cut(4)
    psA, psL = m.PS[0:ET, 0:2 * P], m.PS[:, 512:512 + ET]
    srec3 = m.srec[:, :].rearrange("p (t c) -> p t c", c=8)
    loaded, filled, cleared, turned, rowed = (sem("re_loaded"), sem("re_filled"), sem("re_cleared"),
                                              sem("re_turned"), sem("re_rowed"))
    cols, wrote, back, flags, flipped = (sem("re_cols"), sem("re_wrote"), sem("re_back"),
                                         sem("re_flags"), sem("re_flipped"))
    kept, dve_own = sem("re_kept"), sem("re_dve")
    nc.all_engine_barrier()
    with nc.Block() as block:
        @block.sync
        def _(sp):
            sp.dma_start(srec3, m.rec_d.rearrange("(t q) c -> q t c", q=P)).then_inc(loaded, 16)
            sp.wait_ge(filled, 4 + ONE)
            sp.dma_start(m.pos_d.rearrange("(p t) c -> p (t c)", p=NQ), clear[0:NQ, :])\
                .then_inc(cleared, 16)
            sp.dma_start(m.row_d[0:1, 0:1], ends[0:1, 0:1]).then_inc(wrote, 16)
            sp.dma_start(m.row_d[0:1, EP + 1:EP + 2], ends[0:1, 1:2]).then_inc(wrote, 16)
            sp.dma_start(m.row_d[2:3, EP:EP + 1], ends[0:1, 2:3]).then_inc(wrote, 16)
            sp.wait_ge(rowed, 1 + ONE)
            sp.dma_start(m.row_d[0, 1:EP + 1].rearrange("(t q) -> t q", q=P), row[0:ET, 0:P])\
                .then_inc(wrote, 16)
            sp.dma_start(m.row_d[1, 0:EP].rearrange("(t q) -> t q", q=P), row[0:ET, P:2 * P])\
                .then_inc(wrote, 16)
            sp.wait_ge(wrote, 80 + ONE)
            sp.dma_start(prev[0:ET, :], m.row_d[0, 0:EP].rearrange("(t q) -> t q", q=P))\
                .then_inc(back, 16)
            sp.dma_start(nxt[0:ET, :], m.row_d[0, 2:EP + 2].rearrange("(t q) -> t q", q=P))\
                .then_inc(back, 16)
            sp.wait_ge(flags, 1 + ONE)
            sp.dma_start(m.row_d[2, 0:EP].rearrange("(t q) -> t q", q=P), keep[0:ET, :])\
                .then_inc(kept, 16)
            sp.wait_ge(kept, 16 + ONE)
            sp.wait_ge(cleared, 16 + ONE)

        @block.gpsimd
        def _(pool):
            pool.memset(clear, FAR).then_inc(filled, 1)
            pool.memset(m.posn[:, :], FAR).then_inc(filled, 1)
            pool.memset(ends[:, 0:2], -5.0).then_inc(filled, 1)
            pool.memset(ends[:, 2:4], 0.0).then_inc(filled, 1)
            pool.iota(m.place[:, :], pattern=[[P, ET]], base=0, channel_multiplier=1).then_inc(filled, 1)

        @block.vector
        def _(dve):
            link = Link(dve, dve_own)
            dve.wait_ge(loaded, 16 + ONE)
            dve.memset(m.dstc[:, 0:1], -5.0)
            dve.tensor_copy(m.dstc[:, 1:ET + 1], srec3[:, :, 1])
            dve.tensor_copy(m.relc[:, :], srec3[:, :, 2]).then_inc(cols, 1)
            dve.wait_ge(back, 32 + ONE)
            dve.tensor_tensor(keep[0:ET, :], row[0:ET, 0:P], prev[0:ET, :], ALU.is_equal)
            dve.tensor_tensor(last[0:ET, :], row[0:ET, 0:P], nxt[0:ET, :], ALU.not_equal)\
                .then_inc(flags, 1)
            dve.wait_ge(flipped, 1 + ONE)
            link(dve.tensor_copy(lastc, psL))
            link(dve.tensor_scalar(far, lastc, -float(FAR), float(FAR), ALU.mult, ALU.add))
            link(dve.tensor_tensor(lastc, lastc, m.dstc[:, 1:ET + 1], ALU.mult))
            link(dve.tensor_tensor(lastc, lastc, far, ALU.add))
            dve.tensor_copy(m.posidx[:, :], lastc)

        @block.scalar
        def _(act):
            act.wait_ge(turned, 1 + ONE)
            act.activation(row[0:ET, :], psA, ACT.Copy).then_inc(rowed, 1)

        @block.tensor
        def _(pe):
            pe.wait_ge(cols, 1 + ONE)
            pe.transpose(psA[:, 0:P], m.dstc[:, 1:ET + 1], m.ident[:, :])
            pe.transpose(psA[:, P:2 * P], m.relc[:, :], m.ident[:, :]).then_inc(turned, 1)
            pe.wait_ge(flags, 1 + ONE)
            pe.transpose(psL, last[0:ET, :], m.ident[0:ET, 0:ET]).then_inc(flipped, 1)


def records_by_src(nc, sem, m):
    cut = Carve(m.xs)
    lastc, far = cut(ET), cut(ET)
    row, nxt, last, ends = cut(P), cut(P), cut(P), cut(4)
    psA, psL = m.PS[0:ET, 0:P], m.PS[:, 512:512 + ET]
    loaded, cleared, cols, turned, rowed = (sem("rs_loaded"), sem("rs_cleared"), sem("rs_cols"),
                                            sem("rs_turned"), sem("rs_rowed"))
    wrote, back, flags, flipped, dve_own = (sem("rs_wrote"), sem("rs_back"), sem("rs_flags"),
                                            sem("rs_flipped"), sem("rs_dve"))
    srec3 = m.srec2[:, :].rearrange("p (t c) -> p t c", c=8)
    nc.all_engine_barrier()
    with nc.Block() as block:
        @block.gpsimd
        def _(pool):
            pool.memset(ends, -5.0).then_inc(cleared, 1)

        @block.sync
        def _(sp):
            sp.dma_start(srec3, m.rec2_d.rearrange("(t q) c -> q t c", q=P)).then_inc(loaded, 16)
            sp.wait_ge(cleared, 1 + ONE)
            sp.dma_start(m.row2_d[0:1, EP:EP + 1], ends[0:1, 0:1]).then_inc(wrote, 16)
            sp.wait_ge(rowed, 1 + ONE)
            sp.dma_start(m.row2_d[0, 0:EP].rearrange("(t q) -> t q", q=P), row[0:ET, :])\
                .then_inc(wrote, 16)
            sp.wait_ge(wrote, 32 + ONE)
            sp.dma_start(nxt[0:ET, :], m.row2_d[0, 1:EP + 1].rearrange("(t q) -> t q", q=P))\
                .then_inc(back, 16)
            sp.wait_ge(back, 16 + ONE)

        @block.vector
        def _(dve):
            link = Link(dve, dve_own)
            dve.wait_ge(loaded, 16 + ONE)
            dve.memset(m.srcc[:, 0:1], -5.0)
            dve.tensor_copy(m.srcc[:, 1:ET + 1], srec3[:, :, 0]).then_inc(cols, 1)
            dve.wait_ge(back, 16 + ONE)
            dve.tensor_tensor(last[0:ET, :], row[0:ET, :], nxt[0:ET, :], ALU.not_equal)\
                .then_inc(flags, 1)
            dve.wait_ge(flipped, 1 + ONE)
            link(dve.tensor_copy(lastc, psL))
            link(dve.tensor_scalar(far, lastc, -float(FAR), float(FAR), ALU.mult, ALU.add))
            link(dve.tensor_tensor(lastc, lastc, m.srcc[:, 1:ET + 1], ALU.mult))
            link(dve.tensor_tensor(lastc, lastc, far, ALU.add))
            dve.tensor_copy(m.to_node[:, :], lastc)

        @block.scalar
        def _(act):
            act.wait_ge(turned, 1 + ONE)
            act.activation(row[0:ET, :], psA, ACT.Copy).then_inc(rowed, 1)

        @block.tensor
        def _(pe):
            pe.wait_ge(cols, 1 + ONE)
            pe.transpose(psA, m.srcc[:, 1:ET + 1], m.ident[:, :]).then_inc(turned, 1)
            pe.wait_ge(flags, 1 + ONE)
            pe.transpose(psL, last[0:ET, :], m.ident[0:ET, 0:ET]).then_inc(flipped, 1)


def small_weights(nc, sem, m):
    cut = Carve(m.xs)
    att = [cut(D) for _ in range(3)]
    we, tmp, eas, b2_b = cut(D), cut(2 * D), cut(ED), cut(D)
    ea_all = m.xh[0:EQ, 0:ET * ED]
    meane = m.PS[0:ED, 0:1]
    loaded, eas_in, rowsum, summed, mean, drawn, dve_own = (
        sem("sw_loaded"), sem("sw_eas_in"), sem("sw_rowsum"), sem("sw_summed"), sem("sw_mean"),
        sem("sw_drawn"), sem("sw_dve"))
    staged, gate, sent = sem("sw_staged"), sem("sw_gate"), [sem(f"sw_sent{u}", 0) for u in range(2)]
    drained = [sem(f"sw_drained{u}") for u in range(2)]
    stage = Carve(m.hT[0])
    bufs = ([stage(G).bitcast(I32) for _ in range(2)], [stage(8 * G).bitcast(I32) for _ in range(2)])
    nc.all_engine_barrier()
    with nc.Block() as block:
        @block.gpsimd
        def _(pool):
            with pool.Fori(0, EG // 2) as i:
                for u in range(2):
                    pool.wait_ge(drained[u], i + ONE)
                    scatter_group(pool, m, 0, i * 2 + u, u, i * 2 + u, bufs, sent, staged, gate,
                                  m.rec_d)
            for u in range(2):
                pool.wait_ge(sent[u], EG // 2 * 16 * G)

        @block.sync
        def _(sp):
            sp.dma_start(ea_all, m.ea.rearrange("(p t) c -> p (t c)", t=ET)).then_inc(eas_in, 16)
            sp.dma_start(m.w0[:, :].rearrange("p (k n) -> p k n", k=2),
                         m.W0.rearrange("(k p) n -> p k n", p=P)).then_inc(loaded, 16)
            sp.dma_start(we[0:ED, :], m.Wedge).then_inc(loaded, 16)
            for a, dest in ((m.att_src, att[0]), (m.att_dst, att[1]), (m.att_edge, att[2])):
                sp.dma_start(dest, a.rearrange("h c -> (h c)").partition_broadcast(P))\
                    .then_inc(loaded, 16)
            sp.dma_start(m.bias0_b, m.bias0.partition_broadcast(P)).then_inc(loaded, 16)
            sp.dma_start(m.bias1_b, m.biases[1, :].partition_broadcast(P)).then_inc(loaded, 16)
            sp.dma_start(m.b12_b[:, :], m.b1.partition_broadcast(P)).then_inc(loaded, 16)
            sp.dma_start(b2_b, m.b2.partition_broadcast(P)).then_inc(loaded, 16)
            sp.dma_start(m.comps_b[:, :],
                         m.comps[0:2].rearrange("l r b -> (l r b)").partition_broadcast(P))\
                .then_inc(loaded, 16)
            for k in range(2):
                sp.dma_start(m.b0col[:, k:k + 1], m.biases[0, k * P:(k + 1) * P].unsqueeze(1))\
                    .then_inc(loaded, 16)
            drain(sp, sent, drained)
            sp.wait_ge(loaded, 192 + ONE)
            sp.wait_ge(eas_in, 16 + ONE)

        @block.vector
        def _(dve):
            link = Link(dve, dve_own)
            dve.wait_ge(eas_in, 16 + ONE)
            dve.tensor_reduce(eas[0:EQ, :], ea_all.rearrange("p (t c) -> p c t", c=ED), AX_X,
                              ALU.add).then_inc(rowsum, 1)
            dve.wait_ge(loaded, 192 + ONE)
            for j in range(2):
                for k in range(2):
                    link(dve.tensor_tensor(tmp[:, k * D:(k + 1) * D], m.w0[:, k * D:(k + 1) * D],
                                           att[j], ALU.mult))
                for k in range(2):
                    link(dve.tensor_reduce(m.wa[:, k * 3 * H + j * H:k * 3 * H + (j + 1) * H],
                                           tmp[:, k * D:(k + 1) * D].rearrange(
                                               "p (h c) -> p h c", c=C), AX_X, ALU.add))
            for k in range(2):
                o = k * 3 * H
                dve.tensor_tensor(m.wa[:, o + 2 * H:o + 3 * H], m.wa[:, o:o + H],
                                  m.wa[:, o + H:o + 2 * H], ALU.add)
            dve.tensor_tensor(m.b12_b[:, :], m.b12_b[:, :], b2_b, ALU.add)
            dve.memset(m.pre[:, 0:H], 1.0)
            dve.memset(m.pre[:, H + D:H + 2 * D], 0.0)
            link(dve.tensor_tensor(tmp[0:ED, 0:D], we[0:ED, :], att[2][0:ED, :], ALU.mult))
            link(dve.tensor_reduce(m.we8[:, :], tmp[0:ED, 0:D].rearrange("p (h c) -> p h c", c=C),
                                   AX_X, ALU.add))
            dve.wait_ge(summed, 1 + ONE)
            dve.tensor_scalar(m.emean[:, :], meane, 1.0 / E, None, ALU.mult).then_inc(mean, 1)
            dve.wait_ge(drawn, 1 + ONE)
            dve.tensor_copy(m.amean[:, :], m.PS[0:H, 512:513])

        @block.tensor
        def _(pe):
            pe.wait_ge(rowsum, 1 + ONE)
            pe.matmul(meane, eas[0:EQ, :], m.onesf[0:EQ, 0:1], start=True, stop=True)\
                .then_inc(summed, 1)
            pe.wait_ge(mean, 1 + ONE)
            pe.matmul(m.PS[0:H, 512:513], m.we8[:, :], m.emean[:, :], start=True, stop=True)\
                .then_inc(drawn, 1)


def to_edge_major(dve, link, heads, scratch, out):
    link(dve.transpose(scratch[0:32, :], heads[0:32, :]))
    blocks = scratch[0:32, :].rearrange("p (t j c) -> p t j c", j=4, c=32)
    for j in range(4):
        last = dve.tensor_copy(out[32 * j:32 * j + 32, :].rearrange("p (t c) -> p t c", c=8),
                               blocks[:, :, j, 0:8])
    link(last)


def counts(nc, sem, m):
    sA, sL, sF, sK = (m.big[:, k * EP:(k + 1) * EP] for k in range(4))
    keep_next = m.big[0:R, 3 * EP + 1:4 * EP + 1]
    cut = Carve(m.xs)
    cnt, oh, tmp, sel, w = cut(ET * R), cut(ET * R), cut(ET * R), cut(ET), cut(ET)
    cleared, keeps, rels, dve_own = sem("co_cleared"), sem("co_keeps"), sem("co_rels"), sem("co_dve")

    def by8(ap):
        return ap.rearrange("p (t r) -> p t r", r=R)

    nc.all_engine_barrier()
    with nc.Block() as block:
        @block.gpsimd
        def _(pool):
            pool.memset(sL[0:32, :], 0.0).then_inc(cleared, 1)
            pool.memset(sA[0:32, :], 0.0).then_inc(cleared, 1)

        @block.sync
        def _(sp):
            sp.dma_start(m.big[0:R, 3 * EP:4 * EP + 1],
                         m.row_d[2, 0:EP + 1].partition_broadcast(R)).then_inc(keeps, 16)
            sp.wait_ge(cleared, 1 + ONE)
            sp.dma_start(sL[0:R, :], m.row_d[1, 0:EP].partition_broadcast(R)).then_inc(rels, 16)
            sp.wait_ge(rels, 16 + ONE)
            sp.wait_ge(keeps, 16 + ONE)

        @block.vector
        def _(dve):
            link = Link(dve, dve_own)
            dve.wait_ge(rels, 16 + ONE)
            dve.wait_ge(cleared, 2 + ONE)
            link(dve.tensor_scalar(sA[0:R, :], sL[0:R, :], m.part[0:R, :], None, ALU.is_equal))
            dve.wait_ge(keeps, 16 + ONE)
            link(dve.tensor_tensor_scan(sF[0:R, :], sK[0:R, :], sA[0:R, :], 0.0, ALU.mult, ALU.add))
            link(dve.tensor_tensor_scan(sA[0:R, ::-1], keep_next[:, ::-1], sF[0:R, ::-1], 0.0,
                                        ALU.mult, ALU.max))
            to_edge_major(dve, link, sA, sF, cnt)
            dve.tensor_scalar(m.big[0:R, 3 * EP:4 * EP + 1], m.big[0:R, 3 * EP:4 * EP + 1], -1.0,
                              BIG, ALU.add, ALU.mult)
            dve.tensor_copy(w, m.srec[:, :].bitcast(F32).rearrange("p (t c) -> p t c", c=8)[:, :, 3])
            link(dve.tensor_tensor(by8(oh), m.iota[:, 0:R].unsqueeze(1).to_broadcast([P, ET, R]),
                                   bc(m.relc[:, :], R), ALU.is_equal))
            dve.tensor_tensor(by8(m.co1[:, :]), by8(oh), bc(w, R), ALU.mult)
            link(dve.tensor_tensor(tmp, oh, cnt, ALU.mult))
            link(dve.tensor_reduce(sel, by8(tmp), AX_X, ALU.add))
            link(dve.tensor_scalar(sel, sel, 1.0, None, ALU.max))
            link(dve.reciprocal(sel, sel))
            for l in range(2):
                for b in range(NB):
                    comp = m.comps_b[:, l * R * NB:(l + 1) * R * NB].rearrange(
                        "p (r b) -> p b r", b=NB)[:, b:b + 1, :].to_broadcast([P, ET, R])
                    link(dve.tensor_tensor(by8(tmp), by8(oh), comp, ALU.mult))
                    col = m.co2[l][:, :].rearrange("p (t b) -> p t b", b=NB)[:, :, b:b + 1]
                    link(dve.tensor_reduce(col, by8(tmp), AX_X, ALU.add))
                    link(dve.tensor_tensor(col, col, sel.unsqueeze(2), ALU.mult))


def ln_stats(dve, link, m, rows, u, done):
    n = len(rows)
    for t, r in enumerate(rows):
        last = dve.bn_stats(m.st[:, (u * G + t) * 6:(u * G + t + 1) * 6], r)
    link(last)
    dve.sem_inc(m.gate_dve, 1)
    for t in range(n):
        last = dve.bn_aggr(m.mv[:, (u * G + t) * 2:(u * G + t + 1) * 2],
                           m.st[:, (u * G + t) * 6:(u * G + t + 1) * 6])
    last.then_inc(done, 1)


def ln_parts(m, u, n):
    mv = m.mv[:, u * G * 2:(u * G + n) * 2].rearrange("p (t c) -> p t c", c=2)
    s = [m.ln[:, (u * 4 + k) * G:(u * 4 + k) * G + n] for k in range(4)]
    return mv[:, :, 0], mv[:, :, 1], s


def ln_scales(dve, link, m, u, n, done):
    mean, var, (std, nmr, a, r) = ln_parts(m, u, n)
    link(dve.reciprocal(r, std))
    link(dve.scalar_tensor_tensor(a, var, EPS, r, ALU.add, ALU.mult))
    link(dve.scalar_tensor_tensor(a, a, -0.5, r, ALU.mult, ALU.mult))
    link(dve.scalar_tensor_tensor(std, a, 1.5, r, ALU.add, ALU.mult))
    dve.scalar_tensor_tensor(nmr, mean, -1.0, std, ALU.mult, ALU.mult).then_inc(done, 1)


def ln_apply(act, m, rows, u, h, done):
    _, _, (rstd, nmr, _, _) = ln_parts(m, u, len(rows))
    for t, r in enumerate(rows):
        last = act.activation(h[:, t * D:(t + 1) * D], r, ACT.Relu, scale=rstd[:, t:t + 1],
                              bias=nmr[:, t:t + 1])
    last.then_inc(done, 1)


def turn(pe, m, h, ps, n, done):
    for k in range(2):
        for t in range(n):
            last = pe.transpose(ps[:, k * 512 + t * P:k * 512 + (t + 1) * P],
                                h[:, t * D + k * P:t * D + (k + 1) * P], m.ident[:, :])
    last.then_inc(done, 1)


def logits(nc, sem, m):
    sA, sL, sF, _ = (m.big[:, k * EP:(k + 1) * EP] for k in range(4))
    cut = Carve(sF)
    gs, gd, ge = ([cut(GD) for _ in range(2)], [cut(GD) for _ in range(2)],
                  [cut(G * ED) for _ in range(2)])
    psE, psA, psZ = m.PS[0:ED, 1024:1536], m.PS[0:H, 1536:2048], m.PS[0:H, 2048:2560]
    psY = [m.PS[:, 3072:3584], m.PS[:, 3584:4096]]
    blank, staged, gate = sem("lo_blank"), sem("lo_staged"), sem("lo_gate")
    src_in, dst_in, ea_in = ([sem(f"lo_{k}_in{u}", 0) for u in range(2)] for k in ("src", "dst", "ea"))
    stats, std, scales, hs = (sem("lo_stats"), sem("lo_std"), sem("lo_scales"), sem("lo_h"))
    kept, eturn = ([sem(f"lo_{k}{u}") for u in range(2)] for k in ("kept", "eturn"))
    turned, tout, eout = sem("lo_turned"), sem("lo_tout"), sem("lo_eout")
    prods, pout, logit, lout, dve_own = (sem("lo_prods"), sem("lo_pout"), sem("lo_logit"),
                                         sem("lo_lout"), sem("lo_dve"))

    def tiles(buf):
        return [buf[:, t * D:(t + 1) * D] for t in range(G)]

    nc.all_engine_barrier()
    with nc.Block() as block:
        @block.gpsimd
        def _(pool):
            for b in (*gs, *gd, *ge):
                pool.memset(b, 0.0).then_inc(blank, 1)
            pool.wait_ge(blank, 6 + ONE)
            bx, be = pool.to_reg(N - 1), pool.to_reg(E - 1)
            with pool.Fori(0, EG // 2) as i:
                for u in range(2):
                    g = i * 2 + u
                    pool.wait_ge(kept[u], i + ONE)
                    pool.wait_ge(eturn[u], i + ONE)
                    pool.sem_inc(gate, 1)
                    pool.tensor_copy(m.idx_s[u][:, :], m.srec[:, ds(g * (8 * G), 8 * G)])\
                        .then_inc(staged, 1)
                    pool.wait_ge(staged, g + 1 + ONE)
                    pool.sem_inc(gate, 1)
                    for buf, table, c, bound, came in (
                            (gs, m.x, 0, bx, src_in), (gd, m.x, 1, bx, dst_in),
                            (ge, m.ea, 4, be, ea_in)):
                        w = ED if buf is ge else D
                        for t in range(G):
                            row = bass.IndirectOffsetOnAxis(
                                ap=m.idx_s[u][:, 8 * t + c:8 * t + c + 1], axis=0)
                            pool.indirect_dma_start(buf[u][:, t * w:(t + 1) * w], None,
                                                    table[:, :], row, bounds_check=bound,
                                                    oob_is_err=False).then_inc(came[u], 16)

        @block.vector
        def _(dve):
            link = Link(dve, dve_own)

            def measure(g, u, n):
                for part, (buf, came) in enumerate(((gs, src_in), (gd, dst_in))):
                    dve.wait_ge(came[u], n * (16 * G) + 16 * G)
                    at_least(dve, hs, g * 2)
                    ln_stats(dve, link, m, tiles(buf[u]), part, stats)

            def scale(g, u):
                for part in range(2):
                    dve.wait_ge(std, g * 2 + (part + 1) + ONE)
                    ln_scales(dve, link, m, part, G, scales)
                dve.tensor_tensor(
                    m.xs[:, ds(g * GD, GD)].rearrange("p (t d) -> p t d", t=G),
                    gs[u].rearrange("p (t d) -> p t d", t=G),
                    m.bias0_b.unsqueeze(1).to_broadcast([P, G, D]), ALU.add).then_inc(kept[u], 1)

            def body(g, u, n, first, last):
                if not last:
                    measure(g + 1, 1 - u, n + u)
                for b in range(2):
                    dve.wait_ge(prods, g * 2 + (b + 1) + ONE)
                    dve.tensor_copy(m.xh[:, ds(g * GD + b * 2 * D, 2 * D)], psY[b])\
                        .then_inc(pout, 1)
                if not last:
                    scale(g + 1, 1 - u)

            measure(0, 0, 0)
            scale(0, 0)
            each_group(dve, link, 20, body)

        @block.scalar
        def _(act):
            def normal(g, u):
                for part in range(2):
                    _, var, s = ln_parts(m, part, G)
                    act.wait_ge(stats, g * 2 + (part + 1) + ONE)
                    act.activation(s[0], var, ACT.Sqrt, bias=m.eps[:, :]).then_inc(std, 1)
                for part, buf in enumerate((gs, gd)):
                    act.wait_ge(scales, g * 2 + (part + 1) + ONE)
                    at_least(act, turned, g * 2)
                    ln_apply(act, m, tiles(buf[u]), part, m.h[part], hs)

            def body(g, u, n, first, last):
                for part in range(2):
                    act.wait_ge(turned, g * 2 + (part + 1) + ONE)
                    at_least(act, logit, g)
                    act.activation(m.hT[part][:, :], m.PS[:, 0:1024], ACT.Copy).then_inc(tout, 1)
                act.wait_ge(eturn[u], n + 1 + ONE)
                act.activation(m.eaT[:, :], psE, ACT.Copy).then_inc(eout, 1)
                if not last:
                    normal(g + 1, 1 - u)
                act.wait_ge(logit, g + 1 + ONE)
                act.activation(sA[0:H, ds(g * 512, 512)], psA, ACT.Copy)
                act.activation(sL[0:H, ds(g * 512, 512)], psZ, ACT.Identity,
                               bias=m.amean[:, :]).then_inc(lout, 1)

            normal(0, 0)
            each_group(act, None, 0, body)

        @block.tensor
        def _(pe):
            with pe.Fori(0, EG // 2) as i:
                for u in range(2):
                    g = i * 2 + u
                    for part in range(2):
                        pe.wait_ge(hs, g * 2 + (part + 1) + ONE)
                        pe.wait_ge(tout, g * 2 + part + ONE)
                        turn(pe, m, m.h[part], m.PS[:, 0:1024], G, turned)
                    pe.wait_ge(ea_in[u], i * (16 * G) + 16 * G)
                    pe.wait_ge(eout, g + ONE)
                    pe.sem_inc(m.gate_pe, 1)
                    for t in range(G):
                        last = pe.transpose(psE[:, t * P:(t + 1) * P],
                                            ge[u][:, t * ED:(t + 1) * ED], m.ident[:, :])
                    last.then_inc(eturn[u], 1)
                    pe.wait_ge(tout, g * 2 + 1 + ONE)
                    for b in range(2):
                        pe.wait_ge(pout, g * 2 + b + ONE)
                        for t in (2 * b, 2 * b + 1):
                            for k in range(2):
                                last = pe.matmul(psY[b][:, (t % 2) * D:(t % 2 + 1) * D],
                                                 m.hT[0][:, k * 512 + t * P:k * 512 + (t + 1) * P],
                                                 m.w0[:, k * D:(k + 1) * D],
                                                 start=(k == 0), stop=(k == 1))
                        last.then_inc(prods, 1)
                    pe.wait_ge(lout, g + ONE)
                    pe.wait_ge(tout, g * 2 + 2 + ONE)
                    pe.wait_ge(eout, g + 1 + ONE)
                    for k in range(2):
                        o = k * 3 * H
                        pe.matmul(psA, m.wa[:, o:o + H], m.hT[0][:, k * 512:(k + 1) * 512],
                                  start=(k == 0), stop=False)
                        pe.matmul(psA, m.wa[:, o + H:o + 2 * H], m.hT[1][:, k * 512:(k + 1) * 512],
                                  start=False, stop=False)
                        pe.matmul(psZ, m.wa[:, o + 2 * H:o + 3 * H],
                                  m.hT[1][:, k * 512:(k + 1) * 512], start=(k == 0), stop=(k == 1))
                    pe.matmul(psA, m.we8[:, :], m.eaT[:, :], start=False, stop=True)\
                        .then_inc(logit, 1)


def softmax(nc, sem, m):
    sA, sL, sF, sK = (m.big[0:H, k * EP:(k + 1) * EP] for k in range(4))
    new_next = m.big[0:H, 3 * EP + 1:4 * EP + 1]
    idx_s, val_s = m.idx_t, m.val_t
    staged, gate, posted = sem("sm_staged"), sem("sm_gate"), [sem(f"sm_posted{u}", 0) for u in range(2)]
    drained = [sem(f"sm_drained{u}") for u in range(2)]
    sub, exps, dve_own = sem("sm_sub"), sem("sm_exp"), sem("sm_dve")
    nc.all_engine_barrier()
    with nc.Block() as block:
        @block.sync
        def _(sp):
            drain(sp, posted, drained)

        @block.gpsimd
        def _(pool):
            bound = pool.to_reg(N - 1)
            with pool.Fori(0, EG // 2) as i:
                for u in range(2):
                    pool.wait_ge(drained[u], i + ONE)
                    pool.tensor_copy(idx_s[u][:, :], m.posidx[:, ds((i * 2 + u) * G, G)])\
                        .then_inc(staged, 1)
                    pool.tensor_copy(val_s[u][:, :], m.place[:, ds((i * 2 + u) * G, G)])\
                        .then_inc(staged, 1)
                    pool.wait_ge(staged, i * 4 + (2 * u + 2) + ONE)
                    pool.sem_inc(gate, 1)
                    for t in range(G):
                        pool.indirect_dma_start(
                            m.pos_d[:, :],
                            bass.IndirectOffsetOnAxis(ap=idx_s[u][:, t:t + 1], axis=0),
                            val_s[u][:, t:t + 1], None, bounds_check=bound,
                            oob_is_err=False).then_inc(posted[u], 16)
            for u in range(2):
                pool.wait_ge(posted[u], EG // 2 * 16 * G)

        @block.vector
        def _(dve):
            link = Link(dve, dve_own)
            dve.scalar_tensor_tensor(sA, sA, SLOPE, sA, ALU.mult, ALU.max)
            link(dve.scalar_tensor_tensor(sL, sL, SLOPE, sL, ALU.mult, ALU.max))
            link(dve.tensor_tensor(sF, sA, sL, ALU.max))
            link(dve.tensor_tensor_scan(sF, sK, sF, -BIG, ALU.add, ALU.max))
            link(dve.tensor_tensor_scan(sF[:, ::-1], new_next[:, ::-1], sF[:, ::-1], -BIG,
                                        ALU.add, ALU.max))
            dve.tensor_tensor(sA, sA, sF, ALU.subtract).then_inc(sub, 1)
            dve.tensor_tensor(sL, sL, sF, ALU.subtract).then_inc(sub, 1)
            full = [m.big[:, k * EP:(k + 1) * EP] for k in range(3)]
            dve.wait_ge(sub, 2 + ONE)
            dve.wait_ge(exps, 1 + ONE)
            to_edge_major(dve, link, full[0], full[2], m.ex)
            dve.wait_ge(exps, 2 + ONE)
            to_edge_major(dve, link, full[1], full[2], m.exs)

        @block.scalar
        def _(act):
            for k, s in enumerate((sA, sL)):
                act.wait_ge(sub, k + 1 + ONE)
                act.activation(s, s, ACT.Exp).then_inc(exps, 1)


def weights(nc, sem, m):
    raw = m.h[0], m.h[1]
    loaded, raws, cleared, turned = (sem("we_loaded"), sem("we_raws"), sem("we_cleared"),
                                     sem("we_turned"))
    nc.all_engine_barrier()
    with nc.Block() as block:
        @block.gpsimd
        def _(pool):
            pool.memset(m.bd, 0.0).then_inc(cleared, 1)

        @block.sync
        def _(sp):
            for n, w in enumerate((m.W1, m.W2)):
                sp.dma_start(raw[n][:, 0:2 * D].rearrange("p (j c) -> p j c", j=2),
                             w.rearrange("(j p) c -> p j c", p=P)).then_inc(raws, 16)
            sp.dma_start(m.drow, m.row_d[0, 1:EP + 1].partition_broadcast(P)).then_inc(loaded, 16)
            for l in range(2):
                for k in range(2):
                    sp.dma_start(m.wb[l][:, k * NB * D:(k + 1) * NB * D].rearrange(
                        "p (b o) -> p b o", b=NB),
                        m.bases[l, :, k * P:(k + 1) * P, :].rearrange("b p o -> p b o"))\
                        .then_inc(loaded, 16)
                sp.dma_start(m.wr[l].rearrange("p (k o) -> p k o", k=2),
                             m.roots[l].rearrange("(k p) o -> p k o", p=P)).then_inc(loaded, 16)
            sp.wait_ge(cleared, 1 + ONE)
            for k in range(2):
                for j in range(4):
                    b = 4 * k + j
                    sp.dma_start(
                        m.bd[C * j:C * (j + 1), k * R * P:(k + 1) * R * P].rearrange(
                            "i (r o) -> i r o", r=R)[:, :, C * j:C * (j + 1)],
                        m.L1w[:, b * C * C:(b + 1) * C * C].rearrange("r (i o) -> i r o", i=C))\
                        .then_inc(loaded, 16)
            sp.wait_ge(loaded, 16 * 15 + ONE)

        @block.tensor
        def _(pe):
            pe.wait_ge(raws, 32 + ONE)
            for n in range(2):
                for k in range(2):
                    for j in range(2):
                        last = pe.transpose(
                            m.PS[:, (n * 2 + k) * D + j * P:(n * 2 + k) * D + (j + 1) * P],
                            raw[n][:, j * D + k * P:j * D + (k + 1) * P], m.ident[:, :])
            last.then_inc(turned, 1)

        @block.vector
        def _(dve):
            dve.wait_ge(turned, 1 + ONE)
            dve.tensor_copy(m.w1t, m.PS[:, 0:2 * D])
            dve.tensor_copy(m.w2t, m.PS[:, 2 * D:4 * D])


def equality(dve, m, row, col, tau, s, done):
    dve.tensor_scalar(m.eq[s][:, :], row[:, ds(tau * P, P)], col[:, ds(tau + 1, 1)], None,
                      ALU.is_equal)
    dve.tensor_scalar(m.carry[s][96:P, :], row[96:P, ds(tau * P, P)], col[96:P, ds(tau, 1)],
                      m.e127[96:P, :], ALU.is_equal, ALU.mult).then_inc(done, 1)


def edge_layer0(nc, sem, m):
    cut = Carve(m.work)
    msg = [cut(AW) for _ in range(2)]
    o = [cut(G * AW) for _ in range(2)]
    nrm = [cut(G * AW) for _ in range(2)]
    z = cut(2 * G * H)
    pss = [m.PS[:, 3072:3072 + AW], m.PS[:, 3584:3584 + AW]]
    made, summed, out_of, normed = sem("l0_made"), sem("l0_summed"), sem("l0_out"), sem("l0_norm")
    zeroed, dve_own = sem("l0_zeroed"), sem("l0_dve")
    stored = [sem(f"l0_stored{u}") for u in range(2)]
    idx_s, val_s = m.idx_t, m.val_t
    staged, gate, looked, nodes_in = (sem("l0_staged"), sem("l0_gate"), sem("l0_looked"),
                                      sem("l0_nodes"))
    found = [sem(f"l0_found{u}", 0) for u in range(2)]

    nc.all_engine_barrier()
    with nc.Block() as block:
        @block.gpsimd
        def _(pool):
            pool.memset(o[1][:, 3 * AW:4 * AW], 0.0).then_inc(zeroed, 1)
            with pool.Fori(0, EG // 2) as i:
                for u in range(2):
                    pool.wait_ge(looked, i * 2 + ONE)
                    pool.tensor_copy(idx_s[u][:, :], m.srec[:, ds((i * 2 + u) * (8 * G), 8 * G)]
                                     .rearrange("p (t c) -> p t c", c=8)[:, :, 0])\
                        .then_inc(staged, 1)
                    pool.wait_ge(staged, i * 2 + (u + 1) + ONE)
                    pool.sem_inc(gate, 1)
                    for t in range(G):
                        pool.indirect_dma_start(
                            val_s[u][:, t:t + 1], None, m.pos_d[:, :],
                            bass.IndirectOffsetOnAxis(ap=idx_s[u][:, t:t + 1], axis=0))\
                            .then_inc(found[u], 16)
                    if u == 1:
                        for v in range(2):
                            pool.wait_ge(found[v], i * (16 * G) + 16 * G)
                            pool.tensor_copy(m.poss[:, ds((i * 2 + v) * G, G)], val_s[v][:, :])\
                                .then_inc(looked, 1)

        @block.vector
        def _(dve):
            link = Link(dve, dve_own)

            def norm(g, u, n):
                o4 = o[u].rearrange("p (t c) -> p t c", t=G)
                n4 = nrm[u].rearrange("p (t c) -> p t c", t=G)
                zu = z[:, u * G * H:(u + 1) * G * H].rearrange("p (t h) -> p t h", t=G)
                exs = m.exs[:, ds(g * (G * H), G * H)].rearrange("p (t h) -> p t h", t=G)
                dve.wait_ge(out_of, g * G + (G + 2) + ONE)
                dve.wait_ge(stored[u], n * 32 + ONE)
                link(dve.tensor_tensor(zu, o4[:, :, D:AW], exs, ALU.add))
                link(dve.tensor_scalar(zu, zu, 1e-16, None, ALU.add))
                link(dve.reciprocal(zu, zu))
                for t in range(G):
                    dve.tensor_tensor(n4[:, t, 0:D].rearrange("p (h c) -> p h c", c=C),
                                      o4[:, t, 0:D].rearrange("p (h c) -> p h c", c=C),
                                      bc(zu[:, t, :], C), ALU.mult)
                dve.tensor_tensor(n4[:, :, D:AW], exs, zu, ALU.mult).then_inc(normed, 1)

            def body(g, u, n, first, last):
                for t in range(G):
                    s = t % 2
                    tau = g * G + t
                    dve.wait_ge(summed, tau + 1 + ONE)
                    dve.tensor_tensor(msg[s][:, 0:D].rearrange("p (h c) -> p h c", c=C),
                                      m.xh[:, ds(tau * D, D)].rearrange("p (h c) -> p h c", c=C),
                                      bc(m.ex[:, ds(tau * H, H)], C), ALU.mult)
                    dve.tensor_copy(msg[s][:, D:AW], m.ex[:, ds(tau * H, H)])
                    equality(dve, m, m.drow, m.dstc, tau, s, made)
                    if t == 1 and not first:
                        norm(g - 1, 1 - u, n - (1 - u))

            each_group(dve, link, 6, body)
            norm(EG - 1, 1, EG // 2 - 1)
            dve.wait_ge(looked, EG + ONE)
            link(dve.tensor_scalar(m.masks[:, :], m.poss[:, :], float(EP), None, ALU.is_lt))
            dve.tensor_scalar(m.nmasks[:, :], m.masks[:, :], -1.0, 1.0, ALU.mult, ALU.add)

        @block.tensor
        def _(pe):
            pe.sem_inc(summed, 2)
            pe.wait_ge(zeroed, 1 + ONE)

            def body(g, u, n, first, last):
                for t in range(G):
                    s = t % 2
                    tau = g * G + t
                    prev = (o[u][96:P, (t - 1) * AW:t * AW] if t else o[1 - u][96:P, 3 * AW:4 * AW])
                    pe.wait_ge(made, tau + 1 + ONE)
                    pe.wait_ge(out_of, tau + 1 + ONE)
                    pe.matmul(pss[s], m.eq[s][:, :], msg[s], start=True, stop=False)
                    pe.wait_ge(out_of, tau + 2 + ONE)
                    pe.matmul(pss[s], m.carry[s][96:P, :], prev, start=False, stop=True)\
                        .then_inc(summed, 1)
            each_group(pe, None, 0, body)

        @block.scalar
        def _(act):
            act.sem_inc(out_of, 2)

            def body(g, u, n, first, last):
                if not first:
                    act.wait_ge(normed, g - 1 + ONE)
                for t in range(G):
                    act.wait_ge(summed, g * G + (t + 3) + ONE)
                    act.activation(o[u][:, t * AW:(t + 1) * AW], pss[t % 2], ACT.Copy)\
                        .then_inc(out_of, 1)
            each_group(act, None, 0, body)

        @block.sync
        def _(sp):
            def body(g, u, n, first, last):
                sp.wait_ge(normed, g + 1 + ONE)
                n4 = nrm[u].rearrange("p (t c) -> p t c", t=G)
                sp.dma_start(m.a_d[0].rearrange("(t q) c -> q t c", q=P)[:, ds(g * G, G), :], n4)\
                    .then_inc(stored[u], 16)
                sp.dma_start(m.tab_d.rearrange("(t q) c -> q t c", q=P)[:, ds(g * G, G), 0:H],
                             n4[:, :, D:AW]).then_inc(stored[u], 16)
            sp.dma_start(m.posn[:, 0:NT],
                         m.pos_d[0:NT * P, :].rearrange("(p t) c -> p (t c)", p=P))\
                .then_inc(nodes_in, 16)
            sp.dma_start(m.posn[0:REM, NT:NT + 1], m.pos_d[NT * P:N, :]).then_inc(nodes_in, 16)
            sp.wait_ge(nodes_in, 32 + ONE)
            each_group(sp, None, 0, body)
            for u in range(2):
                sp.wait_ge(stored[u], EG // 2 * 32 + ONE)


def edge_layer(nc, sem, m, k):
    halves = 2 if k == 1 else 1
    comps = 4
    co = {1: m.co1, 2: m.co2[0], 3: m.co2[1]}[k]
    nco = halves * comps
    root = k == 2
    gw = AW if k == 1 else D
    cut = Carve(m.work)
    msg, other = [cut(D) for _ in range(2)], cut(D)
    o = [cut(GD) for _ in range(2)]
    rows = [cut(G * gw) for _ in range(2)]
    a0 = cut(GD) if k == 1 else None
    whole = cut(GD) if k != 2 else None
    psT = m.PS[:, 0:1024]
    psB = [m.PS[:, 1024:2048], m.PS[:, 2048:3072]]
    psR = m.PS[:, 3072:3072 + D]
    psS = [m.PS[:, (3584 if root else 3072):][:, 0:D], m.PS[:, 3584:3584 + D]]
    free = 2 if root else 1
    table = m.a_d[k - 1]
    col = H + (k - 1) * D
    tab = m.tab_d.rearrange("(t q) c -> q t c", q=P)[:, :, col:col + D]

    def s_(name):
        return sem(f"l{k}_{name}")

    blank, staged, gate, zeroed = s_("blank"), s_("staged"), s_("gate"), s_("zeroed")
    stats, std, scales, hs = s_("stats"), s_("std"), s_("scales"), s_("h")
    turned, tout = s_("turned"), s_("tout")
    prods, eaten, rooted, rout = s_("prods"), s_("eaten"), s_("rooted"), s_("rout")
    made, summed, out_of, dve_own = s_("made"), s_("summed"), s_("out"), s_("dve")
    updated, o_sent, tab_sent = ([s_(f"{name}{u}") for u in range(2)] for name in
                                 ("updated", "o_sent", "tab_sent"))
    rows_in = [sem(f"l{k}_rows_in{u}", 0) for u in range(2)]
    if k == 2:
        bufs = [b[:, :] for b in m.idx_t], [cut(8 * G).bitcast(I32) for _ in range(2)]
        moved = [sem(f"l2_moved{u}", 0) for u in range(2)]
        drained, move_staged = [s_(f"drained{u}") for u in range(2)], s_("move_staged")
    alphas, widened, wide_own = s_("alphas"), s_("widened"), s_("wide_own")
    a0_in, joined, whole_sent, pool_own = (s_("a0_in"), s_("joined"), s_("whole_sent"),
                                           s_("pool"))

    nc.all_engine_barrier()
    with nc.Block() as block:
        @block.gpsimd
        def _(pool):
            for b in rows:
                pool.memset(b, 0.0).then_inc(blank, 1)
            pool.memset(o[1][:, 3 * D:4 * D], 0.0).then_inc(zeroed, 1)
            pool.wait_ge(blank, 2 + ONE)
            bound = pool.to_reg(EP - 1)

            def gather(g, u, n):
                pool.wait_ge(updated[u], n + ONE)
                pool.tensor_copy(m.idx_s[u][:, 0:G], m.poss[:, ds(g * G, G)]).then_inc(staged, 1)
                pool.wait_ge(staged, g + 1 + ONE)
                pool.sem_inc(gate, 1)
                for t in range(G):
                    pool.indirect_dma_start(
                        rows[u][:, t * gw:(t + 1) * gw], None, table,
                        bass.IndirectOffsetOnAxis(ap=m.idx_s[u][:, t:t + 1], axis=0),
                        bounds_check=bound, oob_is_err=False).then_inc(rows_in[u], 16)

            def widen(g, u):
                x, xh = m.xs[:, ds(g * GD, GD)], m.xh[:, ds(g * GD, GD)]
                xh8 = xh.rearrange("p (a c) -> p a c", c=C)
                pool.wait_ge(alphas, g + 1 + ONE)
                pool.sem_inc(gate, 1)
                pool.tensor_tensor(xh8, xh8, bc(m.alpha[:, u * G * H:(u + 1) * G * H], C),
                                   ALU.mult).then_inc(wide_own, 1)
                pool.wait_ge(wide_own, g + 1 + ONE)
                pool.sem_inc(gate, 1)
                pool.tensor_tensor(x, x, xh, ALU.add).then_inc(widened, 1)

            def join(g, u):
                bias = (m.bias0_b if k == 1 else m.bias1_b).unsqueeze(1).to_broadcast([P, G, D])
                w3, o3 = (b.rearrange("p (t d) -> p t d", t=G) for b in (whole, o[u]))
                pool.wait_ge(out_of, g * G + (G + 2) + ONE)
                at_least(pool, whole_sent, g * 16)
                pool.sem_inc(gate, 1)
                added = pool.tensor_tensor(w3, o3, bias, ALU.add)
                if k == 1:
                    added.then_inc(pool_own, 1)
                    pool.wait_ge(pool_own, g + 1 + ONE)
                    pool.wait_ge(a0_in, g * 16 + 16 + ONE)
                    pool.sem_inc(gate, 1)
                    added = pool.tensor_tensor(whole, whole, a0, ALU.add)
                added.then_inc(joined, 1)

            def body(g, u, n, first, last):
                if not last:
                    gather(g + 1, 1 - u, n + u)
                if k == 1 and not last:
                    widen(g + 1, 1 - u)
                if k != 2 and not first:
                    join(g - 1, 1 - u)
                if k == 2:
                    at_least(pool, drained[u], n)
                    scatter_group(pool, m, 1, g, u, g, bufs, moved, move_staged, gate, m.rec2_d)

            gather(0, 0, 0)
            if k == 1:
                widen(0, 0)
            each_group(pool, None, 0, body)
            if k != 2:
                join(EG - 1, 1)

        @block.sync
        def _(sp):
            def body(g, u, n, first, last):
                if k == 1:
                    sp.wait_ge(joined, g + ONE)
                    sp.dma_start(a0.rearrange("p (t c) -> p t c", t=G),
                                 table.rearrange("(t q) c -> q t c", q=P)[:, ds(g * G, G), 0:D])\
                        .then_inc(a0_in, 16)
                sp.wait_ge(out_of, g * G + (G + 2) + ONE)
                o4 = o[u].rearrange("p (t c) -> p t c", t=G)
                if k < 3:
                    sp.dma_start(m.a_d[k].rearrange("(t q) c -> q t c", q=P)[:, ds(g * G, G), :],
                                 o4).then_inc(o_sent[u], 16)
                if k == 2:
                    sp.dma_start(tab[:, ds(g * G, G), :], o4).then_inc(tab_sent[u], 16)
                    sp.wait_ge(moved[u], n * (16 * G) + 16 * G)
                    sp.sem_inc(drained[u], 1)
                else:
                    if k == 3:
                        sp.sem_inc(m.gate_sp, 1)
                    sp.wait_ge(joined, g + 1 + ONE)
                    sp.sem_inc(m.gate_sp, 1)
                    sp.dma_start(tab[:, ds(g * G, G), :], whole.rearrange("p (t c) -> p t c", t=G))\
                        .then_inc(whole_sent, 16)

            each_group(sp, None, 0, body)
            for u in range(2):
                if k < 3:
                    sp.wait_ge(o_sent[u], EG // 2 * 16 + ONE)
                if k == 2:
                    sp.wait_ge(tab_sent[u], EG // 2 * 16 + ONE)
            if k != 2:
                sp.wait_ge(whole_sent, EG * 16 + ONE)

        @block.vector
        def _(dve):
            link = Link(dve, dve_own)

            def prepare(g, u, n):
                r4 = rows[u].rearrange("p (t c) -> p t c", t=G)
                dve.wait_ge(rows_in[u], n * (16 * G) + 16 * G)
                dve.wait_ge(hs, g + ONE)
                if k == 3:
                    dve.wait_ge(turned, g + ONE)
                    for t in range(G):
                        last = dve.scalar_tensor_tensor(
                            m.h[u][:, t * D:(t + 1) * D], r4[:, t, 0:D],
                            m.masks[:, ds(g * G + t, 1)], m.xh[:, ds(g * GD + t * D, D)],
                            ALU.mult, ALU.add)
                    value = link.mark(last)
                    link.until(value)
                    dve.sem_inc(hs, 1)
                    dve.sem_inc(updated[u], 1)
                    return
                if k == 1:
                    al = m.alpha[:, u * G * H:(u + 1) * G * H]
                    for t in range(G):
                        last = dve.scalar_tensor_tensor(
                            al[:, t * H:(t + 1) * H], r4[:, t, D:AW],
                            m.masks[:, ds(g * G + t, 1)],
                            m.nmasks[:, ds(g * G + t, 1)].to_broadcast([P, H]),
                            ALU.mult, ALU.add)
                    last.then_inc(alphas, 1)
                    return
                update(g, u)

            def update(g, u):
                r4 = rows[u].rearrange("p (t c) -> p t c", t=G)
                xt = [m.xs[:, ds(g * GD + t * D, D)] for t in range(G)]
                if k == 1:
                    dve.wait_ge(widened, g + 1 + ONE)
                for t in range(G):
                    last = dve.scalar_tensor_tensor(xt[t], r4[:, t, 0:D],
                                                    m.masks[:, ds(g * G + t, 1)], xt[t],
                                                    ALU.mult, ALU.add)
                link(last)
                dve.sem_inc(updated[u], 1)

            def measure(g, u):
                ln_stats(dve, link, m, [m.xs[:, ds(g * GD + t * D, D)] for t in range(G)], u,
                         stats)

            def scale(g, u):
                dve.wait_ge(std, g + 1 + ONE)
                ln_scales(dve, link, m, u, G, scales)

            def message(g, t):
                s, tau = t % 2, g * G + t
                dve.wait_ge(summed, tau + 1 + ONE)
                at_least(dve, made, tau)
                sums, ended = (msg[s], other), [None, None]
                for hf in range(halves):
                    dve.wait_ge(prods, tau * halves + (hf + 1) + ONE)
                    b = psB[hf if halves == 2 else s]
                    for c in range(comps):
                        to = sums[c % 2]
                        if k == 1:
                            part = b.rearrange("p (k r o) -> p k r o", k=2, r=4)[:, :, c, :]
                            to = to.rearrange("p (k o) -> p k o", k=2)
                        else:
                            part = b[:, c * D:(c + 1) * D]
                        w = co[:, ds(tau * nco + hf * comps + c, 1)]
                        if ended[c % 2] is None:
                            last = dve.tensor_scalar(to, part, w, None, ALU.mult)
                        else:
                            link.until(ended[c % 2])
                            last = dve.scalar_tensor_tensor(to, part, w, to, ALU.mult, ALU.add)
                        ended[c % 2] = link.mark(last)
                    link.until(ended[1])
                    dve.sem_inc(eaten, 1)
                dve.tensor_tensor(msg[s], msg[s], other, ALU.add)
                equality(dve, m, m.drow, m.dstc, tau, s, made)

            def body(g, u, n, first, last):
                for t in range(G):
                    message(g, t)
                    if t == 0 and not last:
                        prepare(g + 1, 1 - u, n + u)
                    if t == 1 and not last and k == 1:
                        update(g + 1, 1 - u)
                        measure(g + 1, 1 - u)
                    if t == 0 and not last and k == 2:
                        measure(g + 1, 1 - u)
                    if t == (2 if k == 1 else 0) and not last and k < 3:
                        scale(g + 1, 1 - u)

            dve.sem_inc(eaten, 2)
            prepare(0, 0, 0)
            if k == 1:
                update(0, 0)
            if k < 3:
                measure(0, 0)
                scale(0, 0)
            per = {1: 2 * (4 * 8 + 6), 2: 2 * (4 * 4 + 6), 3: 2 * (4 * 4 + 1)}[k]
            each_group(dve, link, per, body)

        @block.scalar
        def _(act):
            def normal(g, u, n):
                root_of(g, u)
                shape(g, u)

            def root_of(g, u):
                _, var, s = ln_parts(m, u, G)
                act.wait_ge(stats, g + 1 + ONE)
                act.activation(s[0], var, ACT.Sqrt, bias=m.eps[:, :]).then_inc(std, 1)

            def shape(g, u):
                act.wait_ge(scales, g + 1 + ONE)
                ln_apply(act, m, [m.xs[:, ds(g * GD + t * D, D)] for t in range(G)], u, m.h[u], hs)

            def turned_out(g, u):
                act.wait_ge(turned, g + 1 + ONE)
                if k == 3:
                    for c in range(2):
                        last = act.activation(m.hT[u][:, c * 512:(c + 1) * 512],
                                              psT[:, c * 512:(c + 1) * 512], ACT.Relu,
                                              bias=m.b0col[:, c:c + 1])
                else:
                    last = act.activation(m.hT[u][:, :], psT, ACT.Copy)
                last.then_inc(tout, 1)

            def sum_out(tau, u, t):
                act.wait_ge(summed, tau + 3 + ONE)
                act.activation(o[u][:, t * D:(t + 1) * D], psS[t % 2], ACT.Copy)\
                    .then_inc(out_of, 1)

            def root_out(g, t):
                if k == 2:
                    act.wait_ge(rooted, g * G + (t + 1) + ONE)
                    act.activation(m.xh[:, ds((g * G + t) * D, D)], psR, ACT.Copy)\
                        .then_inc(rout, 1)

            def body(g, u, n, first, last):
                root_out(g, 0)
                if not first:
                    sum_out(g * G - 1, 1 - u, 3)
                if k < 3:
                    act.wait_ge(o_sent[u], n * 16 + ONE)
                if k == 2:
                    act.wait_ge(tab_sent[u], n * 16 + ONE)
                elif not first:
                    act.wait_ge(joined, g - 1 + ONE)
                root_out(g, 1)
                if not last and k == 2:
                    normal(g + 1, 1 - u, n + u)
                sum_out(g * G, u, 0)
                if not last and k == 1:
                    root_of(g + 1, 1 - u)
                root_out(g, 2)
                sum_out(g * G + 1, u, 1)
                root_out(g, 3)
                if not last and k == 1:
                    shape(g + 1, 1 - u)
                if not last:
                    turned_out(g + 1, 1 - u)
                sum_out(g * G + 2, u, 2)

            act.sem_inc(out_of, 2)
            if k == 2:
                act.sem_inc(rout, 1)
            if k != 3:
                normal(0, 0, 0)
            turned_out(0, 0)
            each_group(act, None, 0, body)
            sum_out(EP // P - 1, 1, 3)

        @block.tensor
        def _(pe):
            def products(g, u, t):
                tau = g * G + t
                s = t % 2
                hT = [m.hT[u][:, c * 512 + t * P:c * 512 + (t + 1) * P] for c in range(2)]
                pe.wait_ge(tout, g + 1 + ONE)
                if root:
                    pe.wait_ge(rout, tau + 1 + ONE)
                    for c in range(2):
                        last = pe.matmul(psR, hT[c], m.wr[0][:, c * D:(c + 1) * D],
                                         start=(c == 0), stop=(c == 1))
                    last.then_inc(rooted, 1)
                for hf in range(halves):
                    b = psB[hf if halves == 2 else s]
                    pe.wait_ge(eaten, tau * halves + (hf + 1) + ONE)
                    if k == 1:
                        for c in range(2):
                            last = pe.matmul(b[:, c * 512:(c + 1) * 512], hT[c],
                                             m.bd[:, (c * 2 + hf) * 512:(c * 2 + hf + 1) * 512],
                                             start=True, stop=True)
                    else:
                        for j in range(2):
                            for c in range(2):
                                last = pe.matmul(
                                    b[:, j * 512:(j + 1) * 512], hT[c],
                                    m.wb[k - 2][:, (c * 2 + j) * 512:(c * 2 + j + 1) * 512],
                                    start=(c == 0), stop=(c == 1))
                    last.then_inc(prods, 1)

            def sums(tau, u, t):
                s = t % 2
                prev = (o[u][96:P, (t - 1) * D:t * D] if t else o[1 - u][96:P, 3 * D:4 * D])
                pe.wait_ge(made, tau + 1 + ONE)
                pe.wait_ge(out_of, tau + free + ONE)
                pe.matmul(psS[s], m.eq[s][:, :], msg[s], start=True, stop=False)
                pe.wait_ge(out_of, tau + 2 + ONE)
                pe.matmul(psS[s], m.carry[s][96:P, :], prev, start=False, stop=True)\
                    .then_inc(summed, 1)

            def turn_group(g, u):
                pe.wait_ge(hs, g + 1 + ONE)
                pe.wait_ge(tout, g + ONE)
                turn(pe, m, m.h[u], psT, G, turned)

            def body(g, u, n, first, last):
                for t in range(G):
                    products(g, u, t)
                    if t == 3 and not last:
                        turn_group(g + 1, 1 - u)
                    if t:
                        sums(g * G + (t - 1), u, t - 1)
                    elif not first:
                        sums(g * G - 1, 1 - u, 3)

            pe.sem_inc(summed, 2)
            pe.wait_ge(zeroed, 1 + ONE)
            turn_group(0, 0)
            each_group(pe, None, 0, body)
            sums(EP // P - 1, 1, 3)


def sage(nc, sem, m):
    MW = D + 2
    cut, cuth = Carve(m.xs), Carve(m.xh)
    srow = cuth(EP)
    rows, res = [cut(GD) for _ in range(2)], [cut(GD) for _ in range(2)]
    o, msg = [cut(G * MW) for _ in range(2)], [cut(MW) for _ in range(2)]
    inv = cut(2 * G)
    psT = m.PS[:, 0:1024]
    psB = [m.PS[:, 1024:1024 + D], m.PS[:, 1536:1536 + D]]
    psS = [m.PS[:, 2048:2048 + MW], m.PS[:, 2560:2560 + MW]]
    blank, staged, gate, ready, got_row = (sem("sg_blank"), sem("sg_staged"), sem("sg_gate"),
                                           sem("sg_ready"), sem("sg_row"))
    turned, tout, prods, made, summed, out_of, done = (
        sem("sg_turned"), sem("sg_tout"), sem("sg_prods"), sem("sg_made"), sem("sg_summed"),
        sem("sg_out"), sem("sg_done"))
    rows_in, res_in, sent = ([sem(f"sg_{k}{u}", 0) for u in range(2)] for k in
                             ("rows_in", "res_in", "sent"))
    drained = [sem(f"sg_drained{u}") for u in range(2)]
    dve_own, put = sem("sg_dve"), sem("sg_put")
    nc.all_engine_barrier()
    with nc.Block() as block:
        @block.sync
        def _(sp):
            sp.dma_start(srow, m.row2_d[0, 0:EP].partition_broadcast(P)).then_inc(got_row, 16)
            sp.wait_ge(got_row, 16 + ONE)
            drain(sp, sent, drained)

        @block.gpsimd
        def _(pool):
            for b in (*rows, *res):
                pool.memset(b, 0.0).then_inc(blank, 1)
            pool.memset(o[1][:, 3 * MW:4 * MW], 0.0).then_inc(ready, 1)
            for b in msg:
                pool.memset(b[:, D:MW], 1.0).then_inc(ready, 1)
            pool.wait_ge(blank, 4 + ONE)
            bound = pool.to_reg(N - 1)

            def heads(g, u, n):
                at_least(pool, turned, g - 1)
                pool.tensor_copy(m.idx_s[u][:, :], m.srec2[:, ds(g * (8 * G), 8 * G)])\
                    .then_inc(staged, 1)
                pool.wait_ge(staged, g + 1 + ONE)
                pool.sem_inc(gate, 1)
                for t in range(G):
                    pool.indirect_dma_start(
                        rows[u][:, t * D:(t + 1) * D], None, m.h3_d[:, :],
                        bass.IndirectOffsetOnAxis(ap=m.idx_s[u][:, 8 * t + 1:8 * t + 2], axis=0),
                        bounds_check=bound, oob_is_err=False).then_inc(rows_in[u], 16)

            def fetch(g, u, n):
                at_least(pool, drained[u], n)
                pool.sem_inc(gate, 1)
                pool.tensor_copy(m.idx_t[u][:, :], m.to_node[:, ds(g * G, G)]).then_inc(put, 1)
                pool.wait_ge(put, g + 1 + ONE)
                pool.sem_inc(gate, 1)
                for t in range(G):
                    pool.indirect_dma_start(
                        res[u][:, t * D:(t + 1) * D], None, m.out[:, :],
                        bass.IndirectOffsetOnAxis(ap=m.idx_t[u][:, t:t + 1], axis=0),
                        bounds_check=bound, oob_is_err=False).then_inc(res_in[u], 16)

            def scatter(g, u):
                pool.wait_ge(done, g + 1 + ONE)
                pool.sem_inc(gate, 1)
                for t in range(G):
                    pool.indirect_dma_start(
                        m.out[:, :],
                        bass.IndirectOffsetOnAxis(ap=m.idx_t[u][:, t:t + 1], axis=0),
                        res[u][:, t * D:(t + 1) * D], None,
                        bounds_check=bound, oob_is_err=False).then_inc(sent[u], 16)

            def body(g, u, n, first, last):
                if not last:
                    heads(g + 1, 1 - u, n + u)
                if not first:
                    scatter(g - 1, 1 - u)
                if not last:
                    fetch(g + 1, 1 - u, n + u)

            heads(0, 0, 0)
            fetch(0, 0, 0)
            each_group(pool, None, 0, body)
            scatter(EG - 1, 1)
            for u in range(2):
                pool.wait_ge(sent[u], EG // 2 * 16 * G)

        @block.vector
        def _(dve):
            link = Link(dve, dve_own)

            def result(g, u, n):
                o4 = o[u].rearrange("p (t c) -> p t c", t=G)
                iv = inv[:, u * G:(u + 1) * G]
                dve.wait_ge(out_of, g * G + (G + 2) + ONE)
                link(dve.reciprocal(iv.unsqueeze(2), o4[:, :, D:D + 1]))
                dve.wait_ge(res_in[u], n * (16 * G) + 16 * G)
                for t in range(G):
                    r = res[u][:, t * D:(t + 1) * D]
                    last = dve.scalar_tensor_tensor(r, o4[:, t, 0:D], iv[:, t:t + 1], r,
                                                    ALU.mult, ALU.add)
                last.then_inc(done, 1)

            def body(g, u, n, first, last):
                for t in range(G):
                    s, tau = t % 2, g * G + t
                    dve.wait_ge(summed, tau + 1 + ONE)
                    dve.wait_ge(prods, tau + 1 + ONE)
                    dve.tensor_copy(msg[s][:, 0:D], psB[s])
                    equality(dve, m, srow, m.srcc, tau, s, made)
                    if t == 1 and not first:
                        result(g - 1, 1 - u, n - (1 - u))

            dve.wait_ge(got_row, 16 + ONE)
            dve.wait_ge(ready, 3 + ONE)
            each_group(dve, link, 2, body)
            result(EG - 1, 1, EG // 2 - 1)

        @block.scalar
        def _(act):
            def turned_out(g, u):
                act.wait_ge(turned, g + 1 + ONE)
                act.activation(m.hT[u][:, :], psT, ACT.Copy).then_inc(tout, 1)

            def sum_out(tau, u, t):
                act.wait_ge(summed, tau + 3 + ONE)
                act.activation(o[u][:, t * MW:(t + 1) * MW], psS[t % 2], ACT.Copy)\
                    .then_inc(out_of, 1)

            def body(g, u, n, first, last):
                if not first:
                    sum_out(g * G - 1, 1 - u, 3)
                    act.wait_ge(done, g - 1 + ONE)
                sum_out(g * G, u, 0)
                sum_out(g * G + 1, u, 1)
                if not last:
                    turned_out(g + 1, 1 - u)
                sum_out(g * G + 2, u, 2)

            act.sem_inc(out_of, 2)
            turned_out(0, 0)
            each_group(act, None, 0, body)
            sum_out(ET - 1, 1, 3)

        @block.tensor
        def _(pe):
            def turn_group(g, u, n):
                pe.wait_ge(rows_in[u], n * (16 * G) + 16 * G)
                pe.wait_ge(tout, g + ONE)
                turn(pe, m, rows[u], psT, G, turned)

            def product(g, u, t):
                tau, s = g * G + t, t % 2
                pe.wait_ge(tout, g + 1 + ONE)
                if not (isinstance(tau, int) and tau < 2):
                    pe.wait_ge(made, tau - 1 + ONE)
                for c in range(2):
                    last = pe.matmul(psB[s], m.hT[u][:, c * 512 + t * P:c * 512 + (t + 1) * P],
                                     m.w2t[:, c * D:(c + 1) * D], start=(c == 0), stop=(c == 1))
                last.then_inc(prods, 1)

            def sums(tau, u, t):
                s = t % 2
                prev = (o[u][96:P, (t - 1) * MW:t * MW] if t else o[1 - u][96:P, 3 * MW:4 * MW])
                pe.wait_ge(made, tau + 1 + ONE)
                pe.wait_ge(out_of, tau + 1 + ONE)
                pe.matmul(psS[s], m.eq[s][:, :], msg[s], start=True, stop=False)
                pe.wait_ge(out_of, tau + 2 + ONE)
                pe.matmul(psS[s], m.carry[s][96:P, :], prev, start=False, stop=True)\
                    .then_inc(summed, 1)

            def body(g, u, n, first, last):
                for t in range(G):
                    product(g, u, t)
                    if t == 3 and not last:
                        turn_group(g + 1, 1 - u, n + u)
                    if t:
                        sums(g * G + (t - 1), u, t - 1)
                    elif not first:
                        sums(g * G - 1, 1 - u, 3)

            pe.sem_inc(summed, 2)
            pe.wait_ge(ready, 3 + ONE)
            turn_group(0, 0, 0)
            each_group(pe, None, 0, body)
            sums(ET - 1, 1, 3)


def nodes(nc, sem, m):
    STAGES = 3
    NQI = STAGES * NG
    order = [(s, t - s) for t in range(NGRP + 2) for s in range(STAGES) if 0 <= t - s < NGRP]
    HEAD, TRIPS = 3, (NGRP - 4) // NG
    TAIL = HEAD + TRIPS * NQI
    due = [max(p - 3, order.index((s - 1, g)) + 1 if s else 0) for p, (s, g) in enumerate(order)]
    due = [max(due[:p + 1]) for p in range(len(due))]
    cut, cuth = Carve(m.xs), Carve(m.xh)
    work = Carve(m.work)
    xin, xw = ([cut(GD) for _ in range(NG)] for _ in range(2))
    y = [cut(GD), cut(GD), work(GD), work(GD)]
    rows = [cuth(G * TW), cuth(G * TW), cuth(G * TW), m.big[:, 0:G * TW]]
    psT = [m.PS[:, 0:1024], m.PS[:, 1024:2048]]
    psY = [m.PS[:, 2048:3072], m.PS[:, 3072:4096]]
    wts = [m.w0[:, :], m.wr[1], m.w1t]
    x_v = m.x[0:NT * P, :].rearrange("(p t) d -> p (t d)", p=P)
    out_v = m.out[0:NT * P, :].rearrange("(p t) d -> p (t d)", p=P)
    h3_v = m.h3_d[0:NT * P, :].rearrange("(p t) d -> p (t d)", p=P)
    xin_in, stored, h_sent = ([sem(f"n_{k}{g}") for g in range(NG)] for k in
                              ("xin", "stored", "h_sent"))
    rows_in = [sem(f"n_rows{g}", 0) for g in range(NG)]
    filled, staged, gate = sem("n_filled"), sem("n_staged"), sem("n_gate")
    added = [sem(f"n_added{k}") for k in range(3)]
    stats, std, scales, hs = sem("n_stats"), sem("n_std"), sem("n_scales"), sem("n_h")
    first_done, relus = sem("n_first"), sem("n_relus")
    turned, tout, prods, eaten, final = (sem("n_turned"), sem("n_tout"), sem("n_prods"),
                                         sem("n_eaten"), sem("n_final"))
    dve_own = sem("n_dve")

    def size(g):
        return 1 if isinstance(g, int) and g == NGRP - 1 else G

    def where(i, q):
        if i is None:
            s, g = order[q]
            return q, s, g, g % NG, g // NG, size(g)
        s, g = order[q]
        return i * NQI + q, s, i * NG + g, g % NG, i + g // NG, G

    def number(s, g):
        return order.index((s, g)) if isinstance(g, int) else g * STAGES + (4 * s - 3)

    def rows_to_use(i, s, g, n):
        src = xin[g] if s == 0 else xw[g]
        return [src[:, t * D:(t + 1) * D] for t in range(n)]

    def run(eng, link, per, body, rest):
        for q in range(HEAD):
            rest(q)
            body(None, q)
        rest(HEAD)
        with eng.Fori(0, TRIPS) as i:
            if link is not None:
                link.enter(i, per)
            for q in range(HEAD, HEAD + NQI):
                body(i, q)
            if link is not None:
                link.leave(TRIPS)
        for q in range(TAIL, len(order)):
            rest(q)
            body(None, q)

    def steps(eng, first, body):
        for t in range(first):
            body(t, 0, t)
        trips = (NGRP - 7) // NG
        with eng.Fori(0, trips) as i:
            for v in range(first, first + NG):
                body(i * NG + v, i, v)
        for t in range(first + trips * NG, NGRP + 2):
            body(t, 0, t)

    nc.all_engine_barrier()
    with nc.Block() as block:
        @block.sync
        def _(sp):
            def load(g, c):
                if size(g) == G:
                    sp.dma_start(xin[c % NG], x_v[:, ds(g * GD, GD)]).then_inc(xin_in[c % NG], 16)
                else:
                    sp.dma_start(xin[c % NG][0:REM, 0:D], m.x[NT * P:N, :])\
                        .then_inc(xin_in[c % NG], 16)

            def store_h(g, c):
                c = c % NG
                sp.wait_ge(hs, number(2, g) + 1 + ONE)
                sp.sem_inc(m.gate_sp, 1)
                if size(g) == G:
                    sp.dma_start(h3_v[:, ds(g * GD, GD)], y[c]).then_inc(h_sent[c], 16)
                else:
                    sp.dma_start(m.h3_d[NT * P:N, :], y[c][0:REM, 0:D]).then_inc(h_sent[c], 16)

            def store(g, c):
                c = c % NG
                sp.wait_ge(final, g + 1 + ONE)
                sp.sem_inc(m.gate_sp, 1)
                if size(g) == G:
                    sp.dma_start(out_v[:, ds(g * GD, GD)], xw[c]).then_inc(stored[c], 16)
                else:
                    sp.dma_start(m.out[NT * P:N, :], xw[c][0:REM, 0:D]).then_inc(stored[c], 16)

            def body(t, i, v):
                alone = isinstance(t, int)
                if not alone or t + NG < NGRP:
                    sp.wait_ge(added[0], t + 1 + ONE)
                    sp.sem_inc(m.gate_sp, 1)
                    sp.wait_ge(hs, number(0, t) + 1 + ONE)
                    sp.sem_inc(m.gate_sp, 1)
                    load(t + NG, v)
                if not alone or 1 <= t <= NGRP:
                    store_h(t - 1, v - 1)
                if not alone or t >= 2:
                    store(t - 2, v - 2)

            for g in range(NG):
                load(g, g)
            steps(sp, 2, body)
            for g in range(NG):
                sp.wait_ge(stored[g], 16 * NI + ONE)
                sp.wait_ge(h_sent[g], 16 * NI + ONE)

        @block.gpsimd
        def _(pool):
            bound = pool.to_reg(EP - 1)

            def add(c, n, frm, more, k):
                pool.tensor_tensor(xw[c][:, 0:n * D].rearrange("p (t d) -> p t d", t=n),
                                   frm[:, 0:n * D].rearrange("p (t d) -> p t d", t=n),
                                   more, ALU.add).then_inc(added[k], 1)

            def table(c, n, col):
                return rows[c].rearrange("p (t c) -> p t c", t=G)[:, 0:n, col:col + D]

            def gather(g, c):
                pool.wait_ge(filled, g + 1 + ONE)
                pool.sem_inc(gate, 1)
                pool.tensor_copy(m.idx_n[c][:, 0:size(g)], m.posn[:, ds(g * G, size(g))])\
                    .then_inc(staged, 1)
                pool.wait_ge(staged, g + 1 + ONE)
                pool.sem_inc(gate, 1)
                for t in range(size(g)):
                    pool.indirect_dma_start(
                        rows[c][:, t * TW:(t + 1) * TW], None, m.tab_d[:, :],
                        bass.IndirectOffsetOnAxis(ap=m.idx_n[c][:, t:t + 1], axis=0),
                        bounds_check=bound, oob_is_err=False).then_inc(rows_in[c], 16)

            def begin(g, c, n):
                pool.wait_ge(xin_in[c], n * 16 + 16 + ONE)
                at_least(pool, stored[c], n * 16)
                pool.wait_ge(rows_in[c], n * (16 * G) + 16 * size(g))
                pool.sem_inc(gate, 1)
                add(c, size(g), xin[c], table(c, size(g), H), 0)

            def middle(g, c, s):
                n = size(g)
                pool.wait_ge(hs, number(s, g) + 1 + ONE)
                pool.sem_inc(gate, 1)
                add(c, n, xw[c], table(c, n, H + 2 * D) if s == 1 else
                    m.b12_b[:, :].unsqueeze(1).to_broadcast([P, n, D]), s)

            def body(t, i, v):
                alone = isinstance(t, int)
                if not alone or t + 2 < NGRP:
                    gather(t + 2, (v + 2) % NG)
                if not alone or t < NGRP:
                    middle(t, v % NG, 1)
                if not alone or t + 1 < NGRP:
                    begin(t + 1, (v + 1) % NG, i + (v + 1) // NG)
                if not alone or 1 <= t <= NGRP:
                    middle(t - 1, (v - 1) % NG, 2)

            gather(0, 0)
            gather(1, 1)
            begin(0, 0, 0)
            steps(pool, 2, body)

        @block.vector
        def _(dve):
            link = Link(dve, dve_own)

            def prepare(i, q):
                u = q % 2
                Q, s, _, g, times, n = where(i, q)
                if s == 0:
                    dve.wait_ge(xin_in[g], times * 16 + 16 + ONE)
                at_least(dve, turned, Q - 1)
                ln_stats(dve, link, m, rows_to_use(i, s, g, n), u, stats)
                dve.wait_ge(std, Q + 1 + ONE)
                ln_scales(dve, link, m, u, n, scales)

            def consume(i, q):
                u = q % 2
                Q, s, j, g, times, n = where(i, q)
                ps, x = psY[u][:, 0:n * D], xw[g][:, 0:n * D]
                dve.wait_ge(prods, Q + 1 + ONE)
                if s == 0:
                    al = rows[g].rearrange("p (t c) -> p t c", t=G)[:, 0:n, 0:H]\
                        .unsqueeze(3).to_broadcast([P, n, H, C])
                    at_least(dve, h_sent[g], times * 16)
                    dve.wait_ge(rows_in[g], times * (16 * G) + 16 * n)
                    link(dve.tensor_tensor(
                        y[g][:, 0:n * D].rearrange("p (t h c) -> p t h c", h=H, c=C),
                        ps.rearrange("p (t h c) -> p t h c", h=H, c=C), al, ALU.mult))
                    dve.sem_inc(eaten, 1)
                    ps = y[g][:, 0:n * D]
                dve.wait_ge(added[s], j + 1 + ONE)
                link(dve.tensor_tensor(x, x, ps, ALU.add))
                if s > 0:
                    dve.sem_inc(eaten, 1)
                if s == 2:
                    dve.sem_inc(final, 1)

            def body(i, q):
                if i is not None:
                    prepare(i, q + 3)
                consume(i, q)

            def rest(q):
                for p, d in enumerate(due):
                    if d == q and (q != HEAD or p < HEAD + 3):
                        prepare(None, p)

            dve.sem_inc(eaten, 2)
            run(dve, link, NG * (STAGES * 5 + 4), body, rest)

        @block.scalar
        def _(act):
            def normal(i, q):
                u = q % 2
                Q, s, _, g, _, n = where(i, q)
                _, var, sc = ln_parts(m, u, n)
                act.wait_ge(stats, Q + 1 + ONE)
                act.activation(sc[0], var, ACT.Sqrt, bias=m.eps[:, :]).then_inc(std, 1)
                act.wait_ge(scales, Q + 1 + ONE)
                at_least(act, turned, Q - 1)
                ln_apply(act, m, rows_to_use(i, s, g, n), u, y[g] if s == 2 else m.h[u], hs)

            def part(ap, n):
                return ap.rearrange("p (k e) -> p k e", k=2)[:, :, 0:n * P]

            def turned_out(i, q):
                u = q % 2
                Q, _, _, _, _, n = where(i, q)
                act.wait_ge(turned, Q + 1 + ONE)
                at_least(act, prods, Q - 1)
                act.activation(part(m.hT[u][:, :], n), part(psT[u], n), ACT.Copy)\
                    .then_inc(tout, 1)

            def relu(i, q):
                u = q % 2
                _, _, j, _, _, n = where(i, q)
                act.wait_ge(first_done, j + 1 + ONE)
                for c in range(2):
                    last = act.activation(part(m.hT[u][:, :], n)[:, c, :], part(psY[u], n)[:, c, :],
                                          ACT.Relu, bias=m.b0col[:, c:c + 1])
                last.then_inc(relus, 1)

            def fill(g, c):
                at_least(act, added[1], g - NG + 1)
                at_least(act, first_done, g - NG + 1)
                act.activation(rows[c].rearrange("p (t c) -> p t c", t=G),
                               m.pre[:, :].unsqueeze(1).to_broadcast([P, G, TW]), ACT.Copy)\
                    .then_inc(filled, 1)

            def body(i, q):
                Q, s, j, c, _, _ = where(i, q)
                if s == 1:
                    relu(i, q)
                if i is None:
                    for p, d in enumerate(due):
                        if d == q and 0 < p <= q + 1:
                            normal(i, p)
                if i is not None or q + 1 < len(order):
                    turned_out(i, q + 1)
                if i is not None:
                    normal(i, q + 3)
                else:
                    for p, d in enumerate(due):
                        if d == q and p > q + 1:
                            normal(i, p)
                if s == 0 and (i is not None or j + 2 < NGRP):
                    fill(j + 2, (c + 2) % NG)

            def rest(q):
                if q == 0:
                    normal(None, 0)
                    turned_out(None, 0)
                if q == HEAD:
                    for p in range(HEAD, HEAD + 3):
                        if due[p] == HEAD:
                            normal(None, p)

            fill(0, 0)
            fill(1, 1)
            run(act, None, 0, body, rest)

        @block.tensor
        def _(pe):
            def turn_rows(i, q):
                u = q % 2
                Q, s, _, g, _, n = where(i, q)
                pe.wait_ge(hs, Q + 1 + ONE)
                at_least(pe, tout, Q - 1)
                turn(pe, m, y[g] if s == 2 else m.h[u], psT[u], n, turned)

            def first(i, q):
                u = q % 2
                Q, _, _, g, _, n = where(i, q)
                pe.wait_ge(tout, Q + 1 + ONE)
                pe.wait_ge(eaten, Q + 1 + ONE)
                for f in range(2):
                    to = psY[u][:, f * 512:f * 512 + n * P]
                    for c in range(2):
                        pe.matmul(to, m.wr[0][:, c * D + f * P:c * D + (f + 1) * P],
                                  m.hT[u][:, c * 512:c * 512 + n * P], start=(c == 0), stop=False)
                    for t in range(n):
                        at = t * TW + H + D + f * P
                        last = pe.matmul(to[:, t * P:(t + 1) * P], rows[g][:, at:at + P],
                                         m.ident[:, :], start=False, stop=(t == n - 1))
                last.then_inc(first_done, 1)

            def product(i, q):
                u = q % 2
                Q, s, j, _, _, n = where(i, q)
                if s == 1:
                    pe.wait_ge(relus, j + 1 + ONE)
                else:
                    pe.wait_ge(tout, Q + 1 + ONE)
                    pe.wait_ge(eaten, Q + 1 + ONE)
                for t in range(n):
                    for c in range(2):
                        last = pe.matmul(psY[u][:, t * D:(t + 1) * D],
                                         m.hT[u][:, c * 512 + t * P:c * 512 + (t + 1) * P],
                                         wts[s][:, c * D:(c + 1) * D],
                                         start=(c == 0), stop=(c == 1))
                last.then_inc(prods, 1)

            def body(i, q):
                if order[q][0] == 1:
                    first(i, q)
                if i is not None or q + 1 < len(order):
                    turn_rows(i, q + 1)
                product(i, q)

            turn_rows(None, 0)
            run(pe, None, 0, body, lambda q: None)


def build(nc, x, src, dst, ea, rel, ew, W0, Wedge, att_src, att_dst, att_edge, bias0, L1w,
          comps, bases, roots, biases, W1, b1, W2, b2, out):
    ctx = ExitStack()
    m = Store()
    (m.x, m.src, m.dst, m.ea, m.rel, m.ew, m.W0, m.Wedge, m.att_src, m.att_dst, m.att_edge,
     m.bias0, m.L1w, m.comps, m.bases, m.roots, m.biases, m.W1, m.b1, m.W2, m.b2, m.out) = (
         x, src, dst, ea, rel, ew, W0, Wedge, att_src, att_dst, att_edge, bias0, L1w, comps,
         bases, roots, biases, W1, b1, W2, b2, out)
    with ctx:
        def sb(name, shape, dt=F32):
            return ctx.enter_context(nc.sbuf_tensor(name, shape, dt))

        def sem(name):
            return ctx.enter_context(nc.semaphore(name))

        def dram(name, shape, dt=F32):
            return nc.dram_tensor(name, shape, dt, kind="Internal").ap()

        m.rec_d = dram("rec_d", [EP, 8], I32)
        m.row_d = dram("row_d", [3, EP + 2])
        m.pos_d = dram("pos_d", [N, 1], I32)
        m.a_d = [dram("a0_d", [EP, AW])] + [dram(f"a{k}_d", [EP, D]) for k in (1, 2)]
        m.rec2_d = dram("rec2_d", [EP, 8], I32)
        m.row2_d = dram("row2_d", [1, EP + 1])
        m.h3_d = dram("h3_d", [N, D])
        m.tab_d = dram("tab_d", [EP, TW])

        m.xs = sb("xs", [P, ET * D])
        m.xh = sb("xh", [P, ET * D])
        m.big = sb("big", [P, 4 * EP + 1])
        m.w0 = sb("w0", [P, 2 * D])
        m.ident = sb("ident", [P, P])
        m.identb = sb("identb", [P, P], BF16)
        m.ones = sb("ones", [P, HI])
        m.onesf = sb("onesf", [P, P])
        m.iota = sb("iota", [P, HI])
        m.part = sb("part", [P, 1])
        m.e127 = sb("e127", [P, 1])
        m.tri = sb("tri", [P, P])
        m.triu = sb("triu", [P, P])
        m.eps = sb("eps", [P, 1])
        m.pre = sb("pre", [P, TW])
        m.bias0_b, m.bias1_b = m.pre[:, H:H + D], m.pre[:, H + 2 * D:TW]
        m.b12_b = sb("b12_b", [P, D])
        m.b0col = sb("b0col", [P, 2])
        m.srec = sb("srec", [P, ET * 8], I32)
        m.dstc = sb("dstc", [P, ET + 1])
        m.relc = sb("relc", [P, ET])
        m.srec2 = sb("srec2", [P, ET * 8], I32)
        m.srcc = sb("srcc", [P, ET + 1])
        m.to_node = sb("to_node", [P, ET], I32)
        m.ranks = [sb(f"rank{j}", [P, ET], I32)[:, :] for j in range(2)]
        m.posidx = sb("posidx", [P, ET], I32)
        m.place = sb("place", [P, ET], I32)
        m.poss = sb("poss", [P, ET], I32)
        m.masks = sb("masks", [P, ET])
        m.posn = sb("posn", [P, NT + 1], I32)
        m.co1 = sb("co1", [P, ET * R])
        m.co2 = [sb(f"co2_{l}", [P, ET * NB]) for l in range(2)]
        m.ex = sb("ex", [P, ET * H])
        m.exs = sb("exs", [P, ET * H])
        m.h = [sb(f"h{u}", [P, GD]) for u in range(2)]
        m.hT = [sb(f"hT{u}", [P, GD]) for u in range(2)]
        m.st = sb("st", [P, 2 * G * 6])
        m.mv = sb("mv", [P, 2 * G * 2])
        m.ln = sb("ln", [P, 2 * 4 * G])
        m.PS = ctx.enter_context(nc.psum_tensor("PS", [P, 4096], F32))
        m.comps_b = sb("comps_b", [P, 2 * R * NB])
        m.wa = sb("wa", [P, 2 * 3 * H])
        m.we8 = sb("we8", [ED, H])
        m.emean = sb("emean", [ED, 1])
        m.amean = sb("amean", [H, 1])
        m.eaT = sb("eaT", [ED, 512])
        m.idx_s = [sb(f"idx_s{u}", [P, 8 * G], I32) for u in range(2)]
        m.gate_dve, m.gate_pe, m.gate_sp = sem("gate_dve"), sem("gate_pe"), sem("gate_sp")
        m.drow = m.big[:, 0:EP]
        wbig = Carve(m.big[:, EP:])
        m.wb = [wbig(2 * NB * D) for _ in range(2)]
        m.wr = [wbig(2 * D) for _ in range(2)]
        m.w1t, m.w2t = wbig(2 * D), wbig(2 * D)
        m.bd = wbig(2 * R * P)
        m.work = m.big[:, EP + wbig.at:]
        m.eq = [sb(f"eq{u}", [P, P]) for u in range(2)]
        m.carry = [sb(f"carry{u}", [P, P]) for u in range(2)]
        m.alpha = sb("alpha", [P, 2 * G * H])
        m.nmasks = sb("nmasks", [P, ET])
        m.idx_n = [sb(f"idx_n{g}", [P, G], I32) for g in range(NG)]
        m.idx_t = [sb(f"idx_t{u}", [P, G], I32) for u in range(2)]
        m.val_t = [sb(f"val_t{u}", [P, G], I32) for u in range(2)]
        m.recs = [m.h[0][:, 0:8 * ET].bitcast(I32), sb("rec2", [P, 8 * ET], I32)[:, :]]

        for one in (constants, sort_edges, small_weights, records, counts, logits,
                    softmax, weights, edge_layer0):
            with step(nc) as own:
                one(nc, own, m)
        for k in (1, 2, 3):
            with step(nc) as own:
                edge_layer(nc, own, m, k)
        for one in (records_by_src, nodes, sage):
            with step(nc) as own:
                one(nc, own, m)


_INS = ["x", "src", "dst", "edge_attr_64", "edge_type_8", "edge_weight", "L0_gnn_W",
        "L0_gnn_W_edge", "L0_gnn_att_src", "L0_gnn_att_dst", "L0_gnn_att_edge", "L0_gnn_bias",
        "L1_gnn_weight", "L2_gnn_comps", "L2_gnn_bases", "L2_gnn_roots", "L2_gnn_biases",
        "L3_gnn_W1", "L3_gnn_b1", "L3_gnn_W2", "L3_gnn_b2"]


def kernel(**inputs):
    import numpy as _np
    import concourse.bacc as _bacc
    from concourse import mybir as _mybir
    from concourse.bass_utils import run_bass_kernel_spmd as _run

    nc = _bacc.Bacc("TRN2", target_bir_lowering=False, num_devices=1)
    arrays, args = {}, []
    for name in _INS:
        a = _np.ascontiguousarray(inputs[name])
        arrays[f"in_{name}"] = a
        args.append(nc.dram_tensor(f"in_{name}", a.shape, _mybir.dt.from_np(a.dtype),
                                   kind="ExternalInput").ap())
    args.append(nc.dram_tensor("out_0", (N, D), F32, kind="ExternalOutput").ap())
    build(nc, *args)
    r = _run(nc, [arrays], core_ids=[0])
    return r.results[0]["out_0"]
```
